# Optimizing a Trainium2 kernel written in Bass

```python
import numpy as np
import jax
import jax.numpy as jnp

def _softmax(x, axis=-1):
    return jax.nn.softmax(x, axis=axis)

def _gelu(x):
    return jax.nn.gelu(x, approximate=True)

def _silu(x):
    return jax.nn.silu(x)

def _sigmoid(x):
    return jax.nn.sigmoid(x)

def _layernorm(x, axis=-1, eps=1e-05):
    m = jnp.mean(x, axis=axis, keepdims=True)
    v = jnp.var(x, axis=axis, keepdims=True)
    return (x - m) / jnp.sqrt(v + eps)

def _scatter_add(tgt, idx, src, axis=0):
    return tgt.at[idx].add(src)

def _segment_sum(src, seg, n):
    return jax.ops.segment_sum(src, seg, n)
kernel_name = 'mk_flamingo_gated_d2_seqx_r8_d6148a'

def setup_inputs(seed: int=0):
    np.random.seed(seed)
    _w = jnp.asarray

    def _rec_inputs():
        import jax
        import jax.numpy as jnp
        _rk = jax.random.key(seed)
        x = -0.0005207 + 1.001 * jax.random.normal(jax.random.fold_in(_rk, 1), (8, 128, 512), jnp.float32)
        _lenS = 128 - jax.random.randint(jax.random.fold_in(_rk, 7), (8,), 0, max(1, 128 // 4) + 1, jnp.int32)
        _lenS2 = 128 - jax.random.randint(jax.random.fold_in(_rk, 8), (8,), 0, max(1, 128 // 4) + 1, jnp.int32)
        _ctx_4096P = jax.random.normal(jax.random.fold_in(_rk, 11), (8, 16, 512), jnp.float32)
        _ctx_4096c = jax.random.dirichlet(jax.random.fold_in(_rk, 511), 0.3 * jnp.ones((16,), jnp.float32), (8, 128))
        _ctx_4096t = jnp.einsum('bsk,bkd->bsd', _ctx_4096c, _ctx_4096P)
        _ctx_4096t = _ctx_4096t * jax.lax.rsqrt(jnp.mean(jnp.square(_ctx_4096t)) + 1e-12) * 0.953939
        ctx_4096 = -0.00010331 + 0.999899 * (_ctx_4096t + 0.3 * jax.random.normal(jax.random.fold_in(_rk, 611), (8, 128, 512), jnp.float32))
        _g = jax.random.normal(jax.random.fold_in(_rk, 9001), (2, 2), jnp.float32)
        _g = jnp.sign(_g) * jnp.maximum(jnp.abs(_g), 1.0) + (_g == 0) * 1.0
        g_xattn = _g[0]
        g_ffn = _g[1]
        return (x, ctx_4096, g_xattn, g_ffn)
    x, ctx_4096, g_xattn, g_ffn = _rec_inputs()

    def _L0_xattn_setup():
        import jax, jax.numpy as jnp
        import numpy as np
        HEADS = 32
        KV_HEADS = 8
        HEAD_DIM = 128
        EPS = 1e-06

        def rms_norm(x, w):
            var = jnp.mean(jnp.square(x.astype(jnp.float32)), axis=-1, keepdims=True)
            return (x.astype(jnp.float32) * jax.lax.rsqrt(var + EPS)).astype(x.dtype) * w
        key = jax.random.key(seed)
        ks = jax.random.split(key, 6)
        bsz, n_lat, seq, hidden = (8, 64, 512, 512)
        return {'latents': jax.random.normal(ks[0], (bsz, n_lat, hidden), jnp.float32), 'context': jax.random.normal(ks[1], (bsz, seq, hidden), jnp.float32), 'Wq': jax.random.normal(ks[2], (hidden, HEADS * HEAD_DIM), jnp.float32) * 0.02, 'Wk': jax.random.normal(ks[3], (hidden, KV_HEADS * HEAD_DIM), jnp.float32) * 0.02, 'Wv': jax.random.normal(ks[4], (hidden, KV_HEADS * HEAD_DIM), jnp.float32) * 0.02, 'Wo': jax.random.normal(ks[5], (HEADS * HEAD_DIM, hidden), jnp.float32) * 0.02, 'q_norm_w': jnp.ones((HEAD_DIM,), jnp.float32), 'k_norm_w': jnp.ones((HEAD_DIM,), jnp.float32)}
    _L0_xattn_all = _L0_xattn_setup()
    _L0_xattn_in = {k: v for k, v in _L0_xattn_all.items() if k in ('Wq', 'Wk', 'Wv', 'Wo', 'q_norm_w', 'k_norm_w')}
    del _L0_xattn_all

    def _L0_ffn_setup():
        import jax, jax.numpy as jnp
        import numpy as np
        HIDDEN = 512
        INTER = 1376

        def _ternary_quantize(w):
            scale = jnp.mean(jnp.abs(w))
            return jnp.clip(jnp.round(w / scale), -1.0, 1.0) * scale
        key = jax.random.key(seed)
        kx, kg, ku, kd = jax.random.split(key, 4)
        x = jax.random.normal(kx, (2, 256, HIDDEN), dtype=jnp.float32)
        w_gate = _ternary_quantize(jax.random.normal(kg, (INTER, HIDDEN), dtype=jnp.float32) * 0.02)
        w_up = _ternary_quantize(jax.random.normal(ku, (INTER, HIDDEN), dtype=jnp.float32) * 0.02)
        w_down = _ternary_quantize(jax.random.normal(kd, (HIDDEN, INTER), dtype=jnp.float32) * 0.02)
        return {'x': x, 'w_gate': w_gate, 'w_up': w_up, 'w_down': w_down}
    _L0_ffn_all = _L0_ffn_setup()
    _L0_ffn_in = {k: v for k, v in _L0_ffn_all.items() if k in ('w_gate', 'w_up', 'w_down')}
    del _L0_ffn_all

    def _L1_xattn_setup():
        import jax, jax.numpy as jnp
        import numpy as np
        N, C, S = (16, 64, 512)
        rng = jax.random.key(seed)
        k1, k2, k3 = jax.random.split(rng, 3)
        return {'key': jax.random.normal(k1, (N, C, S), dtype=jnp.float32), 'value': jax.random.normal(k2, (N, C, S), dtype=jnp.float32), 'query': jax.random.normal(k3, (N, C, S), dtype=jnp.float32)}
    _L1_xattn_all = _L1_xattn_setup()
    _L1_xattn_in = {k: v for k, v in _L1_xattn_all.items() if k in ()}
    del _L1_xattn_all

    def _L1_ffn_setup():
        import jax, jax.numpy as jnp
        import numpy as np
        DIM = 512
        INTER = 128
        E = 16
        GROUPS = 4
        LIM = 2
        K = 2
        SHARED_INTER = 2 * INTER
        SCALE = 1.0
        key = jax.random.key(seed)
        ks = jax.random.split(key, 16)

        def n(k, shape, s=0.02):
            return jax.random.normal(k, shape, jnp.float32) * s
        return {'x': jax.random.normal(ks[0], (1, 256, DIM), jnp.float32), 'router_w': n(ks[1], (DIM, E)), 'router_b': n(ks[2], (E,)), 'router_bias': n(ks[3], (E,), 1.0), 'ew1': n(ks[4], (E, DIM, INTER)), 'eb1': n(ks[5], (E, INTER)), 'ew2': n(ks[6], (E, DIM, INTER)), 'eb2': n(ks[7], (E, INTER)), 'ew3': n(ks[8], (E, INTER, DIM)), 'eb3': n(ks[9], (E, DIM)), 'sw1': n(ks[10], (DIM, SHARED_INTER)), 'sb1': n(ks[11], (SHARED_INTER,)), 'sw2': n(ks[12], (DIM, SHARED_INTER)), 'sb2': n(ks[13], (SHARED_INTER,)), 'sw3': n(ks[14], (SHARED_INTER, DIM)), 'sb3': n(ks[15], (DIM,))}
    _L1_ffn_all = _L1_ffn_setup()
    _L1_ffn_in = {k: v for k, v in _L1_ffn_all.items() if k in ('router_w', 'router_b', 'router_bias', 'ew1', 'eb1', 'ew2', 'eb2', 'ew3', 'eb3', 'sw1', 'sb1', 'sw2', 'sb2', 'sw3', 'sb3')}
    del _L1_ffn_all
    return {'x': x, 'ctx_4096': ctx_4096, 'g_xattn': g_xattn, 'g_ffn': g_ffn, 'L0_xattn_Wq': _L0_xattn_in['Wq'], 'L0_xattn_Wk': _L0_xattn_in['Wk'], 'L0_xattn_Wv': _L0_xattn_in['Wv'], 'L0_xattn_Wo': _L0_xattn_in['Wo'], 'L0_xattn_q_norm_w': _L0_xattn_in['q_norm_w'], 'L0_xattn_k_norm_w': _L0_xattn_in['k_norm_w'], 'L0_ffn_w_gate': _L0_ffn_in['w_gate'], 'L0_ffn_w_up': _L0_ffn_in['w_up'], 'L0_ffn_w_down': _L0_ffn_in['w_down'], 'L1_ffn_router_w': _L1_ffn_in['router_w'], 'L1_ffn_router_b': _L1_ffn_in['router_b'], 'L1_ffn_router_bias': _L1_ffn_in['router_bias'], 'L1_ffn_ew1': _L1_ffn_in['ew1'], 'L1_ffn_eb1': _L1_ffn_in['eb1'], 'L1_ffn_ew2': _L1_ffn_in['ew2'], 'L1_ffn_eb2': _L1_ffn_in['eb2'], 'L1_ffn_ew3': _L1_ffn_in['ew3'], 'L1_ffn_eb3': _L1_ffn_in['eb3'], 'L1_ffn_sw1': _L1_ffn_in['sw1'], 'L1_ffn_sb1': _L1_ffn_in['sb1'], 'L1_ffn_sw2': _L1_ffn_in['sw2'], 'L1_ffn_sb2': _L1_ffn_in['sb2'], 'L1_ffn_sw3': _L1_ffn_in['sw3'], 'L1_ffn_sb3': _L1_ffn_in['sb3']}

def reference(x, ctx_4096, g_xattn, g_ffn, L0_xattn_Wq, L0_xattn_Wk, L0_xattn_Wv, L0_xattn_Wo, L0_xattn_q_norm_w, L0_xattn_k_norm_w, L0_ffn_w_gate, L0_ffn_w_up, L0_ffn_w_down, L1_ffn_router_w, L1_ffn_router_b, L1_ffn_router_bias, L1_ffn_ew1, L1_ffn_eb1, L1_ffn_ew2, L1_ffn_eb2, L1_ffn_ew3, L1_ffn_eb3, L1_ffn_sw1, L1_ffn_sb1, L1_ffn_sw2, L1_ffn_sb2, L1_ffn_sw3, L1_ffn_sb3):
    import jax
    import jax.numpy as jnp

    def _L0_xattn_ref(latents, context, Wq, Wk, Wv, Wo, q_norm_w, k_norm_w):
        import jax, jax.numpy as jnp
        import numpy as np
        HEADS = 32
        KV_HEADS = 8
        HEAD_DIM = 128
        EPS = 1e-06

        def rms_norm(x, w):
            var = jnp.mean(jnp.square(x.astype(jnp.float32)), axis=-1, keepdims=True)
            return (x.astype(jnp.float32) * jax.lax.rsqrt(var + EPS)).astype(x.dtype) * w
        bsz, q_len, hidden = latents.shape
        kv = jnp.concatenate([context, latents], axis=1)
        kv_len = kv.shape[1]
        groups = HEADS // KV_HEADS
        q = (latents @ Wq).reshape(bsz, q_len, HEADS, HEAD_DIM).transpose(0, 2, 1, 3)
        k = (kv @ Wk).reshape(bsz, kv_len, KV_HEADS, HEAD_DIM).transpose(0, 2, 1, 3)
        v = (kv @ Wv).reshape(bsz, kv_len, KV_HEADS, HEAD_DIM).transpose(0, 2, 1, 3)
        q = rms_norm(q, q_norm_w)
        k = rms_norm(k, k_norm_w)
        qg = q.reshape(bsz, KV_HEADS, groups, q_len, HEAD_DIM)
        scale = 1.0 / np.sqrt(HEAD_DIM)
        scores = jnp.einsum('bhgqd,bhkd->bhgqk', qg, k) * scale
        probs = jax.nn.softmax(scores.astype(jnp.float32), axis=-1).astype(q.dtype)
        out = jnp.einsum('bhgqk,bhkd->bhgqd', probs, v)
        out = out.reshape(bsz, HEADS, q_len, HEAD_DIM).transpose(0, 2, 1, 3)
        out = out.reshape(bsz, q_len, HEADS * HEAD_DIM)
        return out @ Wo

    def _L0_ffn_ref(x, w_gate, w_up, w_down):
        import jax, jax.numpy as jnp
        import numpy as np
        HIDDEN = 512
        INTER = 1376

        def _ternary_quantize(w):
            scale = jnp.mean(jnp.abs(w))
            return jnp.clip(jnp.round(w / scale), -1.0, 1.0) * scale
        xf = x.astype(jnp.float32) / 128.0
        gate = jnp.einsum('bsh,ih->bsi', xf, w_gate)
        up = jnp.einsum('bsh,ih->bsi', xf, w_up)
        inter = jax.nn.silu(gate) * up
        inter_q = jnp.trunc(jnp.clip(inter * 128.0, -128.0, 127.0)).astype(jnp.int8)
        down = jnp.einsum('bsi,hi->bsh', inter_q.astype(jnp.float32), w_down)
        out = jnp.trunc(jnp.clip(down * 128.0, -128.0, 127.0)).astype(jnp.int8)
        return out

    def _L1_xattn_ref(key, value, query):
        import jax, jax.numpy as jnp
        import numpy as np
        N, C, S = (16, 64, 512)
        KC = key.shape[1]
        sim = jnp.einsum('ncs,nds->ncd', key, query) * KC ** (-0.5)
        sim = jax.nn.softmax(sim, axis=1)
        context = jnp.einsum('ncd,nds->ncs', sim, value)
        return context

    def _L1_ffn_ref(x, router_w, router_b, router_bias, ew1, eb1, ew2, eb2, ew3, eb3, sw1, sb1, sw2, sb2, sw3, sb3):
        import jax, jax.numpy as jnp
        import numpy as np
        DIM = 512
        INTER = 128
        E = 16
        GROUPS = 4
        LIM = 2
        K = 2
        SHARED_INTER = 2 * INTER
        SCALE = 1.0
        shape = x.shape
        xt = x.reshape(-1, DIM)
        T = xt.shape[0]
        logits = xt @ router_w + router_b
        scores = jax.nn.softmax(logits.astype(jnp.float32), axis=-1) + router_bias
        g = scores.reshape(T, GROUPS, E // GROUPS)
        _, gidx = jax.lax.top_k(g.max(axis=-1), LIM)
        keep = jnp.zeros((T, GROUPS), bool).at[jnp.arange(T)[:, None], gidx].set(True)
        masked = jnp.where(keep[:, :, None], g, -jnp.inf).reshape(T, E)
        _, idx = jax.lax.top_k(masked, K)
        vals = (jnp.take_along_axis(scores, idx, axis=1) * SCALE).astype(x.dtype)
        gate = jnp.zeros((T, E), x.dtype).at[jnp.arange(T)[:, None], idx].add(vals)

        def step(y, p):
            w1, b1, w2, b2, w3, b3, ge = p
            h = jax.nn.silu(xt @ w1 + b1) * (xt @ w2 + b2)
            return (y + ge[:, None] * (h @ w3 + b3), None)
        y, _ = jax.lax.scan(step, jnp.zeros_like(xt), (ew1, eb1, ew2, eb2, ew3, eb3, gate.T))
        z = jax.nn.silu(xt @ sw1 + sb1) * (xt @ sw2 + sb2) @ sw3 + sb3
        return (y + z).reshape(shape)
    x = x + jnp.tanh(g_xattn[0]) * _L0_xattn_ref(_layernorm(x, axis=-1), ctx_4096, L0_xattn_Wq, L0_xattn_Wk, L0_xattn_Wv, L0_xattn_Wo, L0_xattn_q_norm_w, L0_xattn_k_norm_w)
    x = x + jnp.tanh(g_ffn[0]) * _L0_ffn_ref(_layernorm(x, axis=-1), L0_ffn_w_gate, L0_ffn_w_up, L0_ffn_w_down)
    x = x + jnp.tanh(g_xattn[1]) * _L1_xattn_ref(ctx_4096, ctx_4096, _layernorm(x, axis=-1))
    x = x + jnp.tanh(g_ffn[1]) * _L1_ffn_ref(_layernorm(x, axis=-1), L1_ffn_router_w, L1_ffn_router_b, L1_ffn_router_bias, L1_ffn_ew1, L1_ffn_eb1, L1_ffn_ew2, L1_ffn_eb2, L1_ffn_ew3, L1_ffn_eb3, L1_ffn_sw1, L1_ffn_sb1, L1_ffn_sw2, L1_ffn_sb2, L1_ffn_sw3, L1_ffn_sb3)
    return x

_drawn_inputs = setup_inputs


def setup_inputs(seed=0):
    import zlib

    import numpy as np

    out = dict(_drawn_inputs(seed))
    spreads = {'g_ffn': (-1.0, 0.6), 'L0_xattn_q_norm_w': (1.0, 0.6), 'L0_xattn_k_norm_w': (1.0, 0.6)}
    factors = {'L1_ffn_router_w': 8.0,
     'L1_ffn_router_b': 64.0,
     'L1_ffn_eb1': 8.0,
     'L1_ffn_eb2': 8.0,
     'L1_ffn_sb1': 43.662,
     'L1_ffn_sb2': 41.889,
     'L1_ffn_sb3': 4.053}
    for name, (base, spread) in spreads.items():
        noise = np.random.default_rng([zlib.crc32(name.encode()), seed]).standard_normal(out[name].shape)
        drawn = base * np.exp(spread * noise) if base else spread * noise
        out[name] = jnp.asarray(drawn.astype(out[name].dtype))
    for name, factor in factors.items():
        out[name] = (out[name] * factor).astype(out[name].dtype)
    return out
```

```python
from contextlib import ExitStack

import concourse.bass as bass
from concourse import mybir

F32 = mybir.dt.float32
F32R = mybir.dt.float32r
ALU = mybir.AluOpType
ACT = mybir.ActivationFunctionType
AX = mybir.AxisListType

P = 128
D = 512
KC = D // P
NB = 8
G = 8
R = 4
PAIRS = NB // 2
HD = 128
RMS_EPS = 1e-6
LN_EPS = 1e-5
INTER = 1376
CH = -(-INTER // P)
TAIL = INTER - (CH - 1) * P
ROUND = 1.5 * 2.0 ** 23
E = 16
EG = 4
EA = E + 2
CTX_SCALE = float(P) ** -0.5
LOW = -3.0e38


def build(nc, x, ctx, ctx_t, g_xattn, g_ffn, wq, wkv, wo, q_w, k_w, w_gate, w_up, w_down, router_w, router_b,
          router_bias, e_w12, e_w3, e_b12, e_b3, out):
    with ExitStack() as top:
        def sb(name, shape, dt=F32, scope=top):
            return scope.enter_context(nc.sbuf_tensor(name, shape, dt))

        def sem(name):
            return top.enter_context(nc.semaphore(name))

        x_sb = sb("x_sb", [P, NB, D])
        ident = sb("ident", [P, P])
        minus_half = sb("minus_half", [P, 16])
        gate_rows = sb("gate_rows", [P, 4])
        head_w = sb("head_w", [P, 3])
        ln_stats = [sb(f"ln_stats{i}", [P, 2, 6]) for i in range(2)]
        ln_mv = [sb(f"ln_mv{i}", [P, 2, 2]) for i in range(2)]
        ln_var = [sb(f"ln_var{i}", [P, 2, 1]) for i in range(2)]
        ln_rstd = [sb(f"ln_rstd{i}", [P, 2, 1]) for i in range(2)]
        first_rows = sb("first_rows", [P, 2, D])

        router_wr = sb("router_wr", [P, KC, E])
        router_wh = sb("router_wh", [P, KC, E], F32R)
        router_wl = sb("router_wl", [P, KC, E], F32R)
        router_rows = sb("router_rows", [P, 2, E])
        b12 = sb("b12", [P, EA, 2])
        b_now = sb("b_now", [P, 2, 2])
        logits = sb("logits", [P, NB, E])
        gates = sb("gates", [P, NB, EA])
        start = nc.sbuf_base
        at = [start]

        def put(name, shape, dt=F32):
            size = 4
            for n in shape[1:]:
                size *= n
            t = nc.alloc_sbuf_tensor_at(name, shape, dt, offset=at[0])
            at[0] += -(-size // 32) * 32
            return t

        kv_src_hi = put("kv_src_hi", [P, 2, KC, NB * P], F32R)
        kv_src_lo = put("kv_src_lo", [P, 2, KC, NB * P], F32R)
        wq_raw = put("wq_raw", [P, KC, R * HD])
        wq_hi = put("wq_hi", [P, KC, R * HD], F32R)
        wq_lo = put("wq_lo", [P, KC, R * HD], F32R)
        wkv_raw = put("wkv_raw", [P, KC, 2 * HD])
        wkv_hi = put("wkv_hi", [P, KC, 2 * HD], F32R)
        wkv_lo = put("wkv_lo", [P, KC, 2 * HD], F32R)
        wo_raw = put("wo_raw", [P, R, D])
        wo_hi = put("wo_hi", [P, R, D], F32R)
        wo_lo = put("wo_lo", [P, R, D], F32R)
        q_hi = put("q_hi", [P, 2, R, 2 * P], F32R)
        q_lo = put("q_lo", [P, 2, R, 2 * P], F32R)
        k_hi = put("k_hi", [P, 2, 4 * P], F32R)
        k_lo = put("k_lo", [P, 2, 4 * P], F32R)
        v_hi = put("v_hi", [P, 2, 4, HD], F32R)
        v_lo = put("v_lo", [P, 2, 4, HD], F32R)
        q_rows = put("q_rows", [P, 2, R * HD])
        q_ss = put("q_ss", [P, 2 * R])
        k_rows = put("k_rows", [P, 4, HD])
        k_junk = put("k_junk", [P, 4, HD])
        k_ss, k_var, k_rstd = put("k_ss", [P, 4]), put("k_var", [P, 4]), put("k_rstd", [P, 4])
        q_var, q_rstd = put("q_var", [P, 2 * R]), put("q_rstd", [P, 2, 2 * R])
        row_max, exp_bias = put("row_max", [P, R]), put("exp_bias", [P, R])
        row_sum, row_inv = put("row_sum", [P, R]), put("row_inv", [P, R])
        probs = put("probs", [P, R, 2 * P])
        here = at[0]
        ctx_raw = put("ctx_raw", [P, KC, NB * P])
        at[0] = here
        pt_hi = put("pt_hi", [P, 2, R * P], F32R)
        pt_lo = put("pt_lo", [P, 2, R * P], F32R)
        o_hi = put("o_hi", [P, 2, R * P], F32R)
        o_lo = put("o_lo", [P, 2, R * P], F32R)

        at[0] = start
        gu_raw = put("gu_raw", [P, 2, 2, KC, P])
        wd_raw = put("wd_raw", [P, 2, D])
        e12_raw = put("e12_raw", [P, 2, 2 * KC, P])
        e3_raw = put("e3_raw", [P, 2, D])
        b3 = put("b3", [E + 1, D])
        gu_at = at[0]
        gu_hi = put("gu_hi", [P, 2, 2, KC, P], F32R)
        gu_lo = put("gu_lo", [P, 2, 2, KC, P], F32R)
        xt_hi = put("xt_hi", [P, KC, NB * P], F32R)
        xt_lo = put("xt_lo", [P, KC, NB * P], F32R)
        iq_at = at[0]
        iq = put("iq", [P, CH, NB * P], F32R)
        wd_hi = put("wd_hi", [P, CH, D], F32R)
        wd_lo = put("wd_lo", [P, CH, D], F32R)
        silu_gate = put("silu_gate", [P, 2, D])
        tr_v = put("tr_v", [P, 2 * D])
        tr_abs = put("tr_abs", [P, 2 * D])
        tr_sign = put("tr_sign", [P, 2 * D])
        tr_int = put("tr_int", [P, 2 * D])

        at[0] = gu_at
        ctx_rows = put("ctx_rows", [P, 2, D])
        ctx_cols = put("ctx_cols", [P, 2, KC, P])
        q3 = put("q3", [P, KC, P])
        sim = put("sim", [P, P])
        moe_rows = put("moe_rows", [P, 2, D])
        sim_max, sim_bias = put("sim_max", [P, 1]), put("sim_bias", [P, 1])
        sim_sum, sim_inv = put("sim_sum", [P, 1]), put("sim_inv", [P, 1])

        at[0] = iq_at
        e12_hi = put("e12_hi", [P, 2, 2 * KC, P], F32R)
        e12_lo = put("e12_lo", [P, 2, 2 * KC, P], F32R)
        e3_hi = put("e3_hi", [P, 2, D], F32R)
        e3_lo = put("e3_lo", [P, 2, D], F32R)
        e_silu = put("e_silu", [P, 2, D])
        e_h = put("e_h", [P, 2, D])
        h_hi = put("h_hi", [P, 2, D], F32R)
        h_lo = put("h_lo", [P, 2, D], F32R)
        y_acc = put("y_acc", [P, NB, D])
        r_gt = put("r_gt", [P, NB, E, E])
        r_eq = put("r_eq", [P, NB, E, E])
        r_score = put("r_score", [P, NB, E])
        r_masked = put("r_masked", [P, NB, E])
        r_stat = put("r_stat", [P, 4, NB])
        r_gmax, r_keep, r_low = (put(n, [P, NB, EG]) for n in ("r_gmax", "r_keep", "r_low"))
        r_rank = put("r_rank", [P, NB, E])
        tri = put("tri", [P, E, E])
        gates_t = put("gates_t", [E + 1, NB * P])

        bank = [top.enter_context(nc.psum_tensor(f"bank{i}", [P, 512], F32)) for i in range(8)]
        ln_rows = [first_rows, moe_rows]
        scores_ps = bank[0:2]
        pt_ps = bank[2:4]
        o_ps = bank[4]
        y_ps = bank[5]
        proj_a, proj_b = bank[6], bank[7]

        x_loaded = [sem(f"x_loaded{i}") for i in range(PAIRS)]
        small_loaded = sem("small_loaded")
        consts_ready = sem("consts_ready")
        head_w_ready = sem("head_w_ready")
        gates_ready = sem("gates_ready")
        ctx_loaded = [sem(f"ctx_loaded{i}") for i in range(PAIRS)]
        ctx_hi_ready = sem("ctx_hi_ready")
        ctx_lo_ready = sem("ctx_lo_ready")
        ln_stat = [sem(f"ln_stat{i}") for i in range(2)]
        ln_rstd_ready = [sem(f"ln_rstd_ready{i}") for i in range(2)]
        ln_row_ready = [sem(f"ln_row_ready{i}") for i in range(2)]
        ln_transposed = [sem(f"ln_transposed{i}") for i in range(2)]
        ln_hi_ready = [sem(f"ln_hi_ready{i}") for i in range(2)]
        ln_lo_ready = [sem(f"ln_lo_ready{i}") for i in range(2)]
        wq_loaded, wkv_loaded, wo_loaded = sem("wq_loaded"), sem("wkv_loaded"), sem("wo_loaded")
        wq_hi_ready, wq_lo_ready = sem("wq_hi_ready"), sem("wq_lo_ready")
        wo_hi_ready, wo_lo_ready = sem("wo_hi_ready"), sem("wo_lo_ready")
        wkv_hi_ready, wkv_lo_ready = sem("wkv_hi_ready"), sem("wkv_lo_ready")
        kv_done, k_turned, q_done, q_turned = sem("kv_done"), sem("k_turned"), sem("q_done"), sem("q_turned")
        k_copied, v_hi_ready, v_lo_ready = sem("k_copied"), sem("v_hi_ready"), sem("v_lo_ready")
        k_ss_ready, k_rstd_ready, k_scaled = sem("k_ss_ready"), sem("k_rstd_ready"), sem("k_scaled")
        k_var_ready = sem("k_var_ready")
        k_hi_ready, k_lo_ready = sem("k_hi_ready"), sem("k_lo_ready")
        q_hi_ready, q_lo_ready, q_copied = sem("q_hi_ready"), sem("q_lo_ready"), sem("q_copied")
        q_ss_ready = sem("q_ss_ready")
        q_var_ready, q_rstd_ready = sem("q_var_ready"), sem("q_rstd_ready")
        scores_done, max_ready, bias_ready = sem("scores_done"), sem("max_ready"), sem("bias_ready")
        exp_done, inv_ready, probs_ready = sem("exp_done"), sem("inv_ready"), sem("probs_ready")
        p_turned, pt_hi_ready, pt_lo_ready = sem("p_turned"), sem("pt_hi_ready"), sem("pt_lo_ready")
        o_done, o_hi_ready, o_lo_ready = sem("o_done"), sem("o_hi_ready"), sem("o_lo_ready")
        y_done, y_added = sem("y_done"), sem("y_added")
        stored = sem("stored")
        gu_loaded = [sem(f"gu_loaded{i}") for i in range(2)]
        wd_loaded = [sem(f"wd_loaded{i}") for i in range(2)]
        ctx3_rows_loaded = [sem(f"ctx3_rows_loaded{i}") for i in range(2)]
        ctx3_cols_loaded = [sem(f"ctx3_cols_loaded{i}") for i in range(2)]
        e12_loaded = [sem(f"e12_loaded{i}") for i in range(2)]
        e3_loaded = [sem(f"e3_loaded{i}") for i in range(2)]
        gu_hi_ready = sem("gu_hi_ready")
        gu_lo_ready = sem("gu_lo_ready")
        wd_hi_ready = sem("wd_hi_ready")
        wd_lo_ready = sem("wd_lo_ready")
        gu_done = sem("gu_done")
        inter_step = sem("inter_step")
        iq_ready = sem("iq_ready")
        sign_ready = sem("sign_ready")
        down_done = sem("down_done")
        down_taken = sem("down_taken")
        x2_ready = sem("x2_ready")
        q3_ready = sem("q3_ready")
        sim_done = sem("sim_done")
        sim_max_ready = sem("sim_max_ready")
        sim_bias_ready = sem("sim_bias_ready")
        sim_exp = sem("sim_exp")
        sim_inv_ready = sem("sim_inv_ready")
        sim_ready = sem("sim_ready")
        context_done = sem("context_done")
        x3_ready = sem("x3_ready")
        router_done = sem("router_done")
        logits_ready = sem("logits_ready")
        router_w_hi = sem("router_w_hi")
        router_w_ready = sem("router_w_ready")
        router_step = sem("router_step")
        router_exp = sem("router_exp")
        gates_ready4 = sem("gates_ready4")
        y_zeroed = sem("y_zeroed")
        e_hi_ready = sem("e_hi_ready")
        b_now_ready = sem("b_now_ready")
        e_lo_ready = sem("e_lo_ready")
        h_done = sem("h_done")
        silu_ready = sem("silu_ready")
        h_ready = sem("h_ready")
        h_hi_ready = sem("h_hi_ready")
        h_lo_ready = sem("h_lo_ready")
        e_done = sem("e_done")
        e_added = sem("e_added")
        gates_turned = sem("gates_turned")
        gates_copied = sem("gates_copied")
        bias_done = sem("bias_done")
        bias_added = sem("bias_added")
        x4_ready = sem("x4_ready")
        router_loaded = sem("router_loaded")
        tri_ready = sem("tri_ready")
        silu_gate_ready = [sem(f"silu_gate_ready{i}") for i in range(2)]
        inter_ready = [sem(f"inter_ready{i}") for i in range(2)]

        def three(eng, out_ap, a_hi, a_lo, b_hi, b_lo, start, stop):
            eng.matmul(out_ap, a_lo, b_hi, start=start, stop=False)
            eng.matmul(out_ap, a_hi, b_lo, start=False, stop=False)
            return eng.matmul(out_ap, a_hi, b_hi, start=False, stop=stop)

        def after_start(g, b, back):
            return not (isinstance(g, int) and g * NB + b - back < 0)

        def before_end(g, b, ahead):
            return not (isinstance(g, int) and g * NB + b + ahead >= G * NB)

        def after_first(e):
            return not (isinstance(e, int) and e == 0)

        def groups(eng, one_group):
            one_group(0)
            with eng.Fori(1, G - 1) as g:
                one_group(g)
            one_group(G - 1)

        def chunks(eng, one_chunk):
            for j in range(2):
                one_chunk(j, j, P, P)
            with eng.Fori(1, (CH - 3) // 2) as i:
                for j in range(2):
                    one_chunk(i * 2 + j, j, P, P)
            one_chunk(CH - 3, 0, P, P)
            one_chunk(CH - 2, 1, P, TAIL)
            one_chunk(CH - 1, 0, TAIL, 0)

        def experts(eng, one_expert):
            for j in range(2):
                one_expert(j, j)
            with eng.Fori(1, EA // 2 - 1) as i:
                for j in range(2):
                    one_expert(i * 2 + j, j)
            for j in range(2):
                one_expert(EA - 2 + j, j)

        block = top.enter_context(nc.Block())

        @block.sync
        def _(sp):
            sp.dma_start(head_w[:, 0:1], q_w).then_inc(small_loaded, 16)
            sp.dma_start(head_w[:, 1:2], k_w).then_inc(small_loaded, 16)
            sp.dma_start(gate_rows[:, 0:2], g_xattn.broadcast_to([P, 2])).then_inc(small_loaded, 16)
            sp.dma_start(gate_rows[:, 2:4], g_ffn.broadcast_to([P, 2])).then_inc(small_loaded, 16)
            for p in range(PAIRS):
                sp.dma_start(x_sb[:, 2 * p:2 * p + 2, :], x[2 * p:2 * p + 2, :, :].rearrange("b t d -> t b d"))\
                  .then_inc(x_loaded[p], 16)
                sp.dma_start(ctx_raw[:, :, 256 * p:256 * p + 256], ctx_t[:, :, 256 * p:256 * p + 256])\
                  .then_inc(ctx_loaded[p], 16)

            def load_group(g):
                first = isinstance(g, int)
                if not first:
                    sp.wait_ge(wkv_lo_ready, g)
                sp.dma_start(wkv_raw[:, :, :], wkv[bass.ds(g, 1), :, :, :].rearrange("a p c n -> p (a c) n"))\
                  .then_inc(wkv_loaded, 16)
                if not first:
                    sp.wait_ge(wq_lo_ready, g * R)
                sp.dma_start(wq_raw[:, :, :], wq[bass.ds(g, 1), :, :, :].rearrange("a p c n -> p (a c) n"))\
                  .then_inc(wq_loaded, 16)
                if not first:
                    sp.wait_ge(wo_lo_ready, g * R)
                sp.dma_start(wo_raw[:, :, :], wo[bass.ds(g, 1), :, :, :].rearrange("a p c n -> p (a c) n"))\
                  .then_inc(wo_loaded, 16)

            load_group(0)
            with sp.Fori(1, G) as g:
                load_group(g)

            def load_chunk(c, j, width):
                if width == P:
                    cols = bass.ds(c * P, P)
                else:
                    cols = slice(INTER - width, INTER)
                for i, w in enumerate((w_gate, w_up)):
                    sp.dma_start(gu_raw[:, j, i, :, 0:width], w[:, :, cols]).then_inc(gu_loaded[j], 16)
                rows = bass.ds(c * P, P) if width == P else slice(INTER - width, INTER)
                sp.dma_start(wd_raw[0:width, j, :], w_down[rows, :]).then_inc(wd_loaded[j], 16)

            def load_expert(e, j):
                sp.dma_start(e12_raw[:, j, :, :], e_w12[bass.ds(e, 1), :, :, :].rearrange("a p c n -> p (a c) n"))\
                  .then_inc(e12_loaded[j], 16)
                sp.dma_start(e3_raw[:, j, :], e_w3[bass.ds(e, 1), :, :].rearrange("a p n -> p (a n)"))\
                  .then_inc(e3_loaded[j], 16)

            sp.wait_ge(q_done, 2 * PAIRS * G)
            sp.wait_ge(kv_done, 2 * PAIRS * G)
            load_chunk(0, 0, P)
            load_chunk(1, 1, P)
            load_expert(0, 0)
            load_expert(1, 1)
            for dst, src in ((router_wr[:, :, :], router_w), (router_rows[:, 0, :], router_b.broadcast_to([P, E])),
                             (router_rows[:, 1, :], router_bias.broadcast_to([P, E])), (b12[:, :, :], e_b12),
                             (b3[:, :], e_b3)):
                sp.dma_start(dst, src).then_inc(router_loaded, 16)
            with sp.Fori(1, (CH - 1) // 2) as i:
                for j in range(2):
                    c = i * 2 + j
                    sp.wait_ge(gu_lo_ready, c - 1)
                    sp.wait_ge(wd_lo_ready, c - 1)
                    load_chunk(c, j, P)
            sp.wait_ge(gu_lo_ready, CH - 2)
            sp.wait_ge(wd_lo_ready, CH - 2)
            load_chunk(CH - 1, 0, TAIL)
            sp.wait_ge(gu_done, 4 * CH)
            for t in range(NB):
                if t >= 2:
                    sp.wait_ge(context_done, t - 1)
                sp.dma_start(ctx_rows[:, t % 2, :], ctx[t, :, :]).then_inc(ctx3_rows_loaded[t % 2], 16)
                sp.dma_start(ctx_cols[:, t % 2, :, :], ctx_t[:, :, t * P:t * P + P]).then_inc(ctx3_cols_loaded[t % 2], 16)
            with sp.Fori(1, EA // 2) as i:
                for j in range(2):
                    sp.wait_ge(e_lo_ready, (i * 2 + j - 1) * 2)
                    load_expert(i * 2 + j, j)
            for t in range(NB):
                sp.wait_ge(x4_ready, t + 1)
                sp.dma_start(out[t, :, :], x_sb[:, t, :]).then_inc(stored, 16)
            sp.wait_ge(stored, 16 * NB)

        @block.gpsimd
        def _(pool):
            pool.memset(ident[:, :], 0.0).then_inc(consts_ready, 1)
            pool.memset(minus_half[:, :], -0.5).then_inc(consts_ready, 1)
            pool.wait_ge(consts_ready, 2)
            pool.affine_select(out=ident[:, :], in_=ident[:, :], compare_op=ALU.not_equal, fill=1.0, base=0,
                               pattern=[[-1, P]], channel_multiplier=1).then_inc(consts_ready, 1)

            def ln_root(i, s=0):
                pool.wait_ge(ln_stat[s], 3 * i + 3)
                pool.tensor_tensor(ln_rstd[s][:, i % 2, :], ln_var[s][:, i % 2, :], minus_half[:, 0:1], ALU.pow)\
                    .then_inc(ln_rstd_ready[s], 1)

            def wkv_low(g):
                pool.wait_ge(wkv_hi_ready, g + 1)
                pool.tensor_tensor(wkv_lo[:, :, :], wkv_raw[:, :, :], wkv_hi[:, :, :].bitcast(F32),
                                   ALU.subtract).then_inc(wkv_lo_ready, 1)

            def wq_low(g):
                for h in range(R):
                    cols = slice(h * HD, h * HD + HD)
                    pool.wait_ge(wq_hi_ready, g * R + h + 1)
                    pool.tensor_tensor(wq_lo[:, :, cols], wq_raw[:, :, cols], wq_hi[:, :, cols].bitcast(F32),
                                       ALU.subtract).then_inc(wq_lo_ready, 1)

            def wo_low(g):
                for h in range(R):
                    pool.wait_ge(wo_hi_ready, g * R + h + 1)
                    pool.tensor_tensor(wo_lo[:, h, :], wo_raw[:, h, :], wo_hi[:, h, :].bitcast(F32),
                                       ALU.subtract).then_inc(wo_lo_ready, 1)

            def k_root(pair):
                pool.wait_ge(k_var_ready, pair + 1)
                pool.tensor_tensor(k_rstd[:, :], k_var[:, :], minus_half[:, 0:4], ALU.pow).then_inc(k_rstd_ready, 1)

            def q_root(pair, par):
                pool.wait_ge(q_var_ready, pair + 1)
                pool.tensor_tensor(q_rstd[:, par, :], q_var[:, :], minus_half[:, 0:2 * R], ALU.pow)\
                    .then_inc(q_rstd_ready, 1)

            for t in range(NB):
                ln_root(t)
            wkv_low(0)
            wq_low(0)
            k_root(0)
            q_root(0, 0)

            def one_group(g):
                for b in range(0, NB, 2):
                    next_pair = g * PAIRS + (b // 2 + 1)
                    if b == 2:
                        wo_low(g)
                    if b == 6 and before_end(g, b, 2):
                        wq_low(g + 1)
                    if before_end(g, b, 2):
                        k_root(next_pair)
                    if b == 4 and before_end(g, b, 4):
                        wkv_low(g + 1)
                    if before_end(g, b, 2):
                        q_root(next_pair, (b // 2 + 1) % 2)

            groups(pool, one_group)

            def halves_low(c, j, width):
                pool.wait_ge(wd_hi_ready, c + 1)
                pool.wait_ge(gu_hi_ready, c + 1)
                pool.tensor_tensor(gu_lo[:, j, :, :, 0:width].rearrange("p a c n -> p (a c) n"),
                                   gu_raw[:, j, :, :, 0:width].rearrange("p a c n -> p (a c) n"),
                                   gu_hi[:, j, :, :, 0:width].bitcast(F32).rearrange("p a c n -> p (a c) n"),
                                   ALU.subtract).then_inc(gu_lo_ready, 1)
                dst = bass.ds(c, 1)
                pool.tensor_tensor(wd_lo[0:width, dst, :].rearrange("p a n -> p (a n)"), wd_raw[0:width, j, :],
                                   wd_hi[0:width, dst, :].rearrange("p a n -> p (a n)").bitcast(F32),
                                   ALU.subtract).then_inc(wd_lo_ready, 1)

            halves_low(0, 0, P)
            for t in range(NB):
                ln_root(NB + t)
            chunks(pool, lambda c, j, width, following: following and halves_low(c + 1, 1 - j, following))

            pool.wait_ge(router_w_hi, 1)
            pool.tensor_tensor(router_wl[:, :, :], router_wr[:, :, :], router_wh[:, :, :].bitcast(F32),
                               ALU.subtract).then_inc(router_w_ready, 1)
            for s in range(NB + 3):
                if 0 <= s - 2 < NB:
                    ln_root(s - 2, 1)
                if s < NB:
                    ln_root(2 * NB + s)

            pool.wait_ge(down_done, NB)
            pool.memset(tri[:, :, :], 1.0).then_inc(tri_ready, 1)
            pool.wait_ge(tri_ready, 1)
            pool.affine_select(out=tri[:, :, :], in_=tri[:, :, :], compare_op=ALU.is_gt, fill=0.0, base=0,
                               pattern=[[1, E], [-1, E]], channel_multiplier=0).then_inc(tri_ready, 1)
            def expert_low(e, j):
                pool.wait_ge(e_hi_ready, e * 2 + 2)
                pool.tensor_tensor(e12_lo[:, j, :, :], e12_raw[:, j, :, :], e12_hi[:, j, :, :].bitcast(F32),
                                   ALU.subtract).then_inc(e_lo_ready, 1)
                pool.tensor_tensor(e3_lo[:, j, :], e3_raw[:, j, :], e3_hi[:, j, :].bitcast(F32),
                                   ALU.subtract).then_inc(e_lo_ready, 1)

            experts(pool, expert_low)

        @block.scalar
        def _(act):
            act.wait_ge(small_loaded, 64)
            act.activation(gate_rows[:, :], gate_rows[:, :], ACT.Tanh).then_inc(gates_ready, 1)

            def ln_high(i, dst, s=0):
                act.wait_ge(ln_transposed[s], i + 1)
                act.activation(dst, bank[2 * s + i % 2][:, :].rearrange("p (c n) -> p c n", c=KC), ACT.Copy)\
                   .then_inc(ln_hi_ready[s], 1)

            def wkv_high(g):
                act.wait_ge(wkv_loaded, g * 16 + 16)
                act.wait_ge(kv_done, g * (2 * PAIRS))
                act.activation(wkv_hi[:, :, :], wkv_raw[:, :, :], ACT.Copy).then_inc(wkv_hi_ready, 1)

            def wq_high(g):
                act.wait_ge(wq_loaded, g * 16 + 16)
                act.wait_ge(q_done, g * (2 * PAIRS))
                for h in range(R):
                    cols = slice(h * HD, h * HD + HD)
                    act.activation(wq_hi[:, :, cols], wq_raw[:, :, cols], ACT.Copy).then_inc(wq_hi_ready, 1)

            def wo_high(g):
                act.wait_ge(wo_loaded, g * 16 + 16)
                act.wait_ge(y_done, g * NB)
                for h in range(R):
                    act.activation(wo_hi[:, h, :], wo_raw[:, h, :], ACT.Copy).then_inc(wo_hi_ready, 1)

            def kv_high(pair, half, par):
                act.wait_ge(kv_done, pair * 2 + (half + 1))
                ps = (proj_a, proj_b)[half][:, :].rearrange("p (t n) -> p t n", t=2)
                act.activation(k_rows[:, 2 * half:2 * half + 2, :], ps[:, :, 0:HD], ACT.Copy).then_inc(k_copied, 1)
                act.activation(v_hi[:, par, 2 * half:2 * half + 2, :], ps[:, :, HD:2 * HD], ACT.Copy)\
                   .then_inc(v_hi_ready, 1)

            def k_high(pair, par):
                act.wait_ge(k_turned, pair + 1)
                act.activation(k_hi[:, par, :], proj_b[:, :], ACT.Copy, scale=head_w[:, 2:3]).then_inc(k_hi_ready, 1)

            def q_copy(pair):
                for i in range(2):
                    act.wait_ge(q_done, pair * 2 + (i + 1))
                    act.activation(q_rows[:, i, :], (proj_a, proj_b)[i][:, :], ACT.Copy).then_inc(q_copied, 1)

            def q_high(pair, par):
                for half in range(2):
                    act.wait_ge(q_turned, pair * 2 + (half + 1))
                    act.activation(q_hi[:, par, 2 * half:2 * half + 2, :].rearrange("p h n -> p (h n)"),
                                   (proj_a, proj_b)[half][:, :], ACT.Copy).then_inc(q_hi_ready, 1)

            def pt_high(n):
                for c in range(2):
                    act.wait_ge(p_turned, 2 * n + (c + 1))
                    act.activation(pt_hi[:, c, :], pt_ps[c][:, :], ACT.Copy).then_inc(pt_hi_ready, 1)

            def o_high(n, par):
                act.wait_ge(o_done, n + 1)
                act.activation(o_hi[:, par, :], o_ps[:, :], ACT.Copy).then_inc(o_hi_ready, 1)

            def exps(n, b):
                act.wait_ge(bias_ready, n + 1)
                act.wait_ge(p_turned, 2 * n)
                for h in range(R):
                    i = (b % 2) * R + h
                    act.activation(probs[:, h, :], scores_ps[h // 2][:, (h % 2) * 256:(h % 2) * 256 + 256], ACT.Exp,
                                   bias=exp_bias[:, h:h + 1], scale=q_rstd[:, (b // 2) % 2, i:i + 1],
                                   accum_out=row_sum[:, h:h + 1]).then_inc(exp_done, 1)

            for p in range(PAIRS):
                for t in (2 * p, 2 * p + 1):
                    ln_high(t, kv_src_hi[:, 1, :, t * P:(t + 1) * P])
                act.wait_ge(ctx_loaded[p], 16)
                act.activation(kv_src_hi[:, 0, :, 256 * p:256 * p + 256], ctx_raw[:, :, 256 * p:256 * p + 256],
                               ACT.Copy).then_inc(ctx_hi_ready, 1)
            wkv_high(0)
            wq_high(0)
            kv_high(0, 0, 0)
            kv_high(0, 1, 0)
            act.wait_ge(head_w_ready, 1)
            k_high(0, 0)
            q_copy(0)
            q_high(0, 0)

            def one_group(g):
                for b in range(NB):
                    n = g * NB + b
                    next_pair, par = g * PAIRS + (b // 2 + 1), (b // 2 + 1) % 2
                    prev = after_start(g, b, 1)
                    if prev:
                        pt_high(n - 1)
                    if b == 2:
                        wo_high(g)
                    if b == 6 and before_end(g, b, 2):
                        wq_high(g + 1)
                    if b % 2 == 1 and before_end(g, b, 1):
                        k_high(next_pair, par)
                    exps(n, b)
                    if prev:
                        o_high(n - 1, (b - 1) % 2)
                    if b == 5 and before_end(g, b, 3):
                        wkv_high(g + 1)
                    if b % 2 == 0 and before_end(g, b, 2):
                        for half in range(2):
                            kv_high(next_pair, half, par)
                    if b % 2 == 1 and before_end(g, b, 1):
                        q_copy(next_pair)
                        q_high(next_pair, par)

            groups(act, one_group)
            pt_high(G * NB - 1)
            o_high(G * NB - 1, 1)

            def halves_high(c, j, width):
                if not (isinstance(c, int) and c < 2):
                    act.wait_ge(gu_done, c * 4 - 4)
                act.wait_ge(gu_loaded[j], (c - j) * 16 + 32)
                act.wait_ge(wd_loaded[j], (c - j) * 8 + 16)
                act.activation(gu_hi[:, j, :, :, 0:width].rearrange("p a c n -> p (a c) n"),
                               gu_raw[:, j, :, :, 0:width].rearrange("p a c n -> p (a c) n"), ACT.Copy)\
                   .then_inc(gu_hi_ready, 1)
                act.activation(wd_hi[0:width, bass.ds(c, 1), :].rearrange("p a n -> p (a n)"), wd_raw[0:width, j, :],
                               ACT.Copy).then_inc(wd_hi_ready, 1)

            def magnitude_and_sign(k, width, cols):
                act.wait_ge(inter_step, k * 4 + 1)
                act.activation(tr_abs[0:width, 0:cols], tr_v[0:width, 0:cols], ACT.Abs).then_inc(sign_ready, 1)
                act.activation(tr_sign[0:width, 0:cols], tr_v[0:width, 0:cols], ACT.Sign, scale=-1.0)\
                   .then_inc(sign_ready, 1)

            def inner_chunk(c, j, width, following):
                if following:
                    halves_high(c + 1, 1 - j, following)
                for half in range(2):
                    act.wait_ge(gu_done, c * 4 + (2 * half + 1))
                    act.activation(silu_gate[0:width, half, :], bank[2 * half][0:width, :], ACT.Silu,
                                   scale=1.0 / 128.0).then_inc(silu_gate_ready[half], 1)
                magnitude_and_sign(c, width, 2 * D)

            act.wait_ge(y_added, G * NB)
            halves_high(0, 0, P)
            for t in range(NB):
                ln_high(NB + t, xt_hi[:, :, t * P:t * P + P])
            chunks(act, inner_chunk)

            act.wait_ge(router_loaded, 16 * 5)
            act.activation(router_wh[:, :, :], router_wr[:, :, :], ACT.Copy).then_inc(router_w_hi, 1)
            for s in range(NB + 3):
                if 0 <= s - 1 < NB:
                    ln_high(2 * NB + s - 1, q3[:, :, :])
                if s < NB:
                    magnitude_and_sign(CH + s, P, D)
                if 0 <= s - 1 < NB:
                    act.wait_ge(sim_bias_ready, s)
                    act.activation(sim[:, :], bank[6][:, 0:P], ACT.Exp, bias=sim_bias[:, :], scale=CTX_SCALE,
                                   accum_out=sim_sum[:, :]).then_inc(sim_exp, 1)
                if 0 <= s - 3 < NB:
                    t = s - 3
                    ln_high(t, xt_hi[:, :, t * P:t * P + P], 1)

            act.wait_ge(router_step, 2)
            act.activation(r_score[:, :, :], r_score[:, :, :], ACT.Exp).then_inc(router_exp, 1)

            def expert_high(e, j):
                act.wait_ge(e12_loaded[j], (e - j) * 8 + 16)
                act.wait_ge(e3_loaded[j], (e - j) * 8 + 16)
                act.activation(e12_hi[:, j, :, :], e12_raw[:, j, :, :], ACT.Copy).then_inc(e_hi_ready, 1)
                act.activation(e3_hi[:, j, :], e3_raw[:, j, :], ACT.Copy).then_inc(e_hi_ready, 1)
                act.activation(b_now[:, j, :], b12[:, bass.ds(e, 1), :].rearrange("p a n -> p (a n)"), ACT.Copy)\
                   .then_inc(b_now_ready, 1)

            def expert_act(e, j):
                for half in range(2):
                    if half == 1 and not (isinstance(e, int) and e == EA - 1):
                        if after_first(e):
                            act.wait_ge(e_done, e * 8)
                        expert_high(e + 1, 1 - j)
                    act.wait_ge(h_done, e * 4 + (2 * half + 1))
                    act.wait_ge(b_now_ready, e + 1)
                    act.activation(e_silu[:, half, :], bank[2 * half][:, :], ACT.Silu, bias=b_now[:, j, 0:1])\
                       .then_inc(silu_ready, 1)
                    act.wait_ge(h_ready, e * 2 + (half + 1))
                    act.activation(h_hi[:, half, :], e_h[:, half, :], ACT.Copy).then_inc(h_hi_ready, 1)

            act.wait_ge(down_done, NB)
            expert_high(0, 0)
            for e in range(2):
                expert_act(e, e)
            for half in range(2):
                act.wait_ge(gates_turned, half + 1)
                act.activation(gates_t[:, half * D:half * D + D], bank[2 * half][0:E + 1, :], ACT.Copy)\
                   .then_inc(gates_copied, 1)
            with act.Fori(1, EA // 2 - 1) as i:
                for j in range(2):
                    expert_act(i * 2 + j, j)
            for j in range(2):
                expert_act(EA - 2 + j, j)

        @block.vector
        def _(dve):
            dve.wait_ge(small_loaded, 64)
            dve.tensor_tensor(head_w[:, 2:3], head_w[:, 0:1], head_w[:, 1:2], ALU.mult).then_inc(head_w_ready, 1)

            def ln_stats_of(i, t, s=0):
                dve.bn_stats(ln_stats[s][:, i % 2, :], x_sb[:, t, :]).then_inc(ln_stat[s], 1)
                dve.wait_ge(ln_stat[s], 3 * i + 1)
                dve.bn_aggr(ln_mv[s][:, i % 2, :], ln_stats[s][:, i % 2, :]).then_inc(ln_stat[s], 1)
                dve.wait_ge(ln_stat[s], 3 * i + 2)
                dve.tensor_scalar(ln_var[s][:, i % 2, :], ln_mv[s][:, i % 2, 1:2], LN_EPS, None, ALU.add)\
                   .then_inc(ln_stat[s], 1)

            def ln_rows_of(i, t, s=0):
                dve.wait_ge(ln_rstd_ready[s], i + 1)
                if i >= 2:
                    dve.wait_ge(ln_transposed[s], i - 1)
                dve.tensor_scalar(ln_rows[s][:, i % 2, :], x_sb[:, t, :], ln_mv[s][:, i % 2, 0:1],
                                  ln_rstd[s][:, i % 2, :], ALU.subtract, ALU.mult).then_inc(ln_row_ready[s], 1)

            def ln_low(i, hi, lo, s=0):
                dve.wait_ge(ln_hi_ready[s], i + 1)
                dve.tensor_tensor(lo, bank[2 * s + i % 2][:, :].rearrange("p (c n) -> p c n", c=KC), hi.bitcast(F32),
                                  ALU.subtract).then_inc(ln_lo_ready[s], 1)

            def v_low(pair, half, par):
                dve.wait_ge(v_hi_ready, pair * 2 + (half + 1))
                ps = (proj_a, proj_b)[half][:, :].rearrange("p (t n) -> p t n", t=2)
                dve.tensor_tensor(v_lo[:, par, 2 * half:2 * half + 2, :], ps[:, :, HD:2 * HD],
                                  v_hi[:, par, 2 * half:2 * half + 2, :].bitcast(F32), ALU.subtract)\
                   .then_inc(v_lo_ready, 1)

            def k_norm(pair):
                dve.wait_ge(k_copied, pair * 2 + 2)
                if not (isinstance(pair, int) and pair == 0):
                    dve.wait_ge(q_ss_ready, pair * 8)
                for i in range(4):
                    dve.tensor_tensor_reduce(k_junk[:, i, :], k_rows[:, i, :], k_rows[:, i, :], 1.0 / HD, 0.0, ALU.mult,
                                             ALU.add, k_ss[:, i:i + 1]).then_inc(k_ss_ready, 1)
                dve.wait_ge(k_ss_ready, pair * 4 + 4)
                dve.tensor_scalar(k_var[:, :], k_ss[:, :], RMS_EPS, None, ALU.add).then_inc(k_var_ready, 1)

            def k_scale(pair):
                dve.wait_ge(k_rstd_ready, pair + 1)
                for i in range(4):
                    dve.tensor_scalar(k_rows[:, i, :], k_rows[:, i, :], k_rstd[:, i:i + 1], None, ALU.mult)\
                       .then_inc(k_scaled, 1)

            def k_low(pair, par):
                dve.wait_ge(k_hi_ready, pair + 1)
                dve.scalar_tensor_tensor(out=k_lo[:, par, :], in0=proj_b[:, :], scalar=head_w[:, 2:3],
                                         in1=k_hi[:, par, :].bitcast(F32), op0=ALU.mult, op1=ALU.subtract)\
                   .then_inc(k_lo_ready, 1)

            def q_norm(pair):
                for i in range(2):
                    dve.wait_ge(q_copied, pair * 2 + (i + 1))
                    if i == 0:
                        dve.wait_ge(k_ss_ready, pair * 4 + 4)
                    else:
                        dve.wait_ge(q_ss_ready, pair * 8 + 4)
                    for h in range(R):
                        row = q_rows[:, i, h * HD:h * HD + HD]
                        dve.tensor_tensor_reduce(k_junk[:, h, :], row, row, 1.0, 0.0, ALU.mult, ALU.add,
                                                 q_ss[:, i * R + h:i * R + h + 1]).then_inc(q_ss_ready, 1)
                dve.wait_ge(q_ss_ready, pair * 8 + 8)
                dve.tensor_scalar(q_var[:, :], q_ss[:, :], HD * RMS_EPS, None, ALU.add).then_inc(q_var_ready, 1)

            def q_low(pair, half, par):
                dve.wait_ge(q_hi_ready, pair * 2 + (half + 1))
                ps = (proj_a, proj_b)[half]
                two = slice(2 * half, 2 * half + 2)
                dve.tensor_tensor(q_lo[:, par, two, :].rearrange("p h n -> p (h n)"), ps[:, :],
                                  q_hi[:, par, two, :].rearrange("p h n -> p (h n)").bitcast(F32), ALU.subtract)\
                   .then_inc(q_lo_ready, 1)

            def maxima(n):
                for half in range(2):
                    dve.wait_ge(scores_done, 2 * n + (half + 1))
                    dve.tensor_reduce(row_max[:, 2 * half:2 * half + 2],
                                      scores_ps[half][:, :].rearrange("p (h n) -> p h n", h=2), AX.X, ALU.max)\
                       .then_inc(max_ready, 1)

            def bias_of(n, b):
                dve.wait_ge(max_ready, 2 * n + 2)
                i = (b % 2) * R
                dve.scalar_tensor_tensor(out=exp_bias[:, :], in0=row_max[:, :], scalar=-1.0, in1=q_rstd[:, (b // 2) % 2, i:i + R],
                                         op0=ALU.mult, op1=ALU.mult).then_inc(bias_ready, 1)

            def pt_low(n):
                for c in range(2):
                    dve.wait_ge(pt_hi_ready, 2 * n + (c + 1))
                    dve.tensor_tensor(pt_lo[:, c, :], pt_ps[c][:, :], pt_hi[:, c, :].bitcast(F32), ALU.subtract)\
                       .then_inc(pt_lo_ready, 1)

            def o_low(n, par):
                dve.wait_ge(o_hi_ready, n + 1)
                dve.tensor_tensor(o_lo[:, par, :], o_ps[:, :], o_hi[:, par, :].bitcast(F32), ALU.subtract)\
                   .then_inc(o_lo_ready, 1)

            def normalise(n):
                dve.wait_ge(exp_done, 4 * n + 4)
                dve.reciprocal(row_inv[:, :], row_sum[:, :]).then_inc(inv_ready, 1)
                dve.wait_ge(inv_ready, n + 1)
                for h in range(R):
                    dve.tensor_scalar(probs[:, h, :], probs[:, h, :], row_inv[:, h:h + 1], None, ALU.mult)\
                       .then_inc(probs_ready, 1)

            def add_y(n, b):
                dve.wait_ge(y_done, n + 1)
                dve.scalar_tensor_tensor(out=x_sb[:, b, :], in0=y_ps[:, :], scalar=gate_rows[:, 0:1],
                                         in1=x_sb[:, b, :], op0=ALU.mult, op1=ALU.add).then_inc(y_added, 1)

            for p in range(PAIRS):
                dve.wait_ge(x_loaded[p], 16)
                for t in (2 * p, 2 * p + 1):
                    ln_stats_of(t, t)
                for t in (2 * p, 2 * p + 1):
                    ln_rows_of(t, t)
                for t in (2 * p, 2 * p + 1):
                    tok = slice(t * P, (t + 1) * P)
                    ln_low(t, kv_src_hi[:, 1, :, tok], kv_src_lo[:, 1, :, tok])
                dve.wait_ge(ctx_hi_ready, p + 1)
                tok = slice(256 * p, 256 * p + 256)
                dve.tensor_tensor(kv_src_lo[:, 0, :, tok], ctx_raw[:, :, tok], kv_src_hi[:, 0, :, tok].bitcast(F32),
                                  ALU.subtract).then_inc(ctx_lo_ready, 1)
            dve.wait_ge(gates_ready, 1)
            v_low(0, 0, 0)
            v_low(0, 1, 0)
            k_norm(0)
            k_scale(0)
            k_low(0, 0)
            q_norm(0)
            q_low(0, 0, 0)
            q_low(0, 1, 0)

            def one_group(g):
                for b in range(NB):
                    n = g * NB + b
                    next_pair, par = g * PAIRS + (b // 2 + 1), (b // 2 + 1) % 2
                    if after_start(g, b, 3):
                        add_y(n - 3, (b - 3) % NB)
                    maxima(n)
                    if after_start(g, b, 1):
                        pt_low(n - 1)
                    if b % 2 == 1 and before_end(g, b, 1):
                        k_low(next_pair, par)
                    if b % 2 == 0:
                        dve.wait_ge(q_rstd_ready, g * PAIRS + (b // 2 + 1))
                    bias_of(n, b)
                    if after_start(g, b, 1):
                        o_low(n - 1, (b - 1) % 2)
                    normalise(n)
                    if b % 2 == 1 and before_end(g, b, 1):
                        q_norm(next_pair)
                    for half in range(2):
                        if b % 2 == 0 and before_end(g, b, 2):
                            v_low(next_pair, half, par)
                        if b % 2 == 1 and before_end(g, b, 1):
                            q_low(next_pair, half, par)
                    if b % 2 == 0 and before_end(g, b, 2):
                        k_norm(next_pair)
                        k_scale(next_pair)

            groups(dve, one_group)
            last = G * NB - 1
            add_y(last - 2, NB - 3)
            pt_low(last)
            o_low(last, 1)
            add_y(last - 1, NB - 2)
            add_y(last, NB - 1)

            for t in range(0, NB, 2):
                for u in (t, t + 1):
                    ln_stats_of(NB + u, u)
                for u in (t, t + 1):
                    ln_rows_of(NB + u, u)
                for u in (t, t + 1):
                    tok = slice(u * P, u * P + P)
                    ln_low(NB + u, xt_hi[:, :, tok], xt_lo[:, :, tok])

            def truncate(k, width, cols, dst, done):
                part = lambda t: t[0:width, 0:cols]
                dve.wait_ge(sign_ready, k * 2 + 1)
                dve.tensor_scalar(part(tr_int), part(tr_abs), ROUND, ROUND, ALU.add, ALU.subtract)\
                   .then_inc(inter_step, 1)
                dve.wait_ge(inter_step, k * 4 + 2)
                dve.tensor_tensor(part(tr_v), part(tr_int), part(tr_abs), ALU.subtract).then_inc(inter_step, 1)
                dve.wait_ge(inter_step, k * 4 + 3)
                dve.scalar_tensor_tensor(out=part(tr_v), in0=part(tr_v), scalar=0.0, in1=part(tr_int),
                                         op0=ALU.is_gt, op1=ALU.subtract).then_inc(inter_step, 1)
                dve.wait_ge(inter_step, k * 4 + 4)
                dve.tensor_tensor(dst, part(tr_v), part(tr_sign), ALU.mult).then_inc(done, 1)

            def inner_chunk(c, j, width, following):
                if after_first(c):
                    dve.wait_ge(iq_ready, c)
                for half in range(2):
                    dve.wait_ge(silu_gate_ready[half], c + 1)
                    dve.wait_ge(gu_done, c * 4 + (2 * half + 2))
                    dve.tensor_tensor(tr_v[0:width, half * D:half * D + D], silu_gate[0:width, half, :],
                                      bank[2 * half + 1][0:width, :], ALU.mult).then_inc(inter_ready[half], 1)
                dve.wait_ge(inter_ready[1], c + 1)
                dve.wait_ge(inter_ready[0], c + 1)
                dve.tensor_scalar(tr_v[0:width, :], tr_v[0:width, :], 127.0, -128.0, ALU.min, ALU.max)\
                   .then_inc(inter_step, 1)
                dve.wait_ge(sign_ready, c * 2 + 2)
                truncate(c, width, 2 * D, iq[0:width, bass.ds(c, 1), :].rearrange("p a n -> p (a n)"), iq_ready)

            chunks(dve, inner_chunk)

            def down_tile(t):
                k = CH + t
                dve.wait_ge(iq_ready, k)
                dve.wait_ge(down_done, t + 1)
                dve.tensor_scalar(tr_v[:, 0:D], bank[4 + t % 2][:, :], 128.0, 127.0, ALU.mult, ALU.min)\
                   .then_inc(down_taken, 1)
                dve.wait_ge(down_taken, t + 1)
                dve.tensor_scalar(tr_v[:, 0:D], tr_v[:, 0:D], -128.0, None, ALU.max).then_inc(inter_step, 1)
                dve.wait_ge(sign_ready, k * 2 + 2)
                truncate(k, P, D, tr_int[:, D:2 * D], iq_ready)
                dve.wait_ge(iq_ready, k + 1)
                dve.scalar_tensor_tensor(out=x_sb[:, t, :], in0=tr_int[:, D:2 * D], scalar=gate_rows[:, 2:3],
                                         in1=x_sb[:, t, :], op0=ALU.mult, op1=ALU.add).then_inc(x2_ready, 1)
                dve.wait_ge(x2_ready, t + 1)
                ln_stats_of(2 * NB + t, t)

            def sim_max_of(t):
                dve.wait_ge(sim_done, t + 1)
                dve.tensor_reduce(sim_max[:, :], bank[6][:, 0:P], AX.X, ALU.max).then_inc(sim_max_ready, 1)
                dve.wait_ge(sim_max_ready, t + 1)
                dve.tensor_scalar(sim_bias[:, :], sim_max[:, :], -CTX_SCALE, None, ALU.mult).then_inc(sim_bias_ready, 1)

            def sim_norm(t):
                dve.wait_ge(sim_exp, t + 1)
                dve.reciprocal(sim_inv[:, :], sim_sum[:, :]).then_inc(sim_inv_ready, 1)
                dve.wait_ge(sim_inv_ready, t + 1)
                dve.tensor_scalar(sim[:, :], sim[:, :], sim_inv[:, :], None, ALU.mult).then_inc(sim_ready, 1)

            def add_context(t):
                dve.wait_ge(context_done, t + 1)
                dve.scalar_tensor_tensor(out=x_sb[:, t, :], in0=bank[7][:, :], scalar=gate_rows[:, 1:2],
                                         in1=x_sb[:, t, :], op0=ALU.mult, op1=ALU.add).then_inc(x3_ready, 1)
                dve.wait_ge(x3_ready, t + 1)
                ln_stats_of(t, t, 1)

            for s in range(NB + 3):
                if 0 <= s - 1 < NB:
                    ln_rows_of(2 * NB + s - 1, s - 1)
                if 0 <= s - 2 < NB:
                    add_context(s - 2)
                if 0 <= s - 3 < NB:
                    ln_rows_of(s - 3, s - 3, 1)
                if s < NB:
                    down_tile(s)
                if 0 <= s - 1 < NB:
                    sim_max_of(s - 1)
                if 0 <= s - 3 < NB:
                    t = s - 3
                    tok = slice(t * P, t * P + P)
                    ln_low(t, xt_hi[:, :, tok], xt_lo[:, :, tok], 1)
                if 0 <= s - 1 < NB:
                    sim_norm(s - 1)
                if 0 <= s - 3 < NB:
                    dve.wait_ge(router_done, t + 1)
                    dve.tensor_tensor(logits[:, t, :], bank[2 + t % 2][:, 0:E], router_rows[:, 0, :], ALU.add)\
                       .then_inc(logits_ready, 1)

            steps = [0]

            def step(ins):
                steps[0] += 1
                ins.then_inc(router_step, 1)
                dve.wait_ge(router_step, steps[0])

            def spread(ap, n):
                return ap.unsqueeze(len(ap.shape)).broadcast_to(list(ap.shape) + [n])

            dve.wait_ge(logits_ready, NB)
            dve.wait_ge(down_done, NB)
            step(dve.tensor_reduce(r_stat[:, 0, :], logits[:, :, :], AX.X, ALU.max))
            step(dve.tensor_tensor(r_score[:, :, :], logits[:, :, :], spread(r_stat[:, 0, :], E), ALU.subtract))
            dve.wait_ge(router_exp, 1)
            step(dve.tensor_reduce(r_stat[:, 1, :], r_score[:, :, :], AX.X, ALU.add))
            step(dve.reciprocal(r_stat[:, 2, :], r_stat[:, 1, :]))
            step(dve.tensor_tensor(r_score[:, :, :], r_score[:, :, :], spread(r_stat[:, 2, :], E), ALU.mult))
            step(dve.tensor_tensor(r_score[:, :, :], r_score[:, :, :],
                                   router_rows[:, 1, :].unsqueeze(1).broadcast_to([P, NB, E]), ALU.add))
            by_group = lambda t: t[:, :, :].rearrange("p t (g e) -> p t g e", g=EG)

            def ranks(values, n, gt, eq, out_rank):
                others = values.unsqueeze(2).broadcast_to([P, NB, n, n])
                own = spread(values, n)
                first = tri[:, 0:n, 0:n].unsqueeze(1).broadcast_to([P, NB, n, n])
                step(dve.tensor_tensor(gt, others, own, ALU.is_gt))
                step(dve.tensor_tensor(eq, others, own, ALU.is_equal))
                step(dve.tensor_tensor(eq, eq, first, ALU.mult))
                step(dve.tensor_tensor(gt, gt, eq, ALU.add))
                step(dve.tensor_reduce(out_rank, gt, AX.X, ALU.add))

            dve.wait_ge(tri_ready, 2)
            step(dve.tensor_reduce(r_gmax[:, :, :], by_group(r_score), AX.X, ALU.max))
            ranks(r_gmax[:, :, :], EG, r_gt[:, :, 0:EG, 0:EG], r_eq[:, :, 0:EG, 0:EG], r_low[:, :, :])
            step(dve.tensor_scalar(r_keep[:, :, :], r_low[:, :, :], 1.5, None, ALU.is_lt))
            step(dve.tensor_scalar(r_low[:, :, :], r_keep[:, :, :], -1.0, -LOW, ALU.add, ALU.mult))
            step(dve.tensor_tensor(by_group(r_masked), by_group(r_score), spread(r_keep[:, :, :], E // EG), ALU.mult))
            step(dve.tensor_tensor(by_group(r_masked), by_group(r_masked), spread(r_low[:, :, :], E // EG), ALU.add))
            ranks(r_masked[:, :, :], E, r_gt[:, :, :, :], r_eq[:, :, :, :], r_rank[:, :, :])
            step(dve.tensor_scalar(r_rank[:, :, :], r_rank[:, :, :], 1.5, None, ALU.is_lt))
            step(dve.memset(gates[:, :, 0:2], 1.0))
            dve.tensor_tensor(gates[:, :, 2:EA], r_score[:, :, :], r_rank[:, :, :], ALU.mult).then_inc(gates_ready4, 1)
            dve.memset(y_acc[:, :, :], 0.0).then_inc(y_zeroed, 1)
            dve.wait_ge(gates_ready4, 1)
            dve.wait_ge(y_zeroed, 1)

            def hidden(e, j, half):
                dve.wait_ge(silu_ready, e * 2 + (half + 1))
                dve.wait_ge(h_done, e * 4 + (2 * half + 2))
                dve.scalar_tensor_tensor(out=e_h[:, half, :], in0=bank[2 * half + 1][:, :],
                                         scalar=b_now[:, j, 1:2], in1=e_silu[:, half, :],
                                         op0=ALU.add, op1=ALU.mult).then_inc(h_ready, 1)
                dve.wait_ge(h_hi_ready, e * 2 + (half + 1))
                dve.tensor_tensor(h_lo[:, half, :], e_h[:, half, :], h_hi[:, half, :].bitcast(F32),
                                  ALU.subtract).then_inc(h_lo_ready, 1)

            def add_expert(e, half):
                for i in range(4):
                    t = 4 * half + i
                    dve.wait_ge(e_done, e * 8 + (t + 1))
                    dve.scalar_tensor_tensor(out=y_acc[:, t, :], in0=bank[4 + i][:, :],
                                             scalar=gates[:, t, bass.ds(e, 1)], in1=y_acc[:, t, :],
                                             op0=ALU.mult, op1=ALU.add).then_inc(e_added, 1)

            def expert_dve(e, j):
                hidden(e, j, 0)
                if after_first(e):
                    add_expert(e - 1, 1)
                hidden(e, j, 1)
                add_expert(e, 0)

            for e in range(2):
                expert_dve(e, e)
            add_expert(1, 1)
            for t in range(NB):
                dve.wait_ge(bias_done, t + 1)
                dve.tensor_tensor(y_acc[:, t, :], bank[4 + t % 4][:, :], y_acc[:, t, :], ALU.add)\
                   .then_inc(bias_added, 1)
            dve.wait_ge(bias_added, NB)
            hidden(2, 0, 0)
            hidden(2, 0, 1)
            add_expert(2, 0)
            expert_dve(3, 1)
            with dve.Fori(2, EA // 2) as i:
                for j in range(2):
                    expert_dve(i * 2 + j, j)
            add_expert(EA - 1, 1)
            for t in range(NB):
                dve.wait_ge(e_added, 8 * (EA - 1) + t + 1)
                dve.scalar_tensor_tensor(out=x_sb[:, t, :], in0=y_acc[:, t, :], scalar=gate_rows[:, 3:4],
                                         in1=x_sb[:, t, :], op0=ALU.mult, op1=ALU.add).then_inc(x4_ready, 1)

        @block.tensor
        def _(pe):
            pe.wait_ge(consts_ready, 3)

            def turn_rows(i, s=0):
                pe.wait_ge(ln_row_ready[s], i + 1)
                for c in range(KC):
                    mm = pe.transpose(bank[2 * s + i % 2][:, c * P:c * P + P], ln_rows[s][:, i % 2, c * P:c * P + P],
                                      ident[:, :])
                mm.then_inc(ln_transposed[s], 1)

            def kv_tile(pair, p, i):
                half = i // 2
                tok = slice((2 * p + half) * P, (2 * p + half) * P + P)
                ps = (proj_a, proj_b)[half][:, (i % 2) * 256:(i % 2) * 256 + 256]
                for c in range(KC):
                    mm = three(pe, ps, kv_src_hi[:, i % 2, c, tok], kv_src_lo[:, i % 2, c, tok],
                               wkv_hi[:, c, :], wkv_lo[:, c, :], c == 0, c == KC - 1)
                if i % 2 == 1:
                    mm.then_inc(kv_done, 1)

            def q_tile(p, i):
                tok = slice((2 * p + i) * P, (2 * p + i) * P + P)
                for c in range(KC):
                    mm = three(pe, (proj_a, proj_b)[i][:, :], kv_src_hi[:, 1, c, tok], kv_src_lo[:, 1, c, tok],
                               wq_hi[:, c, :], wq_lo[:, c, :], c == 0, c == KC - 1)
                mm.then_inc(q_done, 1)

            def turn_q(pair):
                pe.wait_ge(q_copied, pair * 2 + 2)
                for half in range(2):
                    for h in range(2):
                        for i in range(2):
                            at_h = (2 * half + h) * HD
                            mm = pe.transpose((proj_a, proj_b)[half][:, h * 256 + i * P:h * 256 + i * P + P],
                                              q_rows[:, i, at_h:at_h + HD], ident[:, :])
                    mm.then_inc(q_turned, 1)

            def kv_half(g, p, half):
                pair = g * PAIRS + p
                if half == 0:
                    if p == 0:
                        pe.wait_ge(wkv_lo_ready, g + 1)
                    if after_start(g, 2 * p, 1):
                        pe.wait_ge(q_lo_ready, pair * 2 - 1)
                elif after_start(g, 2 * p, 1):
                    pe.wait_ge(q_lo_ready, pair * 2)
                kv_tile(pair, p, 2 * half)
                kv_tile(pair, p, 2 * half + 1)

            def q_half(g, p, half):
                pair = g * PAIRS + p
                if half == 0:
                    if p == 0:
                        pe.wait_ge(wq_lo_ready, g * R + R)
                    pe.wait_ge(v_lo_ready, pair * 2 + 1)
                    pe.wait_ge(k_copied, pair * 2 + 1)
                else:
                    pe.wait_ge(k_lo_ready, pair + 1)
                q_tile(p, half)

            def turn_k(pair):
                pe.wait_ge(k_scaled, pair * 4 + 4)
                pe.wait_ge(v_lo_ready, pair * 2 + 2)
                for i in range(4):
                    mm = pe.transpose(proj_b[:, i * P:i * P + P], k_rows[:, i, :], ident[:, :])
                mm.then_inc(k_turned, 1)

            def scores(g, b, half):
                n, pair, par = g * NB + b, g * PAIRS + b // 2, (b // 2) % 2
                pe.wait_ge(q_lo_ready, pair * 2 + (half + 1))
                pe.wait_ge(k_lo_ready, pair + 1)
                if after_start(g, b, 1):
                    pe.wait_ge(exp_done, n * 4 - 2 + 2 * half)
                i = b % 2
                for h in (2 * half, 2 * half + 1):
                    mm = three(pe, scores_ps[half][:, (h % 2) * 256:(h % 2) * 256 + 256],
                               q_hi[:, par, h, i * P:i * P + P], q_lo[:, par, h, i * P:i * P + P],
                               k_hi[:, par, i * 256:i * 256 + 256], k_lo[:, par, i * 256:i * 256 + 256], True, True)
                mm.then_inc(scores_done, 1)

            def turn_probs(n):
                pe.wait_ge(probs_ready, n * 4 + 4)
                for c in range(2):
                    for h in range(R):
                        mm = pe.transpose(pt_ps[c][:, h * P:h * P + P], probs[:, h, c * P:c * P + P], ident[:, :])
                    mm.then_inc(p_turned, 1)

            def weigh_values(g, b):
                n, pair = g * NB + b, g * PAIRS + b // 2
                par, i = (b // 2) % 2, b % 2
                pe.wait_ge(pt_lo_ready, n * 2 + 2)
                pe.wait_ge(v_lo_ready, pair * 2 + 2)
                if after_start(g, b, 1):
                    pe.wait_ge(o_lo_ready, n)
                for c in range(2):
                    mm = three(pe, o_ps[:, :], v_hi[:, par, 2 * i + c, :], v_lo[:, par, 2 * i + c, :],
                               pt_hi[:, c, :], pt_lo[:, c, :], c == 0, c == 1)
                mm.then_inc(o_done, 1)

            def project_out(g, b, heads=range(R)):
                n, par = g * NB + b, b % 2
                if heads[0] == 0:
                    pe.wait_ge(o_lo_ready, n + 1)
                    if after_start(g, b, 1):
                        pe.wait_ge(y_added, n)
                for h in heads:
                    if b == 0:
                        pe.wait_ge(wo_lo_ready, g * R + (h + 1))
                    mm = three(pe, y_ps[:, :], o_hi[:, par, h * P:h * P + P], o_lo[:, par, h * P:h * P + P],
                               wo_hi[:, h, :], wo_lo[:, h, :], h == 0, h == R - 1)
                if heads[-1] == R - 1:
                    mm.then_inc(y_done, 1)

            for t in range(NB):
                if t >= 2:
                    pe.wait_ge(ln_lo_ready[0], t - 1)
                turn_rows(t)
            pe.wait_ge(ctx_lo_ready, PAIRS)
            pe.wait_ge(ln_lo_ready[0], NB)
            kv_half(0, 0, 0)
            kv_half(0, 0, 1)
            turn_k(0)
            q_half(0, 0, 0)
            q_half(0, 0, 1)
            turn_q(0)

            def one_group(g):
                for b in range(NB):
                    n = g * NB + b
                    ng, np_ = (g, b // 2 + 1) if b < NB - 2 else (g + 1, 0)
                    if after_start(g, b, 1):
                        turn_probs(n - 1)
                    scores(g, b, 0)
                    scores(g, b, 1)
                    ahead = before_end(g, b - b % 2, 2)
                    if b % 2 == 1 and ahead:
                        turn_k(g * PAIRS + (b // 2 + 1))
                    if ahead:
                        (kv_half, q_half)[b % 2](ng, np_, 0)
                    if after_start(g, b, 1):
                        weigh_values(g, b - 1)
                    if ahead:
                        (kv_half, q_half)[b % 2](ng, np_, 1)
                    back = (g, b - 2) if b >= 2 else (g - 1, b + NB - 2)
                    if after_start(g, b, 2):
                        project_out(*back, range(0, 2))
                    if b % 2 == 1 and ahead:
                        turn_q(g * PAIRS + (b // 2 + 1))
                    if after_start(g, b, 2):
                        project_out(*back, range(2, R))

            groups(pe, one_group)
            turn_probs(G * NB - 1)
            weigh_values(G - 1, NB - 1)
            project_out(G - 1, NB - 2)
            project_out(G - 1, NB - 1)

            for t in range(NB):
                if t >= 2:
                    pe.wait_ge(ln_lo_ready[0], NB + t - 1)
                turn_rows(NB + t)
            pe.wait_ge(ln_lo_ready[0], 2 * NB)

            def inner_chunk(c, j, width, following):
                pe.wait_ge(gu_lo_ready, c + 1)
                for half in range(2):
                    if after_first(c):
                        pe.wait_ge(inter_ready[half], c)
                    tok = slice(half * D, half * D + D)
                    for i in range(2):
                        for k in range(KC):
                            mm = three(pe, bank[2 * half + i][0:width, :], gu_hi[:, j, i, k, 0:width],
                                       gu_lo[:, j, i, k, 0:width], xt_hi[:, k, tok], xt_lo[:, k, tok],
                                       k == 0, k == KC - 1)
                        mm.then_inc(gu_done, 1)

            chunks(pe, inner_chunk)

            def down(t):
                if t == 0:
                    pe.wait_ge(iq_ready, CH)
                    pe.wait_ge(wd_lo_ready, CH)
                if t >= 2:
                    pe.wait_ge(down_taken, t - 1)
                tok = slice(t * P, t * P + P)
                for c in range(CH):
                    rows = P if c < CH - 1 else TAIL
                    for w in (wd_lo, wd_hi):
                        mm = pe.matmul(bank[4 + t % 2][:, :], iq[0:rows, c, tok], w[0:rows, c, :],
                                       start=(c == 0 and w is wd_lo), stop=(c == CH - 1 and w is wd_hi))
                mm.then_inc(down_done, 1)

            def similarity(t):
                pe.wait_ge(ln_hi_ready[0], 2 * NB + t + 1)
                pe.wait_ge(ctx3_cols_loaded[t % 2], 16 * (t // 2 + 1))
                if t >= 1:
                    pe.wait_ge(sim_exp, t)
                for c in range(KC):
                    mm = pe.matmul(bank[6][:, 0:P], q3[:, c, :], ctx_cols[:, t % 2, c, :], start=(c == 0),
                                   stop=(c == KC - 1))
                mm.then_inc(sim_done, 1)

            def context(t):
                pe.wait_ge(sim_ready, t + 1)
                pe.wait_ge(ctx3_rows_loaded[t % 2], 16 * (t // 2 + 1))
                if t >= 1:
                    pe.wait_ge(x3_ready, t)
                pe.matmul(bank[7][:, :], sim[:, :], ctx_rows[:, t % 2, :], start=True, stop=True)\
                  .then_inc(context_done, 1)

            def route(t):
                pe.wait_ge(ln_lo_ready[1], t + 1)
                if t == 0:
                    pe.wait_ge(router_w_ready, 1)
                tok = slice(t * P, t * P + P)
                for c in range(KC):
                    mm = three(pe, bank[2 + t % 2][:, 0:E], xt_hi[:, c, tok], xt_lo[:, c, tok],
                               router_wh[:, c, :], router_wl[:, c, :], c == 0, c == KC - 1)
                mm.then_inc(router_done, 1)

            for s in range(NB + 3):
                if 0 <= s - 1 < NB:
                    if s >= 3:
                        pe.wait_ge(ln_hi_ready[0], 2 * NB + s - 2)
                    turn_rows(2 * NB + s - 1)
                if 0 <= s - 2 < NB:
                    context(s - 2)
                if s < NB:
                    down(s)
                if 0 <= s - 1 < NB:
                    similarity(s - 1)
                if 0 <= s - 3 < NB:
                    if s - 3 >= 2:
                        pe.wait_ge(logits_ready, s - 4)
                    turn_rows(s - 3, 1)
                    route(s - 3)

            def inner(e, j, half):
                if half == 0:
                    pe.wait_ge(e_lo_ready, e * 2 + 2)
                if after_first(e):
                    pe.wait_ge(h_ready, e * 2 + (half - 1))
                tok = slice(half * D, half * D + D)
                for i in range(2):
                    for k in range(KC):
                        mm = three(pe, bank[2 * half + i][:, :], e12_hi[:, j, i * KC + k, :], e12_lo[:, j, i * KC + k, :],
                                   xt_hi[:, k, tok], xt_lo[:, k, tok], k == 0, k == KC - 1)
                    mm.then_inc(h_done, 1)

            def outer(e, j, half):
                pe.wait_ge(h_lo_ready, e * 2 + (half + 1))
                for i in range(4):
                    if after_first(e) or half == 1:
                        pe.wait_ge(e_added, e * 8 + (4 * half + i - 3))
                    tok = slice(i * P, i * P + P)
                    three(pe, bank[4 + i][:, :], h_hi[:, half, tok], h_lo[:, half, tok], e3_hi[:, j, :], e3_lo[:, j, :],
                          True, True).then_inc(e_done, 1)

            def expert_pe(e, j):
                inner(e, j, 0)
                if after_first(e):
                    outer(e - 1, 1 - j, 1)
                inner(e, j, 1)
                outer(e, j, 0)

            pe.wait_ge(logits_ready, NB)
            for e in range(2):
                expert_pe(e, e)
            outer(1, 1, 1)
            pe.wait_ge(gates_ready4, 1)
            pe.wait_ge(h_ready, 4)
            for half in range(2):
                for i in range(4):
                    mm = pe.transpose(bank[2 * half][0:E + 1, i * P:i * P + P], gates[:, 4 * half + i, 1:EA], ident[:, :])
                mm.then_inc(gates_turned, 1)
            pe.wait_ge(gates_copied, 2)
            for t in range(NB):
                if t < 4:
                    pe.wait_ge(e_added, 12 + t + 1)
                else:
                    pe.wait_ge(bias_added, t - 3)
                pe.matmul(bank[4 + t % 4][:, :], gates_t[:, t * P:t * P + P], b3[:, :], start=True, stop=True)\
                  .then_inc(bias_done, 1)
            pe.wait_ge(bias_added, NB)
            inner(2, 0, 0)
            inner(2, 0, 1)
            outer(2, 0, 0)
            expert_pe(3, 1)
            with pe.Fori(2, EA // 2) as i:
                for j in range(2):
                    expert_pe(i * 2 + j, j)
            outer(EA - 1, 1, 1)


def kernel(**inputs):
    import numpy as np
    import concourse.bacc as bacc
    from concourse.bass_utils import run_bass_kernel_spmd

    nc = bacc.Bacc("TRN2", target_bir_lowering=False, num_devices=1)
    a = {k: np.asarray(v) for k, v in inputs.items()}
    wq = a["L0_xattn_Wq"].reshape(KC, P, G, R * HD).transpose(2, 1, 0, 3)
    wk = a["L0_xattn_Wk"].reshape(KC, P, G, HD).transpose(2, 1, 0, 3)
    wv = a["L0_xattn_Wv"].reshape(KC, P, G, HD).transpose(2, 1, 0, 3)

    def by_expert(shared, routed):
        s = a["L1_ffn_" + shared].reshape(KC, P, 2, P).transpose(2, 1, 0, 3)
        return np.concatenate([s, a["L1_ffn_" + routed].reshape(E, KC, P, P).transpose(0, 2, 1, 3)], axis=0)

    arrays = {
        "x": a["x"],
        "ctx_t": a["ctx_4096"].reshape(NB * P, KC, P).transpose(2, 1, 0),
        "g_xattn": a["g_xattn"].reshape(1, 2),
        "g_ffn": a["g_ffn"].reshape(1, 2),
        "wq": wq,
        "wkv": np.concatenate([wk, wv], axis=3),
        "wo": a["L0_xattn_Wo"].reshape(G, R, HD, D).transpose(0, 2, 1, 3),
        "q_w": a["L0_xattn_q_norm_w"].reshape(HD, 1),
        "k_w": a["L0_xattn_k_norm_w"].reshape(HD, 1),
        "ctx": a["ctx_4096"],
        "w_gate": a["L0_ffn_w_gate"].T.reshape(KC, P, INTER).transpose(1, 0, 2),
        "w_up": a["L0_ffn_w_up"].T.reshape(KC, P, INTER).transpose(1, 0, 2),
        "w_down": a["L0_ffn_w_down"].T,
        "router_w": a["L1_ffn_router_w"].reshape(KC, P, E).transpose(1, 0, 2),
        "router_b": a["L1_ffn_router_b"].reshape(1, E),
        "router_bias": a["L1_ffn_router_bias"].reshape(1, E),
        "e_w12": np.concatenate([by_expert("sw1", "ew1"), by_expert("sw2", "ew2")], axis=2),
        "e_w3": np.concatenate([a["L1_ffn_sw3"].reshape(2, P, D), a["L1_ffn_ew3"]], axis=0),
        "e_b12": np.stack([np.concatenate([a[f"L1_ffn_sb{i}"].reshape(2, P), a[f"L1_ffn_eb{i}"]], axis=0).T
                           for i in (1, 2)], axis=2),
        "e_b3": np.concatenate([a["L1_ffn_sb3"].reshape(1, D), a["L1_ffn_eb3"]], axis=0),
    }
    arrays = {k: np.ascontiguousarray(v) for k, v in arrays.items()}
    args = {k: nc.dram_tensor(k, v.shape, mybir.dt.from_np(v.dtype), kind="ExternalInput").ap()
            for k, v in arrays.items()}
    out = nc.dram_tensor("out", (NB, P, D), F32, kind="ExternalOutput").ap()
    build(nc, out=out, **args)
    r = run_bass_kernel_spmd(nc, [arrays], core_ids=[0])
    return r.results[0]["out"]
```

```python
from contextlib import ExitStack

import concourse.bass as bass
from concourse import mybir

F32 = mybir.dt.float32
F32R = mybir.dt.float32r
ALU = mybir.AluOpType
ACT = mybir.ActivationFunctionType
AX = mybir.AxisListType

P = 128
D = 512
KC = D // P
NB = 8
G = 8
R = 4
PAIRS = NB // 2
HD = 128
RMS_EPS = 1e-6
LN_EPS = 1e-5
INTER = 1376
CH = -(-INTER // P)
TAIL = INTER - (CH - 1) * P
ROUND = 1.5 * 2.0 ** 23
E = 16
EG = 4
EA = E + 2
CTX_SCALE = float(P) ** -0.5
LOW = -3.0e38


def build(nc, x, ctx, ctx_t, g_xattn, g_ffn, wq, wkv, wo, q_w, k_w, w_gate, w_up, w_down, router_w, router_b,
          router_bias, e_w12, e_w3, e_b12, e_b3, out):
    with ExitStack() as top:
        def sb(name, shape, dt=F32, scope=top):
            return scope.enter_context(nc.sbuf_tensor(name, shape, dt))

        def sem(name):
            return top.enter_context(nc.semaphore(name))

        x_sb = sb("x_sb", [P, NB, D])
        ident = sb("ident", [P, P])
        minus_half = sb("minus_half", [P, 16])
        gate_rows = sb("gate_rows", [P, 4])
        head_w = sb("head_w", [P, 3])
        ln_stats = [sb(f"ln_stats{i}", [P, 2, 6]) for i in range(2)]
        ln_mv = [sb(f"ln_mv{i}", [P, 2, 2]) for i in range(2)]
        ln_var = [sb(f"ln_var{i}", [P, 2, 1]) for i in range(2)]
        ln_rstd = [sb(f"ln_rstd{i}", [P, 2, 1]) for i in range(2)]
        first_rows = sb("first_rows", [P, 2, D])

        router_wr = sb("router_wr", [P, KC, E])
        router_wh = sb("router_wh", [P, KC, E], F32R)
        router_wl = sb("router_wl", [P, KC, E], F32R)
        router_rows = sb("router_rows", [P, 2, E])
        b12 = sb("b12", [P, EA, 2])
        b_now = sb("b_now", [P, 2, 2])
        logits = sb("logits", [P, NB, E])
        gates = sb("gates", [P, NB, EA])
        start = nc.sbuf_base
        at = [start]

        def put(name, shape, dt=F32):
            size = 4
            for n in shape[1:]:
                size *= n
            t = nc.alloc_sbuf_tensor_at(name, shape, dt, offset=at[0])
            at[0] += -(-size // 32) * 32
            return t

        kv_src_hi = put("kv_src_hi", [P, 2, KC, NB * P], F32R)
        kv_src_lo = put("kv_src_lo", [P, 2, KC, NB * P], F32R)
        wq_raw = put("wq_raw", [P, KC, R * HD])
        wq_hi = put("wq_hi", [P, KC, R * HD], F32R)
        wq_lo = put("wq_lo", [P, KC, R * HD], F32R)
        wkv_raw = put("wkv_raw", [P, KC, 2 * HD])
        wkv_hi = put("wkv_hi", [P, KC, 2 * HD], F32R)
        wkv_lo = put("wkv_lo", [P, KC, 2 * HD], F32R)
        wo_raw = put("wo_raw", [P, R, D])
        wo_hi = put("wo_hi", [P, R, D], F32R)
        wo_lo = put("wo_lo", [P, R, D], F32R)
        q_hi = put("q_hi", [P, 2, R, 2 * P], F32R)
        q_lo = put("q_lo", [P, 2, R, 2 * P], F32R)
        k_hi = put("k_hi", [P, 2, 4 * P], F32R)
        k_lo = put("k_lo", [P, 2, 4 * P], F32R)
        v_hi = put("v_hi", [P, 2, 4, HD], F32R)
        v_lo = put("v_lo", [P, 2, 4, HD], F32R)
        q_rows = put("q_rows", [P, 2, R * HD])
        q_ss = put("q_ss", [P, 2 * R])
        k_rows = put("k_rows", [P, 4, HD])
        k_junk = put("k_junk", [P, 4, HD])
        k_ss, k_var, k_rstd = put("k_ss", [P, 4]), put("k_var", [P, 4]), put("k_rstd", [P, 4])
        q_var, q_rstd = put("q_var", [P, 2 * R]), put("q_rstd", [P, 2, 2 * R])
        row_max, exp_bias = put("row_max", [P, R]), put("exp_bias", [P, R])
        row_sum, row_inv = put("row_sum", [P, R]), put("row_inv", [P, R])
        probs = put("probs", [P, R, 2 * P])
        here = at[0]
        ctx_raw = put("ctx_raw", [P, KC, NB * P])
        at[0] = here
        pt_hi = put("pt_hi", [P, 2, R * P], F32R)
        pt_lo = put("pt_lo", [P, 2, R * P], F32R)
        o_hi = put("o_hi", [P, 2, R * P], F32R)
        o_lo = put("o_lo", [P, 2, R * P], F32R)

        at[0] = start
        gu_raw = put("gu_raw", [P, 2, 2, KC, P])
        wd_raw = put("wd_raw", [P, 2, D])
        e12_raw = put("e12_raw", [P, 2, 2 * KC, P])
        e3_raw = put("e3_raw", [P, 2, D])
        b3 = put("b3", [E + 1, D])
        gu_at = at[0]
        gu_hi = put("gu_hi", [P, 2, 2, KC, P], F32R)
        gu_lo = put("gu_lo", [P, 2, 2, KC, P], F32R)
        xt_hi = put("xt_hi", [P, KC, NB * P], F32R)
        xt_lo = put("xt_lo", [P, KC, NB * P], F32R)
        iq_at = at[0]
        iq = put("iq", [P, CH, NB * P], F32R)
        wd_hi = put("wd_hi", [P, CH, D], F32R)
        wd_lo = put("wd_lo", [P, CH, D], F32R)
        silu_gate = put("silu_gate", [P, 2, D])
        tr_v = put("tr_v", [P, 2 * D])
        tr_abs = put("tr_abs", [P, 2 * D])
        tr_sign = put("tr_sign", [P, 2 * D])
        tr_int = put("tr_int", [P, 2 * D])

        at[0] = gu_at
        ctx_rows = put("ctx_rows", [P, 2, D])
        ctx_cols = put("ctx_cols", [P, 2, KC, P])
        q3 = put("q3", [P, KC, P])
        sim = put("sim", [P, P])
        moe_rows = put("moe_rows", [P, 2, D])
        sim_max, sim_bias = put("sim_max", [P, 1]), put("sim_bias", [P, 1])
        sim_sum, sim_inv = put("sim_sum", [P, 1]), put("sim_inv", [P, 1])

        at[0] = iq_at
        e12_hi = put("e12_hi", [P, 2, 2 * KC, P], F32R)
        e12_lo = put("e12_lo", [P, 2, 2 * KC, P], F32R)
        e3_hi = put("e3_hi", [P, 2, D], F32R)
        e3_lo = put("e3_lo", [P, 2, D], F32R)
        e_silu = put("e_silu", [P, 2, D])
        e_h = put("e_h", [P, 2, D])
        h_hi = put("h_hi", [P, 2, D], F32R)
        h_lo = put("h_lo", [P, 2, D], F32R)
        r_score, r_masked, r_work, r_rest, r_first, r_both = (
            put(n, [P, NB, E]) for n in ("r_score", "r_masked", "r_work", "r_rest", "r_first", "r_both"))
        r_gmax, r_gwork, r_grest, r_gfirst, r_keep, r_low = (
            put(n, [P, NB, EG]) for n in ("r_gmax", "r_gwork", "r_grest", "r_gfirst", "r_keep", "r_low"))
        r_stat = put("r_stat", [P, 2, NB])
        tri = put("tri", [P, E, E])
        order = put("order", [P, E])
        logits_t = put("logits_t", [E, 2, 4 * P])
        gates_t_hi, gates_t_lo = (put(n, [E + 1, NB * P], F32R) for n in ("gates_t_hi", "gates_t_lo"))
        b3_hi, b3_lo = put("b3_hi", [E + 1, D], F32R), put("b3_lo", [E + 1, D], F32R)

        bank = [top.enter_context(nc.psum_tensor(f"bank{i}", [P, 512], F32)) for i in range(8)]
        ln_rows = [first_rows, moe_rows]
        scores_ps = bank[0:2]
        pt_ps = bank[2:4]
        o_ps = bank[4]
        y_ps = bank[5]
        proj_a, proj_b = bank[6], bank[7]

        x_loaded = [sem(f"x_loaded{i}") for i in range(PAIRS)]
        small_loaded = sem("small_loaded")
        consts_ready = sem("consts_ready")
        head_w_ready = sem("head_w_ready")
        gates_ready = sem("gates_ready")
        ctx_loaded = [sem(f"ctx_loaded{i}") for i in range(PAIRS)]
        ctx_hi_ready = sem("ctx_hi_ready")
        ctx_lo_ready = sem("ctx_lo_ready")
        ln_stat = [sem(f"ln_stat{i}") for i in range(2)]
        ln_rstd_ready = [sem(f"ln_rstd_ready{i}") for i in range(2)]
        ln_row_ready = [sem(f"ln_row_ready{i}") for i in range(2)]
        ln_transposed = [sem(f"ln_transposed{i}") for i in range(2)]
        ln_hi_ready = [sem(f"ln_hi_ready{i}") for i in range(2)]
        ln_lo_ready = [sem(f"ln_lo_ready{i}") for i in range(2)]
        wq_loaded, wkv_loaded, wo_loaded = sem("wq_loaded"), sem("wkv_loaded"), sem("wo_loaded")
        wq_hi_ready, wq_lo_ready = sem("wq_hi_ready"), sem("wq_lo_ready")
        wo_hi_ready, wo_lo_ready = sem("wo_hi_ready"), sem("wo_lo_ready")
        wkv_hi_ready, wkv_lo_ready = sem("wkv_hi_ready"), sem("wkv_lo_ready")
        kv_done, k_turned, q_done, q_turned = sem("kv_done"), sem("k_turned"), sem("q_done"), sem("q_turned")
        k_copied, v_hi_ready, v_lo_ready = sem("k_copied"), sem("v_hi_ready"), sem("v_lo_ready")
        k_ss_ready, k_rstd_ready, k_scaled = sem("k_ss_ready"), sem("k_rstd_ready"), sem("k_scaled")
        k_var_ready = sem("k_var_ready")
        k_hi_ready, k_lo_ready = sem("k_hi_ready"), sem("k_lo_ready")
        q_hi_ready, q_lo_ready, q_copied = sem("q_hi_ready"), sem("q_lo_ready"), sem("q_copied")
        q_ss_ready = sem("q_ss_ready")
        q_var_ready, q_rstd_ready = sem("q_var_ready"), sem("q_rstd_ready")
        scores_done, max_ready, bias_ready = sem("scores_done"), sem("max_ready"), sem("bias_ready")
        exp_done, inv_ready, probs_ready = sem("exp_done"), sem("inv_ready"), sem("probs_ready")
        p_turned, pt_hi_ready, pt_lo_ready = sem("p_turned"), sem("pt_hi_ready"), sem("pt_lo_ready")
        o_done, o_hi_ready, o_lo_ready = sem("o_done"), sem("o_hi_ready"), sem("o_lo_ready")
        y_done, y_added = sem("y_done"), sem("y_added")
        stored = sem("stored")
        gu_loaded = [sem(f"gu_loaded{i}") for i in range(2)]
        wd_loaded = [sem(f"wd_loaded{i}") for i in range(2)]
        ctx3_rows_loaded = [sem(f"ctx3_rows_loaded{i}") for i in range(2)]
        ctx3_cols_loaded = [sem(f"ctx3_cols_loaded{i}") for i in range(2)]
        e12_loaded = [sem(f"e12_loaded{i}") for i in range(2)]
        e3_loaded = [sem(f"e3_loaded{i}") for i in range(2)]
        gu_hi_ready = sem("gu_hi_ready")
        gu_lo_ready = sem("gu_lo_ready")
        wd_hi_ready = sem("wd_hi_ready")
        wd_lo_ready = sem("wd_lo_ready")
        gu_done = sem("gu_done")
        inter_step = sem("inter_step")
        iq_ready = sem("iq_ready")
        sign_ready = sem("sign_ready")
        down_done = sem("down_done")
        x2_ready = sem("x2_ready")
        q3_ready = sem("q3_ready")
        sim_done = sem("sim_done")
        sim_max_ready = sem("sim_max_ready")
        sim_bias_ready = sem("sim_bias_ready")
        sim_exp = sem("sim_exp")
        sim_inv_ready = sem("sim_inv_ready")
        sim_ready = sem("sim_ready")
        context_done = sem("context_done")
        x3_ready = sem("x3_ready")
        router_done = sem("router_done")
        logits_ready = sem("logits_ready")
        router_w_hi = sem("router_w_hi")
        router_w_ready = sem("router_w_ready")
        router_step = sem("router_step")
        router_exp = sem("router_exp")
        router_gates_ready = sem("router_gates_ready")
        shared_gate_ready = sem("shared_gate_ready")
        e_hi_ready = sem("e_hi_ready")
        b_now_ready = sem("b_now_ready")
        e_lo_ready = sem("e_lo_ready")
        h_done = sem("h_done")
        silu_ready = sem("silu_ready")
        h_ready = sem("h_ready")
        h_hi_ready = sem("h_hi_ready")
        h_lo_ready = sem("h_lo_ready")
        e_done = sem("e_done")
        e_added = sem("e_added")
        gates_turned = sem("gates_turned")
        gates_high = sem("gates_high")
        gates_low = sem("gates_low")
        b3_high = sem("b3_high")
        b3_low = sem("b3_low")
        logits_copied = sem("logits_copied")
        logits_turned = sem("logits_turned")
        bias_done = sem("bias_done")
        bias_added = sem("bias_added")
        router_loaded = sem("router_loaded")
        tri_ready = sem("tri_ready")
        silu_gate_ready = [sem(f"silu_gate_ready{i}") for i in range(2)]
        inter_ready = [sem(f"inter_ready{i}") for i in range(2)]

        def three(eng, out_ap, a_hi, a_lo, b_hi, b_lo, start, stop):
            eng.matmul(out_ap, a_lo, b_hi, start=start, stop=False)
            eng.matmul(out_ap, a_hi, b_lo, start=False, stop=False)
            return eng.matmul(out_ap, a_hi, b_hi, start=False, stop=stop)

        def after_start(g, b, back):
            return not (isinstance(g, int) and g * NB + b - back < 0)

        def before_end(g, b, ahead):
            return not (isinstance(g, int) and g * NB + b + ahead >= G * NB)

        def after_first(e):
            return not (isinstance(e, int) and e == 0)

        def groups(eng, one_group):
            one_group(0)
            with eng.Fori(1, G - 1) as g:
                one_group(g)
            one_group(G - 1)

        def chunks(eng, one_chunk):
            for j in range(2):
                one_chunk(j, j, P, P)
            with eng.Fori(1, (CH - 3) // 2) as i:
                for j in range(2):
                    one_chunk(i * 2 + j, j, P, P)
            one_chunk(CH - 3, 0, P, P)
            one_chunk(CH - 2, 1, P, TAIL)
            one_chunk(CH - 1, 0, TAIL, 0)

        block = top.enter_context(nc.Block())

        @block.sync
        def _(sp):
            sp.dma_start(head_w[:, 0:1], q_w).then_inc(small_loaded, 16)
            sp.dma_start(head_w[:, 1:2], k_w).then_inc(small_loaded, 16)
            sp.dma_start(gate_rows[:, 0:2], g_xattn.broadcast_to([P, 2])).then_inc(small_loaded, 16)
            sp.dma_start(gate_rows[:, 2:4], g_ffn.broadcast_to([P, 2])).then_inc(small_loaded, 16)
            for p in range(PAIRS):
                sp.dma_start(x_sb[:, 2 * p:2 * p + 2, :], x[2 * p:2 * p + 2, :, :].rearrange("b t d -> t b d"))\
                  .then_inc(x_loaded[p], 16)
                sp.dma_start(ctx_raw[:, :, 256 * p:256 * p + 256], ctx_t[:, :, 256 * p:256 * p + 256])\
                  .then_inc(ctx_loaded[p], 16)

            def load_group(g):
                first = isinstance(g, int)
                if not first:
                    sp.wait_ge(wkv_lo_ready, g)
                sp.dma_start(wkv_raw[:, :, :], wkv[bass.ds(g, 1), :, :, :].rearrange("a p c n -> p (a c) n"))\
                  .then_inc(wkv_loaded, 16)
                if not first:
                    sp.wait_ge(wq_lo_ready, g * R)
                sp.dma_start(wq_raw[:, :, :], wq[bass.ds(g, 1), :, :, :].rearrange("a p c n -> p (a c) n"))\
                  .then_inc(wq_loaded, 16)
                if not first:
                    sp.wait_ge(wo_lo_ready, g * R)
                sp.dma_start(wo_raw[:, :, :], wo[bass.ds(g, 1), :, :, :].rearrange("a p c n -> p (a c) n"))\
                  .then_inc(wo_loaded, 16)

            load_group(0)
            with sp.Fori(1, G) as g:
                load_group(g)

            def load_chunk(c, j, width):
                if width == P:
                    cols = bass.ds(c * P, P)
                else:
                    cols = slice(INTER - width, INTER)
                for i, w in enumerate((w_gate, w_up)):
                    sp.dma_start(gu_raw[:, j, i, :, 0:width], w[:, :, cols]).then_inc(gu_loaded[j], 16)
                rows = bass.ds(c * P, P) if width == P else slice(INTER - width, INTER)
                sp.dma_start(wd_raw[0:width, j, :], w_down[rows, :]).then_inc(wd_loaded[j], 16)

            def load_expert(e, j):
                sp.dma_start(e12_raw[:, j, :, :], e_w12[bass.ds(e, 1), :, :, :].rearrange("a p c n -> p (a c) n"))\
                  .then_inc(e12_loaded[j], 16)
                sp.dma_start(e3_raw[:, j, :], e_w3[bass.ds(e, 1), :, :].rearrange("a p n -> p (a n)"))\
                  .then_inc(e3_loaded[j], 16)

            sp.wait_ge(q_done, 2 * PAIRS * G)
            sp.wait_ge(kv_done, 2 * PAIRS * G)
            load_chunk(0, 0, P)
            load_chunk(1, 1, P)
            load_expert(0, 0)
            load_expert(1, 1)
            for dst, src in ((router_wr[:, :, :], router_w), (router_rows[:, 0, :], router_b.broadcast_to([P, E])),
                             (router_rows[:, 1, :], router_bias.broadcast_to([P, E])), (b12[:, :, :], e_b12),
                             (b3[:, :], e_b3)):
                sp.dma_start(dst, src).then_inc(router_loaded, 16)
            with sp.Fori(1, (CH - 1) // 2) as i:
                for j in range(2):
                    c = i * 2 + j
                    sp.wait_ge(gu_lo_ready, c - 1)
                    sp.wait_ge(wd_lo_ready, c - 1)
                    load_chunk(c, j, P)
            sp.wait_ge(gu_lo_ready, CH - 2)
            sp.wait_ge(wd_lo_ready, CH - 2)
            load_chunk(CH - 1, 0, TAIL)
            sp.wait_ge(gu_done, 4 * CH)
            for t in range(NB):
                if t >= 2:
                    sp.wait_ge(context_done, t - 1)
                sp.dma_start(ctx_rows[:, t % 2, :], ctx[t, :, :]).then_inc(ctx3_rows_loaded[t % 2], 16)
                sp.dma_start(ctx_cols[:, t % 2, :, :], ctx_t[:, :, t * P:t * P + P]).then_inc(ctx3_cols_loaded[t % 2], 16)
            with sp.Fori(1, EA // 2) as i:
                for j in range(2):
                    sp.wait_ge(e_lo_ready, (i * 2 + j - 1) * 2)
                    load_expert(i * 2 + j, j)
            for t in range(NB):
                sp.wait_ge(e_added, 8 * (EA - 1) + t + 1)
                sp.dma_start(out[t, :, :], x_sb[:, t, :]).then_inc(stored, 16)
            sp.wait_ge(stored, 16 * NB)

        @block.gpsimd
        def _(pool):
            pool.memset(ident[:, :], 0.0).then_inc(consts_ready, 1)
            pool.memset(minus_half[:, :], -0.5).then_inc(consts_ready, 1)
            pool.wait_ge(consts_ready, 2)
            pool.affine_select(out=ident[:, :], in_=ident[:, :], compare_op=ALU.not_equal, fill=1.0, base=0,
                               pattern=[[-1, P]], channel_multiplier=1).then_inc(consts_ready, 1)

            def ln_root(i, s=0):
                pool.wait_ge(ln_stat[s], 3 * i + 3)
                pool.tensor_tensor(ln_rstd[s][:, i % 2, :], ln_var[s][:, i % 2, :], minus_half[:, 0:1], ALU.pow)\
                    .then_inc(ln_rstd_ready[s], 1)

            def wkv_low(g):
                pool.wait_ge(wkv_hi_ready, g + 1)
                pool.tensor_tensor(wkv_lo[:, :, :], wkv_raw[:, :, :], wkv_hi[:, :, :].bitcast(F32),
                                   ALU.subtract).then_inc(wkv_lo_ready, 1)

            def wq_low(g):
                for h in range(R):
                    cols = slice(h * HD, h * HD + HD)
                    pool.wait_ge(wq_hi_ready, g * R + h + 1)
                    pool.tensor_tensor(wq_lo[:, :, cols], wq_raw[:, :, cols], wq_hi[:, :, cols].bitcast(F32),
                                       ALU.subtract).then_inc(wq_lo_ready, 1)

            def wo_low(g):
                for h in range(R):
                    pool.wait_ge(wo_hi_ready, g * R + h + 1)
                    pool.tensor_tensor(wo_lo[:, h, :], wo_raw[:, h, :], wo_hi[:, h, :].bitcast(F32),
                                       ALU.subtract).then_inc(wo_lo_ready, 1)

            def k_root(pair):
                pool.wait_ge(k_var_ready, pair + 1)
                pool.tensor_tensor(k_rstd[:, :], k_var[:, :], minus_half[:, 0:4], ALU.pow).then_inc(k_rstd_ready, 1)

            def q_root(pair, par):
                pool.wait_ge(q_var_ready, pair + 1)
                pool.tensor_tensor(q_rstd[:, par, :], q_var[:, :], minus_half[:, 0:2 * R], ALU.pow)\
                    .then_inc(q_rstd_ready, 1)

            for t in range(NB):
                ln_root(t)
            wkv_low(0)
            wq_low(0)
            k_root(0)
            q_root(0, 0)

            def one_group(g):
                for b in range(0, NB, 2):
                    next_pair = g * PAIRS + (b // 2 + 1)
                    if b == 2:
                        wo_low(g)
                    if b == 6 and before_end(g, b, 2):
                        wq_low(g + 1)
                    if before_end(g, b, 2):
                        k_root(next_pair)
                    if b == 4 and before_end(g, b, 4):
                        wkv_low(g + 1)
                    if before_end(g, b, 2):
                        q_root(next_pair, (b // 2 + 1) % 2)

            groups(pool, one_group)

            def halves_low(c, j, width):
                pool.wait_ge(wd_hi_ready, c + 1)
                pool.wait_ge(gu_hi_ready, c + 1)
                pool.tensor_tensor(gu_lo[:, j, :, :, 0:width].rearrange("p a c n -> p (a c) n"),
                                   gu_raw[:, j, :, :, 0:width].rearrange("p a c n -> p (a c) n"),
                                   gu_hi[:, j, :, :, 0:width].bitcast(F32).rearrange("p a c n -> p (a c) n"),
                                   ALU.subtract).then_inc(gu_lo_ready, 1)
                dst = bass.ds(c, 1)
                pool.tensor_tensor(wd_lo[0:width, dst, :].rearrange("p a n -> p (a n)"), wd_raw[0:width, j, :],
                                   wd_hi[0:width, dst, :].rearrange("p a n -> p (a n)").bitcast(F32),
                                   ALU.subtract).then_inc(wd_lo_ready, 1)

            halves_low(0, 0, P)
            for t in range(NB):
                ln_root(NB + t)
            chunks(pool, lambda c, j, width, following: following and halves_low(c + 1, 1 - j, following))

            pool.wait_ge(router_w_hi, 1)
            pool.tensor_tensor(router_wl[:, :, :], router_wr[:, :, :], router_wh[:, :, :].bitcast(F32),
                               ALU.subtract).then_inc(router_w_ready, 1)

            def expert_low(e, j):
                pool.wait_ge(e_hi_ready, e * 2 + 2)
                pool.tensor_tensor(e12_lo[:, j, :, :], e12_raw[:, j, :, :], e12_hi[:, j, :, :].bitcast(F32),
                                   ALU.subtract).then_inc(e_lo_ready, 1)
                pool.tensor_tensor(e3_lo[:, j, :], e3_raw[:, j, :], e3_hi[:, j, :].bitcast(F32),
                                   ALU.subtract).then_inc(e_lo_ready, 1)

            for s in range(NB + 2):
                if 0 <= s - 2 < NB:
                    ln_root(s - 2, 1)
                if s < NB:
                    ln_root(2 * NB + s)
                if s == NB - 1:
                    expert_low(0, 0)

            pool.wait_ge(down_done, NB)
            pool.memset(tri[:, :, :], 1.0).then_inc(tri_ready, 1)
            pool.wait_ge(tri_ready, 1)
            pool.affine_select(out=tri[:, :, :], in_=tri[:, :, :], compare_op=ALU.is_gt, fill=0.0, base=0,
                               pattern=[[1, E], [-1, E]], channel_multiplier=0).then_inc(tri_ready, 1)
            pool.wait_ge(b3_high, 1)
            pool.tensor_tensor(b3_lo[:, :], b3[:, :], b3_hi[:, :].bitcast(F32), ALU.subtract).then_inc(b3_low, 1)
            expert_low(1, 1)
            with pool.Fori(1, EA // 2) as i:
                for j in range(2):
                    expert_low(i * 2 + j, j)

        @block.scalar
        def _(act):
            act.wait_ge(small_loaded, 64)
            act.activation(gate_rows[:, :], gate_rows[:, :], ACT.Tanh).then_inc(gates_ready, 1)

            def ln_high(i, dst, s=0):
                act.wait_ge(ln_transposed[s], i + 1)
                act.activation(dst, bank[2 * s + i % 2][:, :].rearrange("p (c n) -> p c n", c=KC), ACT.Copy)\
                   .then_inc(ln_hi_ready[s], 1)

            def wkv_high(g):
                act.wait_ge(wkv_loaded, g * 16 + 16)
                act.wait_ge(kv_done, g * (2 * PAIRS))
                act.activation(wkv_hi[:, :, :], wkv_raw[:, :, :], ACT.Copy).then_inc(wkv_hi_ready, 1)

            def wq_high(g):
                act.wait_ge(wq_loaded, g * 16 + 16)
                act.wait_ge(q_done, g * (2 * PAIRS))
                for h in range(R):
                    cols = slice(h * HD, h * HD + HD)
                    act.activation(wq_hi[:, :, cols], wq_raw[:, :, cols], ACT.Copy).then_inc(wq_hi_ready, 1)

            def wo_high(g):
                act.wait_ge(wo_loaded, g * 16 + 16)
                act.wait_ge(y_done, g * NB)
                for h in range(R):
                    act.activation(wo_hi[:, h, :], wo_raw[:, h, :], ACT.Copy).then_inc(wo_hi_ready, 1)

            def kv_high(pair, half, par):
                act.wait_ge(kv_done, pair * 2 + (half + 1))
                ps = (proj_a, proj_b)[half][:, :].rearrange("p (t n) -> p t n", t=2)
                act.activation(k_rows[:, 2 * half:2 * half + 2, :], ps[:, :, 0:HD], ACT.Copy).then_inc(k_copied, 1)
                act.activation(v_hi[:, par, 2 * half:2 * half + 2, :], ps[:, :, HD:2 * HD], ACT.Copy)\
                   .then_inc(v_hi_ready, 1)

            def k_high(pair, par):
                act.wait_ge(k_turned, pair + 1)
                act.activation(k_hi[:, par, :], proj_b[:, :], ACT.Copy, scale=head_w[:, 2:3]).then_inc(k_hi_ready, 1)

            def q_copy(pair):
                for i in range(2):
                    act.wait_ge(q_done, pair * 2 + (i + 1))
                    act.activation(q_rows[:, i, :], (proj_a, proj_b)[i][:, :], ACT.Copy).then_inc(q_copied, 1)

            def q_high(pair, par):
                for half in range(2):
                    act.wait_ge(q_turned, pair * 2 + (half + 1))
                    act.activation(q_hi[:, par, 2 * half:2 * half + 2, :].rearrange("p h n -> p (h n)"),
                                   (proj_a, proj_b)[half][:, :], ACT.Copy).then_inc(q_hi_ready, 1)

            def pt_high(n):
                for c in range(2):
                    act.wait_ge(p_turned, 2 * n + (c + 1))
                    act.activation(pt_hi[:, c, :], pt_ps[c][:, :], ACT.Copy).then_inc(pt_hi_ready, 1)

            def o_high(n, par):
                act.wait_ge(o_done, n + 1)
                act.activation(o_hi[:, par, :], o_ps[:, :], ACT.Copy).then_inc(o_hi_ready, 1)

            def exps(n, b):
                act.wait_ge(bias_ready, n + 1)
                act.wait_ge(p_turned, 2 * n)
                for h in range(R):
                    i = (b % 2) * R + h
                    act.activation(probs[:, h, :], scores_ps[h // 2][:, (h % 2) * 256:(h % 2) * 256 + 256], ACT.Exp,
                                   bias=exp_bias[:, h:h + 1], scale=q_rstd[:, (b // 2) % 2, i:i + 1],
                                   accum_out=row_sum[:, h:h + 1]).then_inc(exp_done, 1)

            for p in range(PAIRS):
                for t in (2 * p, 2 * p + 1):
                    ln_high(t, kv_src_hi[:, 1, :, t * P:(t + 1) * P])
                act.wait_ge(ctx_loaded[p], 16)
                act.activation(kv_src_hi[:, 0, :, 256 * p:256 * p + 256], ctx_raw[:, :, 256 * p:256 * p + 256],
                               ACT.Copy).then_inc(ctx_hi_ready, 1)
            wkv_high(0)
            wq_high(0)
            kv_high(0, 0, 0)
            kv_high(0, 1, 0)
            act.wait_ge(head_w_ready, 1)
            k_high(0, 0)
            q_copy(0)
            q_high(0, 0)

            def one_group(g):
                for b in range(NB):
                    n = g * NB + b
                    next_pair, par = g * PAIRS + (b // 2 + 1), (b // 2 + 1) % 2
                    prev = after_start(g, b, 1)
                    if prev:
                        pt_high(n - 1)
                    if b == 2:
                        wo_high(g)
                    if b == 6 and before_end(g, b, 2):
                        wq_high(g + 1)
                    if b % 2 == 1 and before_end(g, b, 1):
                        k_high(next_pair, par)
                    exps(n, b)
                    if prev:
                        o_high(n - 1, (b - 1) % 2)
                    if b == 5 and before_end(g, b, 3):
                        wkv_high(g + 1)
                    if b % 2 == 0 and before_end(g, b, 2):
                        for half in range(2):
                            kv_high(next_pair, half, par)
                    if b % 2 == 1 and before_end(g, b, 1):
                        q_copy(next_pair)
                        q_high(next_pair, par)

            groups(act, one_group)
            pt_high(G * NB - 1)
            o_high(G * NB - 1, 1)

            def halves_high(c, j, width):
                if not (isinstance(c, int) and c < 2):
                    act.wait_ge(gu_done, c * 4 - 4)
                act.wait_ge(gu_loaded[j], (c - j) * 16 + 32)
                act.wait_ge(wd_loaded[j], (c - j) * 8 + 16)
                act.activation(gu_hi[:, j, :, :, 0:width].rearrange("p a c n -> p (a c) n"),
                               gu_raw[:, j, :, :, 0:width].rearrange("p a c n -> p (a c) n"), ACT.Copy)\
                   .then_inc(gu_hi_ready, 1)
                act.activation(wd_hi[0:width, bass.ds(c, 1), :].rearrange("p a n -> p (a n)"), wd_raw[0:width, j, :],
                               ACT.Copy).then_inc(wd_hi_ready, 1)

            def magnitude_and_sign(c, width):
                act.wait_ge(inter_step, c * 4 + 1)
                act.activation(tr_abs[0:width, :], tr_v[0:width, :], ACT.Abs).then_inc(sign_ready, 1)
                act.activation(tr_sign[0:width, :], tr_v[0:width, :], ACT.Sign, scale=-1.0).then_inc(sign_ready, 1)

            def inner_chunk(c, j, width, following):
                if following:
                    halves_high(c + 1, 1 - j, following)
                for half in range(2):
                    act.wait_ge(gu_done, c * 4 + (2 * half + 1))
                    act.activation(silu_gate[0:width, half, :], bank[2 * half][0:width, :], ACT.Silu,
                                   scale=1.0 / 128.0).then_inc(silu_gate_ready[half], 1)
                magnitude_and_sign(c, width)

            act.wait_ge(y_added, G * NB)
            halves_high(0, 0, P)
            for t in range(NB):
                ln_high(NB + t, xt_hi[:, :, t * P:t * P + P])
            chunks(act, inner_chunk)

            def expert_high(e, j):
                act.wait_ge(e12_loaded[j], (e - j) * 8 + 16)
                act.wait_ge(e3_loaded[j], (e - j) * 8 + 16)
                act.activation(e12_hi[:, j, :, :], e12_raw[:, j, :, :], ACT.Copy).then_inc(e_hi_ready, 1)
                act.activation(e3_hi[:, j, :], e3_raw[:, j, :], ACT.Copy).then_inc(e_hi_ready, 1)
                act.activation(b_now[:, j, :], b12[:, bass.ds(e, 1), :].rearrange("p a n -> p (a n)"), ACT.Copy)\
                   .then_inc(b_now_ready, 1)

            def expert_half(e, j, half):
                if half == 1 and not (isinstance(e, int) and e == EA - 1):
                    if after_first(e):
                        act.wait_ge(e_done, e * 8)
                    expert_high(e + 1, 1 - j)
                act.wait_ge(h_done, e * 4 + (2 * half + 1))
                act.wait_ge(b_now_ready, e + 1)
                act.activation(e_silu[:, half, :], bank[2 * half][:, :], ACT.Silu, bias=b_now[:, j, 0:1])\
                   .then_inc(silu_ready, 1)
                act.wait_ge(h_ready, e * 2 + (half + 1))
                act.activation(h_hi[:, half, :], e_h[:, half, :], ACT.Copy).then_inc(h_hi_ready, 1)

            def expert_act(e, j):
                expert_half(e, j, 0)
                expert_half(e, j, 1)

            act.wait_ge(router_loaded, 16 * 5)
            act.activation(router_wh[:, :, :], router_wr[:, :, :], ACT.Copy).then_inc(router_w_hi, 1)

            def down_magnitude(t):
                cols = slice(t % 2 * D, t % 2 * D + D)
                act.wait_ge(down_done, t + 1)
                if t >= 1:
                    act.wait_ge(iq_ready, CH + t - 1)
                act.activation(tr_abs[:, cols], bank[4 + t % 2][:, :], ACT.Abs, scale=128.0).then_inc(sign_ready, 1)
                act.activation(tr_sign[:, cols], bank[4 + t % 2][:, :], ACT.Sign, scale=-1.0).then_inc(sign_ready, 1)

            def copy_logits(half):
                act.wait_ge(router_done, half + 1)
                act.activation(logits_t[:, half, :], bank[4 + half][0:E, :], ACT.Copy).then_inc(logits_copied, 1)

            down_magnitude(0)
            for s in range(NB + 2):
                if 0 <= s - 1 < NB:
                    ln_high(2 * NB + s - 1, q3[:, :, :])
                    act.wait_ge(sim_bias_ready, s)
                    if s >= 2:
                        act.wait_ge(context_done, s - 1)
                    act.activation(sim[:, :], bank[6][:, 0:P], ACT.Exp, bias=sim_bias[:, :], scale=CTX_SCALE,
                                   accum_out=sim_sum[:, :]).then_inc(sim_exp, 1)
                if s + 1 < NB:
                    down_magnitude(s + 1)
                if s == NB:
                    copy_logits(0)
                if 0 <= s - 2 < NB:
                    t = s - 2
                    ln_high(t, xt_hi[:, :, t * P:t * P + P], 1)
                if s == NB - 1:
                    act.wait_ge(down_done, NB)
                    expert_high(0, 0)

            act.activation(b3_hi[:, :], b3[:, :], ACT.Copy).then_inc(b3_high, 1)
            copy_logits(1)
            expert_act(0, 0)
            act.wait_ge(router_step, 2)
            act.activation(r_score[:, :, :], r_score[:, :, :], ACT.Exp).then_inc(router_exp, 1)
            expert_act(1, 1)
            expert_half(2, 0, 0)
            for half in range(2):
                act.wait_ge(gates_turned, half + 1)
                act.activation(gates_t_hi[:, half * D:half * D + D], bank[4 + half][0:E + 1, :], ACT.Copy)\
                   .then_inc(gates_high, 1)
            expert_half(2, 0, 1)
            expert_act(3, 1)
            with act.Fori(2, EA // 2 - 1) as i:
                for j in range(2):
                    expert_act(i * 2 + j, j)
            for j in range(2):
                expert_act(EA - 2 + j, j)

        @block.vector
        def _(dve):
            dve.wait_ge(small_loaded, 64)
            dve.tensor_tensor(head_w[:, 2:3], head_w[:, 0:1], head_w[:, 1:2], ALU.mult).then_inc(head_w_ready, 1)

            def ln_stats_of(i, t, s=0):
                dve.bn_stats(ln_stats[s][:, i % 2, :], x_sb[:, t, :]).then_inc(ln_stat[s], 1)
                dve.wait_ge(ln_stat[s], 3 * i + 1)
                dve.bn_aggr(ln_mv[s][:, i % 2, :], ln_stats[s][:, i % 2, :]).then_inc(ln_stat[s], 1)
                dve.wait_ge(ln_stat[s], 3 * i + 2)
                dve.tensor_scalar(ln_var[s][:, i % 2, :], ln_mv[s][:, i % 2, 1:2], LN_EPS, None, ALU.add)\
                   .then_inc(ln_stat[s], 1)

            def ln_rows_of(i, t, s=0):
                dve.wait_ge(ln_rstd_ready[s], i + 1)
                if i >= 2:
                    dve.wait_ge(ln_transposed[s], i - 1)
                dve.tensor_scalar(ln_rows[s][:, i % 2, :], x_sb[:, t, :], ln_mv[s][:, i % 2, 0:1],
                                  ln_rstd[s][:, i % 2, :], ALU.subtract, ALU.mult).then_inc(ln_row_ready[s], 1)

            def ln_low(i, hi, lo, s=0):
                dve.wait_ge(ln_hi_ready[s], i + 1)
                dve.tensor_tensor(lo, bank[2 * s + i % 2][:, :].rearrange("p (c n) -> p c n", c=KC), hi.bitcast(F32),
                                  ALU.subtract).then_inc(ln_lo_ready[s], 1)

            def v_low(pair, half, par):
                dve.wait_ge(v_hi_ready, pair * 2 + (half + 1))
                ps = (proj_a, proj_b)[half][:, :].rearrange("p (t n) -> p t n", t=2)
                dve.tensor_tensor(v_lo[:, par, 2 * half:2 * half + 2, :], ps[:, :, HD:2 * HD],
                                  v_hi[:, par, 2 * half:2 * half + 2, :].bitcast(F32), ALU.subtract)\
                   .then_inc(v_lo_ready, 1)

            def k_norm(pair):
                dve.wait_ge(k_copied, pair * 2 + 2)
                if not (isinstance(pair, int) and pair == 0):
                    dve.wait_ge(q_ss_ready, pair * 8)
                for i in range(4):
                    dve.tensor_tensor_reduce(k_junk[:, i, :], k_rows[:, i, :], k_rows[:, i, :], 1.0 / HD, 0.0, ALU.mult,
                                             ALU.add, k_ss[:, i:i + 1]).then_inc(k_ss_ready, 1)
                dve.wait_ge(k_ss_ready, pair * 4 + 4)
                dve.tensor_scalar(k_var[:, :], k_ss[:, :], RMS_EPS, None, ALU.add).then_inc(k_var_ready, 1)

            def k_scale(pair):
                dve.wait_ge(k_rstd_ready, pair + 1)
                for i in range(4):
                    dve.tensor_scalar(k_rows[:, i, :], k_rows[:, i, :], k_rstd[:, i:i + 1], None, ALU.mult)\
                       .then_inc(k_scaled, 1)

            def k_low(pair, par):
                dve.wait_ge(k_hi_ready, pair + 1)
                dve.scalar_tensor_tensor(out=k_lo[:, par, :], in0=proj_b[:, :], scalar=head_w[:, 2:3],
                                         in1=k_hi[:, par, :].bitcast(F32), op0=ALU.mult, op1=ALU.subtract)\
                   .then_inc(k_lo_ready, 1)

            def q_norm(pair):
                for i in range(2):
                    dve.wait_ge(q_copied, pair * 2 + (i + 1))
                    if i == 0:
                        dve.wait_ge(k_ss_ready, pair * 4 + 4)
                    else:
                        dve.wait_ge(q_ss_ready, pair * 8 + 4)
                    for h in range(R):
                        row = q_rows[:, i, h * HD:h * HD + HD]
                        dve.tensor_tensor_reduce(k_junk[:, h, :], row, row, 1.0, 0.0, ALU.mult, ALU.add,
                                                 q_ss[:, i * R + h:i * R + h + 1]).then_inc(q_ss_ready, 1)
                dve.wait_ge(q_ss_ready, pair * 8 + 8)
                dve.tensor_scalar(q_var[:, :], q_ss[:, :], HD * RMS_EPS, None, ALU.add).then_inc(q_var_ready, 1)

            def q_low(pair, half, par):
                dve.wait_ge(q_hi_ready, pair * 2 + (half + 1))
                ps = (proj_a, proj_b)[half]
                two = slice(2 * half, 2 * half + 2)
                dve.tensor_tensor(q_lo[:, par, two, :].rearrange("p h n -> p (h n)"), ps[:, :],
                                  q_hi[:, par, two, :].rearrange("p h n -> p (h n)").bitcast(F32), ALU.subtract)\
                   .then_inc(q_lo_ready, 1)

            def maxima(n):
                for half in range(2):
                    dve.wait_ge(scores_done, 2 * n + (half + 1))
                    dve.tensor_reduce(row_max[:, 2 * half:2 * half + 2],
                                      scores_ps[half][:, :].rearrange("p (h n) -> p h n", h=2), AX.X, ALU.max)\
                       .then_inc(max_ready, 1)

            def bias_of(n, b):
                dve.wait_ge(max_ready, 2 * n + 2)
                i = (b % 2) * R
                dve.scalar_tensor_tensor(out=exp_bias[:, :], in0=row_max[:, :], scalar=-1.0, in1=q_rstd[:, (b // 2) % 2, i:i + R],
                                         op0=ALU.mult, op1=ALU.mult).then_inc(bias_ready, 1)

            def pt_low(n):
                for c in range(2):
                    dve.wait_ge(pt_hi_ready, 2 * n + (c + 1))
                    dve.tensor_tensor(pt_lo[:, c, :], pt_ps[c][:, :], pt_hi[:, c, :].bitcast(F32), ALU.subtract)\
                       .then_inc(pt_lo_ready, 1)

            def o_low(n, par):
                dve.wait_ge(o_hi_ready, n + 1)
                dve.tensor_tensor(o_lo[:, par, :], o_ps[:, :], o_hi[:, par, :].bitcast(F32), ALU.subtract)\
                   .then_inc(o_lo_ready, 1)

            def normalise(n):
                dve.wait_ge(exp_done, 4 * n + 4)
                dve.reciprocal(row_inv[:, :], row_sum[:, :]).then_inc(inv_ready, 1)
                dve.wait_ge(inv_ready, n + 1)
                for h in range(R):
                    dve.tensor_scalar(probs[:, h, :], probs[:, h, :], row_inv[:, h:h + 1], None, ALU.mult)\
                       .then_inc(probs_ready, 1)

            def add_y(n, b):
                dve.wait_ge(y_done, n + 1)
                dve.scalar_tensor_tensor(out=x_sb[:, b, :], in0=y_ps[:, :], scalar=gate_rows[:, 0:1],
                                         in1=x_sb[:, b, :], op0=ALU.mult, op1=ALU.add).then_inc(y_added, 1)

            for p in range(PAIRS):
                dve.wait_ge(x_loaded[p], 16)
                for t in (2 * p, 2 * p + 1):
                    ln_stats_of(t, t)
                for t in (2 * p, 2 * p + 1):
                    ln_rows_of(t, t)
                for t in (2 * p, 2 * p + 1):
                    tok = slice(t * P, (t + 1) * P)
                    ln_low(t, kv_src_hi[:, 1, :, tok], kv_src_lo[:, 1, :, tok])
                dve.wait_ge(ctx_hi_ready, p + 1)
                tok = slice(256 * p, 256 * p + 256)
                dve.tensor_tensor(kv_src_lo[:, 0, :, tok], ctx_raw[:, :, tok], kv_src_hi[:, 0, :, tok].bitcast(F32),
                                  ALU.subtract).then_inc(ctx_lo_ready, 1)
            dve.wait_ge(gates_ready, 1)
            v_low(0, 0, 0)
            v_low(0, 1, 0)
            k_norm(0)
            k_scale(0)
            k_low(0, 0)
            q_norm(0)
            q_low(0, 0, 0)
            q_low(0, 1, 0)

            def one_group(g):
                for b in range(NB):
                    n = g * NB + b
                    next_pair, par = g * PAIRS + (b // 2 + 1), (b // 2 + 1) % 2
                    if after_start(g, b, 3):
                        add_y(n - 3, (b - 3) % NB)
                    maxima(n)
                    if after_start(g, b, 1):
                        pt_low(n - 1)
                    if b % 2 == 1 and before_end(g, b, 1):
                        k_low(next_pair, par)
                    if b % 2 == 0:
                        dve.wait_ge(q_rstd_ready, g * PAIRS + (b // 2 + 1))
                    bias_of(n, b)
                    if after_start(g, b, 1):
                        o_low(n - 1, (b - 1) % 2)
                    normalise(n)
                    if b % 2 == 1 and before_end(g, b, 1):
                        q_norm(next_pair)
                    for half in range(2):
                        if b % 2 == 0 and before_end(g, b, 2):
                            v_low(next_pair, half, par)
                        if b % 2 == 1 and before_end(g, b, 1):
                            q_low(next_pair, half, par)
                    if b % 2 == 0 and before_end(g, b, 2):
                        k_norm(next_pair)
                        k_scale(next_pair)

            groups(dve, one_group)
            last = G * NB - 1
            add_y(last - 2, NB - 3)
            pt_low(last)
            o_low(last, 1)
            add_y(last - 1, NB - 2)
            add_y(last, NB - 1)

            for t in range(0, NB, 2):
                for u in (t, t + 1):
                    ln_stats_of(NB + u, u)
                for u in (t, t + 1):
                    ln_rows_of(NB + u, u)
                for u in (t, t + 1):
                    tok = slice(u * P, u * P + P)
                    ln_low(NB + u, xt_hi[:, :, tok], xt_lo[:, :, tok])

            def inner_chunk(c, j, width, following):
                if after_first(c):
                    dve.wait_ge(iq_ready, c)
                for half in range(2):
                    dve.wait_ge(silu_gate_ready[half], c + 1)
                    dve.wait_ge(gu_done, c * 4 + (2 * half + 2))
                    dve.tensor_tensor(tr_v[0:width, half * D:half * D + D], silu_gate[0:width, half, :],
                                      bank[2 * half + 1][0:width, :], ALU.mult).then_inc(inter_ready[half], 1)
                dve.wait_ge(inter_ready[1], c + 1)
                dve.wait_ge(inter_ready[0], c + 1)
                dve.tensor_scalar(tr_v[0:width, :], tr_v[0:width, :], 127.0, -128.0, ALU.min, ALU.max)\
                   .then_inc(inter_step, 1)
                dve.wait_ge(sign_ready, c * 2 + 2)
                dve.tensor_scalar(tr_int[0:width, :], tr_abs[0:width, :], ROUND, ROUND, ALU.add, ALU.subtract)\
                   .then_inc(inter_step, 1)
                dve.wait_ge(inter_step, c * 4 + 2)
                dve.tensor_tensor(tr_v[0:width, :], tr_int[0:width, :], tr_abs[0:width, :], ALU.subtract)\
                   .then_inc(inter_step, 1)
                dve.wait_ge(inter_step, c * 4 + 3)
                dve.scalar_tensor_tensor(out=tr_v[0:width, :], in0=tr_v[0:width, :], scalar=0.0,
                                         in1=tr_int[0:width, :], op0=ALU.is_gt, op1=ALU.subtract).then_inc(inter_step, 1)
                dve.wait_ge(inter_step, c * 4 + 4)
                dve.tensor_tensor(iq[0:width, bass.ds(c, 1), :].rearrange("p a n -> p (a n)"), tr_v[0:width, :],
                                  tr_sign[0:width, :], ALU.mult).then_inc(iq_ready, 1)

            chunks(dve, inner_chunk)

            def down_whole(t):
                k, cols = CH + t, slice(t % 2 * D, t % 2 * D + D)
                dve.wait_ge(iq_ready, k)
                dve.wait_ge(sign_ready, k * 2 + 1)
                dve.tensor_scalar(tr_int[:, cols], tr_abs[:, cols], ROUND, ROUND, ALU.add, ALU.subtract)\
                   .then_inc(inter_step, 1)
                dve.wait_ge(inter_step, k * 4 + 1)
                dve.tensor_tensor(tr_v[:, cols], tr_int[:, cols], tr_abs[:, cols], ALU.subtract).then_inc(inter_step, 1)
                dve.wait_ge(inter_step, k * 4 + 2)
                dve.scalar_tensor_tensor(out=tr_v[:, cols], in0=tr_v[:, cols], scalar=0.0, in1=tr_int[:, cols],
                                         op0=ALU.is_gt, op1=ALU.subtract).then_inc(inter_step, 1)
                dve.wait_ge(inter_step, k * 4 + 3)
                dve.wait_ge(sign_ready, k * 2 + 2)
                dve.tensor_tensor(tr_int[:, cols], tr_v[:, cols], tr_sign[:, cols], ALU.mult).then_inc(inter_step, 1)

            def down_add(t):
                k, cols = CH + t, slice(t % 2 * D, t % 2 * D + D)
                dve.wait_ge(inter_step, k * 4 + 4)
                dve.tensor_scalar(tr_int[:, cols], tr_int[:, cols], 127.0, -128.0, ALU.min, ALU.max)\
                   .then_inc(iq_ready, 1)
                dve.wait_ge(iq_ready, k + 1)
                dve.scalar_tensor_tensor(out=x_sb[:, t, :], in0=tr_int[:, cols], scalar=gate_rows[:, 2:3],
                                         in1=x_sb[:, t, :], op0=ALU.mult, op1=ALU.add).then_inc(x2_ready, 1)
                dve.wait_ge(x2_ready, t + 1)
                ln_stats_of(2 * NB + t, t)

            def sim_max_of(t):
                dve.wait_ge(sim_done, t + 1)
                dve.tensor_reduce(sim_max[:, :], bank[6][:, 0:P], AX.X, ALU.max).then_inc(sim_max_ready, 1)
                dve.wait_ge(sim_max_ready, t + 1)
                dve.tensor_scalar(sim_bias[:, :], sim_max[:, :], -CTX_SCALE, None, ALU.mult).then_inc(sim_bias_ready, 1)

            def sim_norm(t):
                dve.wait_ge(sim_exp, t + 1)
                dve.reciprocal(sim_inv[:, :], sim_sum[:, :]).then_inc(sim_inv_ready, 1)
                dve.wait_ge(sim_inv_ready, t + 1)
                dve.tensor_scalar(sim[:, :], sim[:, :], sim_inv[:, :], None, ALU.mult).then_inc(sim_ready, 1)

            def add_context(t):
                dve.wait_ge(context_done, t + 1)
                dve.scalar_tensor_tensor(out=x_sb[:, t, :], in0=bank[7][:, :], scalar=gate_rows[:, 1:2],
                                         in1=x_sb[:, t, :], op0=ALU.mult, op1=ALU.add).then_inc(x3_ready, 1)
                dve.wait_ge(x3_ready, t + 1)
                ln_stats_of(t, t, 1)

            def router_in_low(t):
                tok = slice(t * P, t * P + P)
                ln_low(t, xt_hi[:, :, tok], xt_lo[:, :, tok], 1)

            for s in range(NB + 2):
                if 0 <= s - 2 < NB:
                    add_context(s - 2)
                if 0 <= s - 3 < NB:
                    router_in_low(s - 3)
                if s < NB:
                    down_whole(s)
                if 0 <= s - 1 < NB:
                    sim_max_of(s - 1)
                if s < NB:
                    down_add(s)
                if 0 <= s - 1 < NB:
                    sim_norm(s - 1)
                if 0 <= s - 2 < NB:
                    ln_rows_of(s - 2, s - 2, 1)
                if s < NB:
                    ln_rows_of(2 * NB + s, s)
            router_in_low(NB - 1)

            steps = [0]

            def step(ins):
                steps[0] += 1
                ins.then_inc(router_step, 1)
                dve.wait_ge(router_step, steps[0])

            def spread(ap, n):
                return ap.unsqueeze(len(ap.shape)).broadcast_to(list(ap.shape) + [n])

            def by_group(t):
                return t[:, :, :].rearrange("p t (g e) -> p t g e", g=EG)

            def first_of_largest(values, n, work, chosen):
                step(dve.tensor_reduce(r_stat[:, 0, :], values, AX.X, ALU.max))
                step(dve.tensor_tensor(work, values, spread(r_stat[:, 0, :], n), ALU.is_equal))
                step(dve.tensor_tensor(work, work, order[:, 0:n].unsqueeze(1).broadcast_to([P, NB, n]), ALU.mult))
                step(dve.tensor_reduce(r_stat[:, 1, :], work, AX.X, ALU.max))
                step(dve.tensor_tensor(chosen, work, spread(r_stat[:, 1, :], n), ALU.is_equal))

            def two_largest(values, n, rest, work, first, both):
                first_of_largest(values, n, work, first)
                step(dve.scalar_tensor_tensor(out=rest, in0=first, scalar=LOW, in1=values, op0=ALU.mult, op1=ALU.add))
                first_of_largest(rest, n, work, both)
                step(dve.tensor_tensor(both, both, first, ALU.add))

            def take_logits(half):
                dve.wait_ge(logits_turned, half + 1)
                dve.tensor_tensor(logits[:, 4 * half:4 * half + 4, :],
                                  bank[4 + half][:, 0:4 * E].rearrange("p (t e) -> p t e", e=E),
                                  router_rows[:, 0, :].unsqueeze(1).broadcast_to([P, 4, E]), ALU.add)\
                   .then_inc(logits_ready, 1)

            def router_shift():
                dve.wait_ge(logits_ready, 2)
                dve.wait_ge(down_done, NB)
                step(dve.tensor_reduce(r_stat[:, 0, :], logits[:, :, :], AX.X, ALU.max))
                step(dve.tensor_tensor(r_score[:, :, :], logits[:, :, :], spread(r_stat[:, 0, :], E), ALU.subtract))

            def router_groups():
                dve.wait_ge(router_exp, 1)
                step(dve.tensor_reduce(r_stat[:, 0, :], r_score[:, :, :], AX.X, ALU.add))
                step(dve.reciprocal(r_stat[:, 1, :], r_stat[:, 0, :]))
                step(dve.tensor_tensor(r_score[:, :, :], r_score[:, :, :], spread(r_stat[:, 1, :], E), ALU.mult))
                step(dve.tensor_tensor(r_score[:, :, :], r_score[:, :, :],
                                       router_rows[:, 1, :].unsqueeze(1).broadcast_to([P, NB, E]), ALU.add))
                dve.wait_ge(tri_ready, 2)
                step(dve.tensor_reduce(order[:, :], tri[:, :, :], AX.X, ALU.add))
                step(dve.tensor_scalar(order[:, :], order[:, :], -1.0, float(E), ALU.mult, ALU.add))
                step(dve.tensor_reduce(r_gmax[:, :, :], by_group(r_score), AX.X, ALU.max))
                two_largest(r_gmax[:, :, :], EG, r_grest[:, :, :], r_gwork[:, :, :], r_gfirst[:, :, :], r_keep[:, :, :])

            def router_choice():
                step(dve.tensor_scalar(r_low[:, :, :], r_keep[:, :, :], -1.0, -LOW, ALU.add, ALU.mult))
                step(dve.tensor_tensor(by_group(r_masked), by_group(r_score), spread(r_keep[:, :, :], E // EG),
                                       ALU.mult))
                step(dve.tensor_tensor(by_group(r_masked), by_group(r_masked), spread(r_low[:, :, :], E // EG),
                                       ALU.add))
                two_largest(r_masked[:, :, :], E, r_rest[:, :, :], r_work[:, :, :], r_first[:, :, :], r_both[:, :, :])
                dve.scalar_tensor_tensor(out=gates[:, :, 2:EA], in0=r_score[:, :, :], scalar=gate_rows[:, 3:4],
                                         in1=r_both[:, :, :], op0=ALU.mult, op1=ALU.mult).then_inc(router_gates_ready, 1)

            def hidden(e, j, half):
                dve.wait_ge(silu_ready, e * 2 + (half + 1))
                dve.wait_ge(h_done, e * 4 + (2 * half + 2))
                dve.scalar_tensor_tensor(out=e_h[:, half, :], in0=bank[2 * half + 1][:, :],
                                         scalar=b_now[:, j, 1:2], in1=e_silu[:, half, :],
                                         op0=ALU.add, op1=ALU.mult).then_inc(h_ready, 1)
                dve.wait_ge(h_hi_ready, e * 2 + (half + 1))
                dve.tensor_tensor(h_lo[:, half, :], e_h[:, half, :], h_hi[:, half, :].bitcast(F32),
                                  ALU.subtract).then_inc(h_lo_ready, 1)

            def add_expert(e, half):
                for i in range(4):
                    t = 4 * half + i
                    dve.wait_ge(e_done, e * 8 + (t + 1))
                    dve.scalar_tensor_tensor(out=x_sb[:, t, :], in0=bank[4 + i][:, :],
                                             scalar=gates[:, t, bass.ds(e, 1)], in1=x_sb[:, t, :],
                                             op0=ALU.mult, op1=ALU.add).then_inc(e_added, 1)

            def expert_dve(e, j):
                hidden(e, j, 0)
                if after_first(e):
                    add_expert(e - 1, 1)
                hidden(e, j, 1)
                add_expert(e, 0)

            dve.tensor_scalar(gates[:, :, 0:2], minus_half[:, :].rearrange("p (t a) -> p t a", a=2), 0.0,
                              gate_rows[:, 3:4], ALU.mult, ALU.add).then_inc(shared_gate_ready, 1)
            take_logits(0)
            hidden(0, 0, 0)
            take_logits(1)
            hidden(0, 0, 1)
            router_shift()
            dve.wait_ge(shared_gate_ready, 1)
            add_expert(0, 0)
            router_groups()
            hidden(1, 1, 0)
            add_expert(0, 1)
            router_choice()
            hidden(1, 1, 1)
            add_expert(1, 0)
            add_expert(1, 1)
            hidden(2, 0, 0)
            for half in range(2):
                dve.wait_ge(gates_high, half + 1)
                cols = slice(half * D, half * D + D)
                dve.tensor_tensor(gates_t_lo[:, cols], bank[4 + half][0:E + 1, :], gates_t_hi[:, cols].bitcast(F32),
                                  ALU.subtract).then_inc(gates_low, 1)
            for t in range(NB):
                dve.wait_ge(bias_done, t + 1)
                dve.tensor_tensor(x_sb[:, t, :], bank[4 + t % 4][:, :], x_sb[:, t, :], ALU.add)\
                   .then_inc(bias_added, 1)
            hidden(2, 0, 1)
            dve.wait_ge(bias_added, NB)
            dve.wait_ge(router_gates_ready, 1)
            add_expert(2, 0)
            expert_dve(3, 1)
            with dve.Fori(2, EA // 2) as i:
                for j in range(2):
                    expert_dve(i * 2 + j, j)
            add_expert(EA - 1, 1)

        @block.tensor
        def _(pe):
            pe.wait_ge(consts_ready, 3)

            def turn_rows(i, s=0):
                pe.wait_ge(ln_row_ready[s], i + 1)
                for c in range(KC):
                    mm = pe.transpose(bank[2 * s + i % 2][:, c * P:c * P + P], ln_rows[s][:, i % 2, c * P:c * P + P],
                                      ident[:, :])
                mm.then_inc(ln_transposed[s], 1)

            def kv_tile(pair, p, i):
                half = i // 2
                tok = slice((2 * p + half) * P, (2 * p + half) * P + P)
                ps = (proj_a, proj_b)[half][:, (i % 2) * 256:(i % 2) * 256 + 256]
                for c in range(KC):
                    mm = three(pe, ps, kv_src_hi[:, i % 2, c, tok], kv_src_lo[:, i % 2, c, tok],
                               wkv_hi[:, c, :], wkv_lo[:, c, :], c == 0, c == KC - 1)
                if i % 2 == 1:
                    mm.then_inc(kv_done, 1)

            def q_tile(p, i):
                tok = slice((2 * p + i) * P, (2 * p + i) * P + P)
                for c in range(KC):
                    mm = three(pe, (proj_a, proj_b)[i][:, :], kv_src_hi[:, 1, c, tok], kv_src_lo[:, 1, c, tok],
                               wq_hi[:, c, :], wq_lo[:, c, :], c == 0, c == KC - 1)
                mm.then_inc(q_done, 1)

            def turn_q(pair):
                pe.wait_ge(q_copied, pair * 2 + 2)
                for half in range(2):
                    for h in range(2):
                        for i in range(2):
                            at_h = (2 * half + h) * HD
                            mm = pe.transpose((proj_a, proj_b)[half][:, h * 256 + i * P:h * 256 + i * P + P],
                                              q_rows[:, i, at_h:at_h + HD], ident[:, :])
                    mm.then_inc(q_turned, 1)

            def kv_half(g, p, half):
                pair = g * PAIRS + p
                if half == 0:
                    if p == 0:
                        pe.wait_ge(wkv_lo_ready, g + 1)
                    if after_start(g, 2 * p, 1):
                        pe.wait_ge(q_lo_ready, pair * 2 - 1)
                elif after_start(g, 2 * p, 1):
                    pe.wait_ge(q_lo_ready, pair * 2)
                kv_tile(pair, p, 2 * half)
                kv_tile(pair, p, 2 * half + 1)

            def q_half(g, p, half):
                pair = g * PAIRS + p
                if half == 0:
                    if p == 0:
                        pe.wait_ge(wq_lo_ready, g * R + R)
                    pe.wait_ge(v_lo_ready, pair * 2 + 1)
                    pe.wait_ge(k_copied, pair * 2 + 1)
                else:
                    pe.wait_ge(k_lo_ready, pair + 1)
                q_tile(p, half)

            def turn_k(pair):
                pe.wait_ge(k_scaled, pair * 4 + 4)
                pe.wait_ge(v_lo_ready, pair * 2 + 2)
                for i in range(4):
                    mm = pe.transpose(proj_b[:, i * P:i * P + P], k_rows[:, i, :], ident[:, :])
                mm.then_inc(k_turned, 1)

            def scores(g, b, half):
                n, pair, par = g * NB + b, g * PAIRS + b // 2, (b // 2) % 2
                pe.wait_ge(q_lo_ready, pair * 2 + (half + 1))
                pe.wait_ge(k_lo_ready, pair + 1)
                if after_start(g, b, 1):
                    pe.wait_ge(exp_done, n * 4 - 2 + 2 * half)
                i = b % 2
                for h in (2 * half, 2 * half + 1):
                    mm = three(pe, scores_ps[half][:, (h % 2) * 256:(h % 2) * 256 + 256],
                               q_hi[:, par, h, i * P:i * P + P], q_lo[:, par, h, i * P:i * P + P],
                               k_hi[:, par, i * 256:i * 256 + 256], k_lo[:, par, i * 256:i * 256 + 256], True, True)
                mm.then_inc(scores_done, 1)

            def turn_probs(n):
                pe.wait_ge(probs_ready, n * 4 + 4)
                for c in range(2):
                    for h in range(R):
                        mm = pe.transpose(pt_ps[c][:, h * P:h * P + P], probs[:, h, c * P:c * P + P], ident[:, :])
                    mm.then_inc(p_turned, 1)

            def weigh_values(g, b):
                n, pair = g * NB + b, g * PAIRS + b // 2
                par, i = (b // 2) % 2, b % 2
                pe.wait_ge(pt_lo_ready, n * 2 + 2)
                pe.wait_ge(v_lo_ready, pair * 2 + 2)
                if after_start(g, b, 1):
                    pe.wait_ge(o_lo_ready, n)
                for c in range(2):
                    mm = three(pe, o_ps[:, :], v_hi[:, par, 2 * i + c, :], v_lo[:, par, 2 * i + c, :],
                               pt_hi[:, c, :], pt_lo[:, c, :], c == 0, c == 1)
                mm.then_inc(o_done, 1)

            def project_out(g, b, heads=range(R)):
                n, par = g * NB + b, b % 2
                if heads[0] == 0:
                    pe.wait_ge(o_lo_ready, n + 1)
                    if after_start(g, b, 1):
                        pe.wait_ge(y_added, n)
                for h in heads:
                    if b == 0:
                        pe.wait_ge(wo_lo_ready, g * R + (h + 1))
                    mm = three(pe, y_ps[:, :], o_hi[:, par, h * P:h * P + P], o_lo[:, par, h * P:h * P + P],
                               wo_hi[:, h, :], wo_lo[:, h, :], h == 0, h == R - 1)
                if heads[-1] == R - 1:
                    mm.then_inc(y_done, 1)

            for t in range(NB):
                if t >= 2:
                    pe.wait_ge(ln_lo_ready[0], t - 1)
                turn_rows(t)
            pe.wait_ge(ctx_lo_ready, PAIRS)
            pe.wait_ge(ln_lo_ready[0], NB)
            kv_half(0, 0, 0)
            kv_half(0, 0, 1)
            turn_k(0)
            q_half(0, 0, 0)
            q_half(0, 0, 1)
            turn_q(0)

            def one_group(g):
                for b in range(NB):
                    n = g * NB + b
                    ng, np_ = (g, b // 2 + 1) if b < NB - 2 else (g + 1, 0)
                    if after_start(g, b, 1):
                        turn_probs(n - 1)
                    scores(g, b, 0)
                    scores(g, b, 1)
                    ahead = before_end(g, b - b % 2, 2)
                    if b % 2 == 1 and ahead:
                        turn_k(g * PAIRS + (b // 2 + 1))
                    if ahead:
                        (kv_half, q_half)[b % 2](ng, np_, 0)
                    if after_start(g, b, 1):
                        weigh_values(g, b - 1)
                    if ahead:
                        (kv_half, q_half)[b % 2](ng, np_, 1)
                    back = (g, b - 2) if b >= 2 else (g - 1, b + NB - 2)
                    if after_start(g, b, 2):
                        project_out(*back, range(0, 2))
                    if b % 2 == 1 and ahead:
                        turn_q(g * PAIRS + (b // 2 + 1))
                    if after_start(g, b, 2):
                        project_out(*back, range(2, R))

            groups(pe, one_group)
            turn_probs(G * NB - 1)
            weigh_values(G - 1, NB - 1)
            project_out(G - 1, NB - 2)
            project_out(G - 1, NB - 1)

            for t in range(NB):
                if t >= 2:
                    pe.wait_ge(ln_lo_ready[0], NB + t - 1)
                turn_rows(NB + t)
            pe.wait_ge(ln_lo_ready[0], 2 * NB)

            def inner_chunk(c, j, width, following):
                pe.wait_ge(gu_lo_ready, c + 1)
                for half in range(2):
                    if after_first(c):
                        pe.wait_ge(inter_ready[half], c)
                    tok = slice(half * D, half * D + D)
                    for i in range(2):
                        for k in range(KC):
                            mm = three(pe, bank[2 * half + i][0:width, :], gu_hi[:, j, i, k, 0:width],
                                       gu_lo[:, j, i, k, 0:width], xt_hi[:, k, tok], xt_lo[:, k, tok],
                                       k == 0, k == KC - 1)
                        mm.then_inc(gu_done, 1)

            chunks(pe, inner_chunk)

            def down(t, first, last):
                if t >= 2 and first == 0:
                    pe.wait_ge(sign_ready, 2 * (CH + t) - 2)
                tok = slice(t * P, t * P + P)
                for c in range(first, last):
                    rows = P if c < CH - 1 else TAIL
                    for w in (wd_lo, wd_hi):
                        mm = pe.matmul(bank[4 + t % 2][:, :], iq[0:rows, c, tok], w[0:rows, c, :],
                                       start=(c == 0 and w is wd_lo), stop=(c == CH - 1 and w is wd_hi))
                if last == CH:
                    mm.then_inc(down_done, 1)

            def similarity(t):
                pe.wait_ge(ln_hi_ready[0], 2 * NB + t + 1)
                pe.wait_ge(ctx3_cols_loaded[t % 2], 16 * (t // 2 + 1))
                if t >= 1:
                    pe.wait_ge(sim_exp, t)
                for c in range(KC):
                    mm = pe.matmul(bank[6][:, 0:P], q3[:, c, :], ctx_cols[:, t % 2, c, :], start=(c == 0),
                                   stop=(c == KC - 1))
                mm.then_inc(sim_done, 1)

            def context(t):
                pe.wait_ge(sim_ready, t + 1)
                pe.wait_ge(ctx3_rows_loaded[t % 2], 16 * (t // 2 + 1))
                if t >= 1:
                    pe.wait_ge(x3_ready, t)
                pe.matmul(bank[7][:, :], sim[:, :], ctx_rows[:, t % 2, :], start=True, stop=True)\
                  .then_inc(context_done, 1)

            def route(half):
                pe.wait_ge(ln_lo_ready[1], 4 * half + 4)
                pe.wait_ge(router_w_ready, 1)
                pe.wait_ge(sign_ready, 2 * (CH + NB))
                tok = slice(half * D, half * D + D)
                for c in range(KC):
                    mm = three(pe, bank[4 + half][0:E, :], router_wh[:, c, :], router_wl[:, c, :],
                               xt_hi[:, c, tok], xt_lo[:, c, tok], c == 0, c == KC - 1)
                mm.then_inc(router_done, 1)

            def turn_logits(half):
                pe.wait_ge(logits_copied, half + 1)
                for i in range(4):
                    mm = pe.transpose(bank[4 + half][:, i * E:i * E + E], logits_t[:, half, i * P:i * P + P],
                                      ident[0:E, 0:E])
                mm.then_inc(logits_turned, 1)

            def inner(e, j, half):
                if half == 0:
                    pe.wait_ge(e_lo_ready, e * 2 + 2)
                if after_first(e):
                    pe.wait_ge(h_ready, e * 2 + (half - 1))
                tok = slice(half * D, half * D + D)
                for i in range(2):
                    for k in range(KC):
                        mm = three(pe, bank[2 * half + i][:, :], e12_hi[:, j, i * KC + k, :], e12_lo[:, j, i * KC + k, :],
                                   xt_hi[:, k, tok], xt_lo[:, k, tok], k == 0, k == KC - 1)
                    mm.then_inc(h_done, 1)

            def outer(e, j, half):
                pe.wait_ge(h_lo_ready, e * 2 + (half + 1))
                for i in range(4):
                    if after_first(e) or half == 1:
                        pe.wait_ge(e_added, e * 8 + (4 * half + i - 3))
                    tok = slice(i * P, i * P + P)
                    three(pe, bank[4 + i][:, :], h_hi[:, half, tok], h_lo[:, half, tok], e3_hi[:, j, :], e3_lo[:, j, :],
                          True, True).then_inc(e_done, 1)

            def expert_pe(e, j):
                inner(e, j, 0)
                if after_first(e):
                    outer(e - 1, 1 - j, 1)
                inner(e, j, 1)
                outer(e, j, 0)

            pe.wait_ge(iq_ready, CH - 1)
            pe.wait_ge(wd_lo_ready, CH)
            down(0, 0, CH - 1)
            down(1, 0, CH - 1)
            pe.wait_ge(iq_ready, CH)
            down(0, CH - 1, CH)
            down(1, CH - 1, CH)
            for s in range(NB + 2):
                if 0 <= s - 1 < NB:
                    if s >= 3:
                        pe.wait_ge(ln_hi_ready[0], 2 * NB + s - 2)
                    turn_rows(2 * NB + s - 1)
                if 2 <= s + 1 < NB:
                    down(s + 1, 0, CH // 2)
                if 0 <= s - 1 < NB:
                    similarity(s - 1)
                if 2 <= s + 1 < NB:
                    down(s + 1, CH // 2, CH)
                if s == NB:
                    route(0)
                if 0 <= s - 1 < NB:
                    context(s - 1)
                if 0 <= s - 2 < NB:
                    if s - 2 >= 2:
                        pe.wait_ge(ln_lo_ready[1], s - 3)
                    turn_rows(s - 2, 1)
                if s == NB:
                    pe.wait_ge(ln_hi_ready[0], 3 * NB)
                    inner(0, 0, 0)
            turn_logits(0)
            route(1)
            pe.wait_ge(ln_lo_ready[1], NB)
            inner(0, 0, 1)
            turn_logits(1)
            pe.wait_ge(logits_ready, 2)
            pe.wait_ge(x3_ready, NB)
            outer(0, 0, 0)
            expert_pe(1, 1)
            outer(1, 1, 1)
            inner(2, 0, 0)
            pe.wait_ge(router_gates_ready, 1)
            pe.wait_ge(e_added, 14)
            for half in range(2):
                for i in range(4):
                    mm = pe.transpose(bank[4 + half][0:E + 1, i * P:i * P + P], gates[:, 4 * half + i, 1:EA], ident[:, :])
                mm.then_inc(gates_turned, 1)
            inner(2, 0, 1)
            pe.wait_ge(gates_low, 2)
            pe.wait_ge(b3_low, 1)
            pe.wait_ge(e_added, 16)
            for t in range(NB):
                if t >= 4:
                    pe.wait_ge(bias_added, t - 3)
                tok = slice(t * P, t * P + P)
                three(pe, bank[4 + t % 4][:, :], gates_t_hi[:, tok], gates_t_lo[:, tok], b3_hi[:, :], b3_lo[:, :],
                      True, True).then_inc(bias_done, 1)
            pe.wait_ge(bias_added, NB)
            outer(2, 0, 0)
            expert_pe(3, 1)
            with pe.Fori(2, EA // 2) as i:
                for j in range(2):
                    expert_pe(i * 2 + j, j)
            outer(EA - 1, 1, 1)


def kernel(**inputs):
    import numpy as np
    import concourse.bacc as bacc
    from concourse.bass_utils import run_bass_kernel_spmd

    nc = bacc.Bacc("TRN2", target_bir_lowering=False, num_devices=1)
    a = {k: np.asarray(v) for k, v in inputs.items()}
    wq = a["L0_xattn_Wq"].reshape(KC, P, G, R * HD).transpose(2, 1, 0, 3)
    wk = a["L0_xattn_Wk"].reshape(KC, P, G, HD).transpose(2, 1, 0, 3)
    wv = a["L0_xattn_Wv"].reshape(KC, P, G, HD).transpose(2, 1, 0, 3)

    def by_expert(shared, routed):
        s = a["L1_ffn_" + shared].reshape(KC, P, 2, P).transpose(2, 1, 0, 3)
        return np.concatenate([s, a["L1_ffn_" + routed].reshape(E, KC, P, P).transpose(0, 2, 1, 3)], axis=0)

    arrays = {
        "x": a["x"],
        "ctx_t": a["ctx_4096"].reshape(NB * P, KC, P).transpose(2, 1, 0),
        "g_xattn": a["g_xattn"].reshape(1, 2),
        "g_ffn": a["g_ffn"].reshape(1, 2),
        "wq": wq,
        "wkv": np.concatenate([wk, wv], axis=3),
        "wo": a["L0_xattn_Wo"].reshape(G, R, HD, D).transpose(0, 2, 1, 3),
        "q_w": a["L0_xattn_q_norm_w"].reshape(HD, 1),
        "k_w": a["L0_xattn_k_norm_w"].reshape(HD, 1),
        "ctx": a["ctx_4096"],
        "w_gate": a["L0_ffn_w_gate"].T.reshape(KC, P, INTER).transpose(1, 0, 2),
        "w_up": a["L0_ffn_w_up"].T.reshape(KC, P, INTER).transpose(1, 0, 2),
        "w_down": a["L0_ffn_w_down"].T,
        "router_w": a["L1_ffn_router_w"].reshape(KC, P, E).transpose(1, 0, 2),
        "router_b": a["L1_ffn_router_b"].reshape(1, E),
        "router_bias": a["L1_ffn_router_bias"].reshape(1, E),
        "e_w12": np.concatenate([by_expert("sw1", "ew1"), by_expert("sw2", "ew2")], axis=2),
        "e_w3": np.concatenate([a["L1_ffn_sw3"].reshape(2, P, D), a["L1_ffn_ew3"]], axis=0),
        "e_b12": np.stack([np.concatenate([a[f"L1_ffn_sb{i}"].reshape(2, P), a[f"L1_ffn_eb{i}"]], axis=0).T
                           for i in (1, 2)], axis=2),
        "e_b3": np.concatenate([a["L1_ffn_sb3"].reshape(1, D), a["L1_ffn_eb3"]], axis=0),
    }
    arrays = {k: np.ascontiguousarray(v) for k, v in arrays.items()}
    args = {k: nc.dram_tensor(k, v.shape, mybir.dt.from_np(v.dtype), kind="ExternalInput").ap()
            for k, v in arrays.items()}
    out = nc.dram_tensor("out", (NB, P, D), F32, kind="ExternalOutput").ap()
    build(nc, out=out, **args)
    r = run_bass_kernel_spmd(nc, [arrays], core_ids=[0])
    return r.results[0]["out"]
```

```python
from contextlib import ExitStack

import concourse.bass as bass
from concourse import mybir

F32 = mybir.dt.float32
F32R = mybir.dt.float32r
ALU = mybir.AluOpType
ACT = mybir.ActivationFunctionType
AX = mybir.AxisListType

P = 128
D = 512
KC = D // P
NB = 8
G = 8
R = 4
PAIRS = NB // 2
HD = 128
RMS_EPS = 1e-6
LN_EPS = 1e-5
INTER = 1376
CH = -(-INTER // P)
TAIL = INTER - (CH - 1) * P
INNER = 2 * CH
ROUND = 1.5 * 2.0 ** 23
E = 16
EG = 4
EA = E + 2
CTX_SCALE = float(P) ** -0.5
LOW = -3.0e38


def build(nc, x, ctx, ctx_t, g_xattn, g_ffn, wq, wkv, wo, q_w, k_w, w_gate, w_up, w_down, router_w, router_b,
          router_bias, e_w12, e_w3, e_b12, e_b3, out):
    with ExitStack() as top:
        def sb(name, shape, dt=F32):
            return top.enter_context(nc.sbuf_tensor(name, shape, dt))

        def sem(name):
            return top.enter_context(nc.semaphore(name))

        x_sb = sb("x_sb", [P, NB, D])
        ident = sb("ident", [P, P])
        minus_half = sb("minus_half", [P, 16])
        gate_rows = sb("gate_rows", [P, 4])
        head_w = sb("head_w", [P, 3])
        ln_stats = [sb(f"ln_stats{i}", [P, NB, 6]) for i in range(2)]
        ln_mv = [sb(f"ln_mv{i}", [P, NB, 2]) for i in range(2)]
        ln_var = [sb(f"ln_var{i}", [P, NB, 1]) for i in range(2)]
        ln_rstd = [sb(f"ln_rstd{i}", [P, NB, 1]) for i in range(2)]
        first_rows = sb("first_rows", [P, 2, D])

        router_wr = sb("router_wr", [P, KC, E])
        router_wh = sb("router_wh", [P, KC, E], F32R)
        router_wl = sb("router_wl", [P, KC, E], F32R)
        router_rows = sb("router_rows", [P, 2, E])
        b12 = sb("b12", [P, EA, 2])
        b_now = sb("b_now", [P, 2, 2])
        logits = sb("logits", [P, NB, E])
        gates = sb("gates", [P, NB, EA])
        start = nc.sbuf_base
        at = [start]

        def put(name, shape, dt=F32):
            size = 4
            for n in shape[1:]:
                size *= n
            t = nc.alloc_sbuf_tensor_at(name, shape, dt, offset=at[0])
            at[0] += -(-size // 32) * 32
            return t

        kv_src_hi = put("kv_src_hi", [P, 2, KC, NB * P], F32R)
        kv_src_lo = put("kv_src_lo", [P, 2, KC, NB * P], F32R)
        wq_raw = put("wq_raw", [P, KC, R * HD])
        wq_hi = put("wq_hi", [P, KC, R * HD], F32R)
        wq_lo = put("wq_lo", [P, KC, R * HD], F32R)
        wkv_raw = put("wkv_raw", [P, KC, 2 * HD])
        wkv_hi = put("wkv_hi", [P, KC, 2 * HD], F32R)
        wkv_lo = put("wkv_lo", [P, KC, 2 * HD], F32R)
        wo_raw = put("wo_raw", [P, R, D])
        wo_hi = put("wo_hi", [P, R, D], F32R)
        wo_lo = put("wo_lo", [P, R, D], F32R)
        q_hi = put("q_hi", [P, 2, R, 2 * P], F32R)
        q_lo = put("q_lo", [P, 2, R, 2 * P], F32R)
        k_hi = put("k_hi", [P, 2, 4 * P], F32R)
        k_lo = put("k_lo", [P, 2, 4 * P], F32R)
        v_hi = put("v_hi", [P, 2, 4, HD], F32R)
        v_lo = put("v_lo", [P, 2, 4, HD], F32R)
        q_rows = put("q_rows", [P, 2, R * HD])
        q_ss = put("q_ss", [P, 2 * R])
        k_rows = put("k_rows", [P, 4, HD])
        k_junk = put("k_junk", [P, 4, HD])
        k_ss, k_var, k_rstd = put("k_ss", [P, 4]), put("k_var", [P, 4]), put("k_rstd", [P, 4])
        q_var, q_rstd = put("q_var", [P, 2 * R]), put("q_rstd", [P, 2, 2 * R])
        row_max, exp_bias = put("row_max", [P, R]), put("exp_bias", [P, R])
        row_sum, row_inv = put("row_sum", [P, R]), put("row_inv", [P, R])
        probs = put("probs", [P, R, 2 * P])
        here = at[0]
        ctx_raw = put("ctx_raw", [P, KC, NB * P])
        at[0] = here
        pt_hi = put("pt_hi", [P, 2, R * P], F32R)
        pt_lo = put("pt_lo", [P, 2, R * P], F32R)
        o_hi = put("o_hi", [P, 2, R * P], F32R)
        o_lo = put("o_lo", [P, 2, R * P], F32R)

        at[0] = start
        gu_raw = put("gu_raw", [P, 2, 2, KC, P])
        wd_raw = put("wd_raw", [P, 2, D])
        e12_raw = put("e12_raw", [P, 2, 2 * KC, P])
        e3_raw = put("e3_raw", [P, 2, D])
        b3 = put("b3", [E + 1, D])
        gu_at = at[0]
        gu_hi = put("gu_hi", [P, 2, 2, KC, P], F32R)
        gu_lo = put("gu_lo", [P, 2, 2, KC, P], F32R)
        xt_hi = put("xt_hi", [P, KC, NB * P], F32R)
        xt_lo = put("xt_lo", [P, KC, NB * P], F32R)
        iq_at = at[0]
        iq = put("iq", [P, CH, NB * P], F32R)
        wd_hi = put("wd_hi", [P, CH, D], F32R)
        wd_lo = put("wd_lo", [P, CH, D], F32R)
        silu_gate = put("silu_gate", [P, 2, D])
        tr_v = put("tr_v", [P, 2 * D])
        tr_abs = put("tr_abs", [P, 2 * D])
        tr_sign = put("tr_sign", [P, 2 * D])
        tr_int = put("tr_int", [P, 2 * D])

        at[0] = gu_at
        ctx_rows = put("ctx_rows", [P, 2, D])
        ctx_cols = put("ctx_cols", [P, 2, KC, P])
        q3 = put("q3", [P, KC, P])
        sim = put("sim", [P, P])
        moe_rows = put("moe_rows", [P, 2, D])
        sim_max, sim_bias = put("sim_max", [P, 1]), put("sim_bias", [P, 1])
        sim_sum, sim_inv = put("sim_sum", [P, 1]), put("sim_inv", [P, 1])

        at[0] = iq_at
        e12_hi = put("e12_hi", [P, 2, 2 * KC, P], F32R)
        e12_lo = put("e12_lo", [P, 2, 2 * KC, P], F32R)
        e3_hi = put("e3_hi", [P, 2, D], F32R)
        e3_lo = put("e3_lo", [P, 2, D], F32R)
        e_silu = put("e_silu", [P, 2, D])
        e_h = put("e_h", [P, 2, D])
        h_hi = put("h_hi", [P, 2, D], F32R)
        h_lo = put("h_lo", [P, 2, D], F32R)
        r_score, r_masked, r_work, r_rest, r_first, r_both = (
            put(n, [P, NB, E]) for n in ("r_score", "r_masked", "r_work", "r_rest", "r_first", "r_both"))
        r_gmax, r_gwork, r_grest, r_gfirst, r_keep, r_low = (
            put(n, [P, NB, EG]) for n in ("r_gmax", "r_gwork", "r_grest", "r_gfirst", "r_keep", "r_low"))
        r_stat = put("r_stat", [P, 2, NB])
        tri = put("tri", [P, E, E])
        order = put("order", [P, E])
        logits_t = put("logits_t", [E, 2, 4 * P])
        gates_t_hi, gates_t_lo = (put(n, [E + 1, NB * P], F32R) for n in ("gates_t_hi", "gates_t_lo"))
        b3_hi, b3_lo = put("b3_hi", [E + 1, D], F32R), put("b3_lo", [E + 1, D], F32R)

        bank = [top.enter_context(nc.psum_tensor(f"bank{i}", [P, 512], F32)) for i in range(8)]
        ln_rows = [first_rows, moe_rows]
        scores_ps = bank[0:2]
        pt_ps = bank[2:4]
        o_ps = bank[4]
        y_ps = bank[5]
        proj_a, proj_b = bank[6], bank[7]
        route_bank = (bank[4], bank[0])

        x_loaded = [sem(f"x_loaded{i}") for i in range(PAIRS)]
        small_loaded = sem("small_loaded")
        consts_ready = sem("consts_ready")
        head_w_ready = sem("head_w_ready")
        gates_ready = sem("gates_ready")
        ctx_loaded = [sem(f"ctx_loaded{i}") for i in range(PAIRS)]
        ctx_hi_ready = sem("ctx_hi_ready")
        ctx_lo_ready = sem("ctx_lo_ready")
        ctx_first_lo_ready = sem("ctx_first_lo_ready")
        ln_stat = [sem(f"ln_stat{i}") for i in range(2)]
        ln_rstd_ready = [sem(f"ln_rstd_ready{i}") for i in range(2)]
        ln_row_ready = [sem(f"ln_row_ready{i}") for i in range(2)]
        ln_transposed = [sem(f"ln_transposed{i}") for i in range(2)]
        ln_hi_ready = [sem(f"ln_hi_ready{i}") for i in range(2)]
        ln_lo_ready = [sem(f"ln_lo_ready{i}") for i in range(2)]
        wq_loaded, wkv_loaded, wo_loaded = sem("wq_loaded"), sem("wkv_loaded"), sem("wo_loaded")
        wq_hi_ready, wq_lo_ready = sem("wq_hi_ready"), sem("wq_lo_ready")
        wo_hi_ready, wo_lo_ready = sem("wo_hi_ready"), sem("wo_lo_ready")
        wkv_hi_ready, wkv_lo_ready = sem("wkv_hi_ready"), sem("wkv_lo_ready")
        kv_done, k_turned, q_done, q_turned = sem("kv_done"), sem("k_turned"), sem("q_done"), sem("q_turned")
        k_copied, v_hi_ready, v_lo_ready = sem("k_copied"), sem("v_hi_ready"), sem("v_lo_ready")
        k_ss_ready, k_rstd_ready, k_scaled = sem("k_ss_ready"), sem("k_rstd_ready"), sem("k_scaled")
        k_var_ready = sem("k_var_ready")
        k_hi_ready, k_lo_ready = sem("k_hi_ready"), sem("k_lo_ready")
        q_hi_ready, q_lo_ready, q_copied = sem("q_hi_ready"), sem("q_lo_ready"), sem("q_copied")
        q_ss_ready = sem("q_ss_ready")
        q_var_ready, q_rstd_ready = sem("q_var_ready"), sem("q_rstd_ready")
        scores_done, max_ready, bias_ready = sem("scores_done"), sem("max_ready"), sem("bias_ready")
        exp_done, inv_ready, probs_ready = sem("exp_done"), sem("inv_ready"), sem("probs_ready")
        p_turned, pt_hi_ready, pt_lo_ready = sem("p_turned"), sem("pt_hi_ready"), sem("pt_lo_ready")
        o_done, o_hi_ready, o_lo_ready = sem("o_done"), sem("o_hi_ready"), sem("o_lo_ready")
        y_done, y_added = sem("y_done"), sem("y_added")
        stored = sem("stored")
        gu_loaded = [sem(f"gu_loaded{i}") for i in range(2)]
        wd_loaded = [sem(f"wd_loaded{i}") for i in range(2)]
        ctx3_rows_loaded = [sem(f"ctx3_rows_loaded{i}") for i in range(2)]
        ctx3_cols_loaded = [sem(f"ctx3_cols_loaded{i}") for i in range(2)]
        e12_loaded = [sem(f"e12_loaded{i}") for i in range(2)]
        e3_loaded = [sem(f"e3_loaded{i}") for i in range(2)]
        gu_hi_ready = sem("gu_hi_ready")
        gu_lo_ready = sem("gu_lo_ready")
        wd_hi_ready = sem("wd_hi_ready")
        wd_lo_ready = sem("wd_lo_ready")
        gu_done = sem("gu_done")
        inter_step = sem("inter_step")
        iq_ready = sem("iq_ready")
        sign_ready = sem("sign_ready")
        down_done = sem("down_done")
        x2_ready = sem("x2_ready")
        sim_done = sem("sim_done")
        sim_max_ready = sem("sim_max_ready")
        sim_bias_ready = sem("sim_bias_ready")
        sim_exp = sem("sim_exp")
        sim_inv_ready = sem("sim_inv_ready")
        sim_ready = sem("sim_ready")
        context_done = sem("context_done")
        x3_ready = sem("x3_ready")
        router_done = sem("router_done")
        logits_ready = sem("logits_ready")
        router_w_hi = sem("router_w_hi")
        router_w_ready = sem("router_w_ready")
        router_step = sem("router_step")
        router_exp = sem("router_exp")
        router_gates_ready = sem("router_gates_ready")
        shared_gate_ready = sem("shared_gate_ready")
        e_hi_ready = sem("e_hi_ready")
        b_now_ready = sem("b_now_ready")
        e_lo_ready = sem("e_lo_ready")
        h_done = sem("h_done")
        silu_ready = sem("silu_ready")
        h_ready = sem("h_ready")
        h_hi_ready = sem("h_hi_ready")
        h_lo_ready = sem("h_lo_ready")
        e_done = sem("e_done")
        e_added = sem("e_added")
        gates_turned = sem("gates_turned")
        gates_high = sem("gates_high")
        gates_low = sem("gates_low")
        b3_high = sem("b3_high")
        b3_low = sem("b3_low")
        logits_copied = sem("logits_copied")
        logits_turned = sem("logits_turned")
        bias_done = sem("bias_done")
        bias_added = sem("bias_added")
        router_loaded = sem("router_loaded")
        tri_ready = sem("tri_ready")
        silu_gate_ready = [sem(f"silu_gate_ready{i}") for i in range(2)]
        inter_ready = [sem(f"inter_ready{i}") for i in range(2)]

        def three(eng, out_ap, a_hi, a_lo, b_hi, b_lo, start, stop):
            eng.matmul(out_ap, a_lo, b_hi, start=start, stop=False)
            eng.matmul(out_ap, a_hi, b_lo, start=False, stop=False)
            return eng.matmul(out_ap, a_hi, b_hi, start=False, stop=stop)

        def ln_bank(s, i):
            if s == 0 and NB - 2 <= i < NB:
                return bank[2 + i % 2]
            return bank[6 + i % 2] if s == 0 and NB <= i < 2 * NB else bank[2 * s + i % 2]

        def last_group(g):
            return isinstance(g, int) and g == G - 1

        def after_start(g, b, back):
            return not (isinstance(g, int) and g * NB + b - back < 0)

        def before_end(g, b, ahead):
            return not (isinstance(g, int) and g * NB + b + ahead >= G * NB)

        def after_first(e):
            return not (isinstance(e, int) and e == 0)

        def groups(eng, one_group):
            one_group(0)
            with eng.Fori(1, G - 1) as g:
                one_group(g)
            one_group(G - 1)

        def chunks(eng, one_chunk):
            for j in range(2):
                one_chunk(j, j, P, P)
            with eng.Fori(1, (CH - 3) // 2) as i:
                for j in range(2):
                    one_chunk(i * 2 + j, j, P, P)
            one_chunk(CH - 3, 0, P, P)
            one_chunk(CH - 2, 1, P, TAIL)
            one_chunk(CH - 1, 0, TAIL, 0)

        block = top.enter_context(nc.Block())

        @block.sync
        def _(sp):
            def load_pair(p):
                sp.dma_start(x_sb[:, 2 * p:2 * p + 2, :], x[2 * p:2 * p + 2, :, :].rearrange("b t d -> t b d"))\
                  .then_inc(x_loaded[p], 16)
                sp.dma_start(ctx_raw[:, :, 256 * p:256 * p + 256], ctx_t[:, :, 256 * p:256 * p + 256])\
                  .then_inc(ctx_loaded[p], 16)

            def load_group(g):
                first = isinstance(g, int)
                if not first:
                    sp.wait_ge(wkv_lo_ready, g)
                sp.dma_start(wkv_raw[:, :, :], wkv[bass.ds(g, 1), :, :, :].rearrange("a p c n -> p (a c) n"))\
                  .then_inc(wkv_loaded, 16)
                if not first:
                    sp.wait_ge(wq_lo_ready, g * R)
                sp.dma_start(wq_raw[:, :, :], wq[bass.ds(g, 1), :, :, :].rearrange("a p c n -> p (a c) n"))\
                  .then_inc(wq_loaded, 16)
                if first:
                    load_pair(1)
                    sp.dma_start(head_w[:, 0:1], q_w).then_inc(small_loaded, 16)
                    sp.dma_start(head_w[:, 1:2], k_w).then_inc(small_loaded, 16)
                    sp.dma_start(gate_rows[:, 0:2], g_xattn.broadcast_to([P, 2])).then_inc(small_loaded, 16)
                    sp.dma_start(gate_rows[:, 2:4], g_ffn.broadcast_to([P, 2])).then_inc(small_loaded, 16)
                    load_pair(2)
                    load_pair(3)
                else:
                    sp.wait_ge(wo_lo_ready, g * R)
                sp.dma_start(wo_raw[:, :, :], wo[bass.ds(g, 1), :, :, :].rearrange("a p c n -> p (a c) n"))\
                  .then_inc(wo_loaded, 16)

            load_pair(0)
            load_group(0)
            with sp.Fori(1, G) as g:
                load_group(g)

            def load_chunk(c, j, width):
                if width == P:
                    cols = bass.ds(c * P, P)
                else:
                    cols = slice(INTER - width, INTER)
                for i, w in enumerate((w_gate, w_up)):
                    sp.dma_start(gu_raw[:, j, i, :, 0:width], w[:, :, cols]).then_inc(gu_loaded[j], 16)
                rows = bass.ds(c * P, P) if width == P else slice(INTER - width, INTER)
                sp.dma_start(wd_raw[0:width, j, :], w_down[rows, :]).then_inc(wd_loaded[j], 16)

            def load_expert(e, j):
                sp.dma_start(e12_raw[:, j, :, :], e_w12[bass.ds(e, 1), :, :, :].rearrange("a p c n -> p (a c) n"))\
                  .then_inc(e12_loaded[j], 16)
                sp.dma_start(e3_raw[:, j, :], e_w3[bass.ds(e, 1), :, :].rearrange("a p n -> p (a n)"))\
                  .then_inc(e3_loaded[j], 16)

            sp.wait_ge(q_done, 2 * PAIRS * G)
            sp.wait_ge(kv_done, 2 * PAIRS * G)
            load_chunk(0, 0, P)
            load_chunk(1, 1, P)
            load_expert(0, 0)
            load_expert(1, 1)
            for dst, src in ((router_wr[:, :, :], router_w), (router_rows[:, 0, :], router_b.broadcast_to([P, E])),
                             (router_rows[:, 1, :], router_bias.broadcast_to([P, E])), (b12[:, :, :], e_b12),
                             (b3[:, :], e_b3)):
                sp.dma_start(dst, src).then_inc(router_loaded, 16)
            with sp.Fori(1, (CH - 1) // 2) as i:
                for j in range(2):
                    c = i * 2 + j
                    sp.wait_ge(gu_lo_ready, c - 1)
                    sp.wait_ge(wd_lo_ready, c - 1)
                    load_chunk(c, j, P)
            sp.wait_ge(gu_lo_ready, CH - 2)
            sp.wait_ge(wd_lo_ready, CH - 2)
            load_chunk(CH - 1, 0, TAIL)
            sp.wait_ge(gu_done, 4 * CH)
            for t in range(NB):
                if t >= 2:
                    sp.wait_ge(context_done, t - 1)
                sp.dma_start(ctx_rows[:, t % 2, :], ctx[t, :, :]).then_inc(ctx3_rows_loaded[t % 2], 16)
                sp.dma_start(ctx_cols[:, t % 2, :, :], ctx_t[:, :, t * P:t * P + P]).then_inc(ctx3_cols_loaded[t % 2], 16)
            with sp.Fori(1, EA // 2) as i:
                for j in range(2):
                    sp.wait_ge(e_lo_ready, (i * 2 + j - 1) * 2)
                    load_expert(i * 2 + j, j)
            for t in range(NB):
                sp.wait_ge(e_added, 8 * (EA - 1) + t + 1)
                sp.dma_start(out[t, :, :], x_sb[:, t, :]).then_inc(stored, 16)
            sp.wait_ge(stored, 16 * NB)

        @block.gpsimd
        def _(pool):
            pool.memset(ident[:, :], 0.0).then_inc(consts_ready, 1)
            pool.memset(minus_half[:, :], -0.5).then_inc(consts_ready, 1)
            pool.wait_ge(consts_ready, 2)
            pool.affine_select(out=ident[:, :], in_=ident[:, :], compare_op=ALU.not_equal, fill=1.0, base=0,
                               pattern=[[-1, P]], channel_multiplier=1).then_inc(consts_ready, 1)

            def ln_root(i, s=0):
                pool.wait_ge(ln_stat[s], 3 * i + 3)
                pool.tensor_tensor(ln_rstd[s][:, i % NB, :], ln_var[s][:, i % NB, :], minus_half[:, 0:1], ALU.pow)\
                    .then_inc(ln_rstd_ready[s], 1)

            def wkv_low(g):
                pool.wait_ge(wkv_hi_ready, g + 1)
                pool.tensor_tensor(wkv_lo[:, :, :], wkv_raw[:, :, :], wkv_hi[:, :, :].bitcast(F32),
                                   ALU.subtract).then_inc(wkv_lo_ready, 1)

            def wq_low(g):
                for h in range(R):
                    cols = slice(h * HD, h * HD + HD)
                    pool.wait_ge(wq_hi_ready, g * R + h + 1)
                    pool.tensor_tensor(wq_lo[:, :, cols], wq_raw[:, :, cols], wq_hi[:, :, cols].bitcast(F32),
                                       ALU.subtract).then_inc(wq_lo_ready, 1)

            def wo_low(g):
                for h in range(R):
                    pool.wait_ge(wo_hi_ready, g * R + h + 1)
                    pool.tensor_tensor(wo_lo[:, h, :], wo_raw[:, h, :], wo_hi[:, h, :].bitcast(F32),
                                       ALU.subtract).then_inc(wo_lo_ready, 1)

            def k_root(pair):
                pool.wait_ge(k_var_ready, pair + 1)
                pool.tensor_tensor(k_rstd[:, :], k_var[:, :], minus_half[:, 0:4], ALU.pow).then_inc(k_rstd_ready, 1)

            def q_root(pair, par):
                pool.wait_ge(q_var_ready, pair + 1)
                pool.tensor_tensor(q_rstd[:, par, :], q_var[:, :], minus_half[:, 0:2 * R], ALU.pow)\
                    .then_inc(q_rstd_ready, 1)

            def ctx_low(p):
                pool.wait_ge(ctx_hi_ready, p + 1)
                tok = slice(256 * p, 256 * p + 256)
                pool.tensor_tensor(kv_src_lo[:, 0, :, tok], ctx_raw[:, :, tok], kv_src_hi[:, 0, :, tok].bitcast(F32),
                                   ALU.subtract).then_inc(ctx_lo_ready, 1)

            ln_root(0)
            ln_root(1)
            wkv_low(0)
            ln_root(2)
            ln_root(3)
            wq_low(0)
            ln_root(4)
            ln_root(5)
            k_root(0)
            ctx_low(1)
            ln_root(6)
            ln_root(7)
            q_root(0, 0)
            ctx_low(2)
            ctx_low(3)

            def one_group(g):
                for b in range(0, NB, 2):
                    next_pair = g * PAIRS + (b // 2 + 1)
                    if b == 2:
                        wo_low(g)
                    if b == 6 and before_end(g, b, 2):
                        wq_low(g + 1)
                    if before_end(g, b, 2):
                        k_root(next_pair)
                    if b == 4 and before_end(g, b, 4):
                        wkv_low(g + 1)
                    if before_end(g, b, 2):
                        q_root(next_pair, (b // 2 + 1) % 2)

            groups(pool, one_group)

            def gu_low(c, j, width):
                pool.wait_ge(gu_hi_ready, c + 1)
                pool.tensor_tensor(gu_lo[:, j, :, :, 0:width].rearrange("p a c n -> p (a c) n"),
                                   gu_raw[:, j, :, :, 0:width].rearrange("p a c n -> p (a c) n"),
                                   gu_hi[:, j, :, :, 0:width].bitcast(F32).rearrange("p a c n -> p (a c) n"),
                                   ALU.subtract).then_inc(gu_lo_ready, 1)

            def wd_low(c, j, width):
                pool.wait_ge(wd_hi_ready, c + 1)
                dst = bass.ds(c, 1)
                pool.tensor_tensor(wd_lo[0:width, dst, :].rearrange("p a n -> p (a n)"), wd_raw[0:width, j, :],
                                   wd_hi[0:width, dst, :].rearrange("p a n -> p (a n)").bitcast(F32),
                                   ALU.subtract).then_inc(wd_lo_ready, 1)

            def next_low(c, j, width, following):
                if following:
                    gu_low(c + 1, 1 - j, following)
                    wd_low(c + 1, 1 - j, following)

            for t in range(5):
                ln_root(NB + t)
            gu_low(0, 0, P)
            for t in range(5, NB):
                ln_root(NB + t)
            wd_low(0, 0, P)
            chunks(pool, next_low)

            pool.wait_ge(router_w_hi, 1)
            pool.tensor_tensor(router_wl[:, :, :], router_wr[:, :, :], router_wh[:, :, :].bitcast(F32),
                               ALU.subtract).then_inc(router_w_ready, 1)

            def inner_low(e, j):
                pool.wait_ge(e_hi_ready, e * 2 + 2)
                pool.tensor_tensor(e12_lo[:, j, :, :], e12_raw[:, j, :, :], e12_hi[:, j, :, :].bitcast(F32),
                                   ALU.subtract).then_inc(e_lo_ready, 1)

            def outer_low(e, j):
                pool.tensor_tensor(e3_lo[:, j, :], e3_raw[:, j, :], e3_hi[:, j, :].bitcast(F32),
                                   ALU.subtract).then_inc(e_lo_ready, 1)

            def expert_low(e, j):
                inner_low(e, j)
                outer_low(e, j)

            def down_sign(t):
                k, cols = INNER + t, slice(t % 2 * D, t % 2 * D + D)
                pool.wait_ge(inter_step, k * 4 + 3)
                pool.wait_ge(sign_ready, k * 2 + 2)
                pool.tensor_tensor(tr_int[:, cols], tr_v[:, cols], tr_sign[:, cols], ALU.mult).then_inc(inter_step, 1)

            for s in range(NB + 2):
                if s < NB:
                    down_sign(s)
                if 0 <= s - 2 < NB:
                    ln_root(s - 2, 1)
                if s == NB - 1:
                    inner_low(0, 0)
                if s < NB:
                    ln_root(2 * NB + s)
                if s == NB - 1:
                    outer_low(0, 0)

            pool.wait_ge(down_done, NB)
            pool.memset(tri[:, :, :], 1.0).then_inc(tri_ready, 1)
            pool.wait_ge(tri_ready, 1)
            pool.affine_select(out=tri[:, :, :], in_=tri[:, :, :], compare_op=ALU.is_gt, fill=0.0, base=0,
                               pattern=[[1, E], [-1, E]], channel_multiplier=0).then_inc(tri_ready, 1)
            pool.wait_ge(b3_high, 1)
            pool.tensor_tensor(b3_lo[:, :], b3[:, :], b3_hi[:, :].bitcast(F32), ALU.subtract).then_inc(b3_low, 1)
            expert_low(1, 1)
            with pool.Fori(1, EA // 2) as i:
                for j in range(2):
                    expert_low(i * 2 + j, j)

        @block.scalar
        def _(act):
            def ln_high(i, dst, s=0):
                act.wait_ge(ln_transposed[s], i + 1)
                act.activation(dst, ln_bank(s, i)[:, :].rearrange("p (c n) -> p c n", c=KC), ACT.Copy)\
                   .then_inc(ln_hi_ready[s], 1)

            def wkv_high(g):
                act.wait_ge(wkv_loaded, g * 16 + 16)
                act.wait_ge(kv_done, g * (2 * PAIRS))
                act.activation(wkv_hi[:, :, :], wkv_raw[:, :, :], ACT.Copy).then_inc(wkv_hi_ready, 1)

            def wq_high(g):
                act.wait_ge(wq_loaded, g * 16 + 16)
                act.wait_ge(q_done, g * (2 * PAIRS))
                for h in range(R):
                    cols = slice(h * HD, h * HD + HD)
                    act.activation(wq_hi[:, :, cols], wq_raw[:, :, cols], ACT.Copy).then_inc(wq_hi_ready, 1)

            def wo_high(g):
                act.wait_ge(wo_loaded, g * 16 + 16)
                act.wait_ge(y_done, g * NB)
                for h in range(R):
                    act.activation(wo_hi[:, h, :], wo_raw[:, h, :], ACT.Copy).then_inc(wo_hi_ready, 1)

            def kv_high(pair, half, par):
                act.wait_ge(kv_done, pair * 2 + (half + 1))
                ps = (proj_a, proj_b)[half][:, :].rearrange("p (t n) -> p t n", t=2)
                act.activation(k_rows[:, 2 * half:2 * half + 2, :], ps[:, :, 0:HD], ACT.Copy).then_inc(k_copied, 1)
                act.activation(v_hi[:, par, 2 * half:2 * half + 2, :], ps[:, :, HD:2 * HD], ACT.Copy)\
                   .then_inc(v_hi_ready, 1)

            def k_high(pair, par):
                act.wait_ge(k_turned, pair + 1)
                act.activation(k_hi[:, par, :], proj_b[:, :], ACT.Copy, scale=head_w[:, 2:3]).then_inc(k_hi_ready, 1)

            def q_copy(pair):
                for i in range(2):
                    act.wait_ge(q_done, pair * 2 + (i + 1))
                    act.activation(q_rows[:, i, :], (proj_a, proj_b)[i][:, :], ACT.Copy).then_inc(q_copied, 1)

            def q_high(pair, par):
                for half in range(2):
                    act.wait_ge(q_turned, pair * 2 + (half + 1))
                    act.activation(q_hi[:, par, 2 * half:2 * half + 2, :].rearrange("p h n -> p (h n)"),
                                   (proj_a, proj_b)[half][:, :], ACT.Copy).then_inc(q_hi_ready, 1)

            def pt_high(n):
                for c in range(2):
                    act.wait_ge(p_turned, 2 * n + (c + 1))
                    act.activation(pt_hi[:, c, :], pt_ps[c][:, :], ACT.Copy).then_inc(pt_hi_ready, 1)

            def o_high(n, par):
                act.wait_ge(o_done, n + 1)
                act.activation(o_hi[:, par, :], o_ps[:, :], ACT.Copy).then_inc(o_hi_ready, 1)

            def exps(n, b):
                act.wait_ge(bias_ready, n + 1)
                act.wait_ge(p_turned, 2 * n)
                for h in range(R):
                    i = (b % 2) * R + h
                    act.activation(probs[:, h, :], scores_ps[h // 2][:, (h % 2) * 256:(h % 2) * 256 + 256], ACT.Exp,
                                   bias=exp_bias[:, h:h + 1], scale=q_rstd[:, (b // 2) % 2, i:i + 1],
                                   accum_out=row_sum[:, h:h + 1]).then_inc(exp_done, 1)

            def key_source_high(t):
                ln_high(t, kv_src_hi[:, 1, :, t * P:(t + 1) * P])

            def ctx_high(p):
                act.wait_ge(ctx_loaded[p], 16)
                act.activation(kv_src_hi[:, 0, :, 256 * p:256 * p + 256], ctx_raw[:, :, 256 * p:256 * p + 256],
                               ACT.Copy).then_inc(ctx_hi_ready, 1)

            ctx_high(0)
            wkv_high(0)
            key_source_high(0)
            key_source_high(1)
            wq_high(0)
            ctx_high(1)
            kv_high(0, 0, 0)
            key_source_high(2)
            key_source_high(3)
            kv_high(0, 1, 0)
            act.wait_ge(small_loaded, 64)
            act.activation(gate_rows[:, :], gate_rows[:, :], ACT.Tanh).then_inc(gates_ready, 1)
            act.wait_ge(head_w_ready, 1)
            k_high(0, 0)
            ctx_high(2)
            key_source_high(4)
            key_source_high(5)
            q_copy(0)
            q_high(0, 0)
            key_source_high(6)
            key_source_high(7)
            ctx_high(3)

            def xt_high(t):
                ln_high(NB + t, xt_hi[:, :, t * P:t * P + P])

            def one_group(g):
                for b in range(NB):
                    n = g * NB + b
                    next_pair, par = g * PAIRS + (b // 2 + 1), (b // 2 + 1) % 2
                    prev = after_start(g, b, 1)
                    if isinstance(g, int) and g == 0 and b == 1:
                        act.wait_ge(ctx_lo_ready, PAIRS - 1)
                    if prev:
                        pt_high(n - 1)
                    if b == 2:
                        wo_high(g)
                    if b == 6 and before_end(g, b, 2):
                        wq_high(g + 1)
                    if b % 2 == 1 and before_end(g, b, 1):
                        k_high(next_pair, par)
                    exps(n, b)
                    if prev:
                        o_high(n - 1, (b - 1) % 2)
                    if b == 5 and before_end(g, b, 3):
                        wkv_high(g + 1)
                    if b % 2 == 0 and before_end(g, b, 2):
                        for half in range(2):
                            kv_high(next_pair, half, par)
                    if b % 2 == 1 and before_end(g, b, 1):
                        q_copy(next_pair)
                        q_high(next_pair, par)
                    if b >= 6 and last_group(g):
                        xt_high(2 * (b - 6))
                        xt_high(2 * (b - 6) + 1)
                    if b == 7 and last_group(g):
                        gu_high(0, 0, P)

            def gu_high(c, j, width):
                if not (isinstance(c, int) and c < 2):
                    act.wait_ge(gu_done, c * 4 - 4)
                act.wait_ge(gu_loaded[j], (c - j) * 16 + 32)
                act.activation(gu_hi[:, j, :, :, 0:width].rearrange("p a c n -> p (a c) n"),
                               gu_raw[:, j, :, :, 0:width].rearrange("p a c n -> p (a c) n"), ACT.Copy)\
                   .then_inc(gu_hi_ready, 1)

            def wd_high(c, j, width):
                act.wait_ge(wd_loaded[j], (c - j) * 8 + 16)
                act.activation(wd_hi[0:width, bass.ds(c, 1), :].rearrange("p a n -> p (a n)"), wd_raw[0:width, j, :],
                               ACT.Copy).then_inc(wd_hi_ready, 1)

            groups(act, one_group)
            pt_high(G * NB - 1)
            xt_high(4)
            o_high(G * NB - 1, 1)
            xt_high(5)

            def magnitude_and_sign(c, width, half):
                cols = slice(half * D, half * D + D)
                act.wait_ge(inter_step, c * 8 + (4 * half + 1))
                act.activation(tr_abs[0:width, cols], tr_v[0:width, cols], ACT.Abs).then_inc(sign_ready, 1)
                act.activation(tr_sign[0:width, cols], tr_v[0:width, cols], ACT.Sign, scale=-1.0)\
                   .then_inc(sign_ready, 1)

            def inner_chunk(c, j, width, following):
                if following:
                    gu_high(c + 1, 1 - j, following)
                    wd_high(c + 1, 1 - j, following)
                for half in range(2):
                    act.wait_ge(gu_done, c * 4 + (2 * half + 1))
                    act.activation(silu_gate[0:width, half, :], bank[2 * half][0:width, :], ACT.Silu,
                                   scale=1.0 / 128.0).then_inc(silu_gate_ready[half], 1)
                    magnitude_and_sign(c, width, half)

            xt_high(6)
            act.wait_ge(y_added, G * NB)
            wd_high(0, 0, P)
            xt_high(7)
            chunks(act, inner_chunk)

            def expert_high(e, j):
                act.wait_ge(e12_loaded[j], (e - j) * 8 + 16)
                act.wait_ge(e3_loaded[j], (e - j) * 8 + 16)
                act.activation(e12_hi[:, j, :, :], e12_raw[:, j, :, :], ACT.Copy).then_inc(e_hi_ready, 1)
                act.activation(e3_hi[:, j, :], e3_raw[:, j, :], ACT.Copy).then_inc(e_hi_ready, 1)
                act.activation(b_now[:, j, :], b12[:, bass.ds(e, 1), :].rearrange("p a n -> p (a n)"), ACT.Copy)\
                   .then_inc(b_now_ready, 1)

            def silu_of(e, j, half):
                act.wait_ge(h_done, e * 4 + (2 * half + 1))
                act.wait_ge(b_now_ready, e + 1)
                act.activation(e_silu[:, half, :], bank[2 * half][:, :], ACT.Silu, bias=b_now[:, j, 0:1])\
                   .then_inc(silu_ready, 1)

            def hidden_high(e, half):
                act.wait_ge(h_ready, e * 2 + (half + 1))
                act.activation(h_hi[:, half, :], e_h[:, half, :], ACT.Copy).then_inc(h_hi_ready, 1)

            def expert_half(e, j, half):
                if half == 1 and not (isinstance(e, int) and e == EA - 1):
                    if after_first(e):
                        act.wait_ge(e_done, e * 8)
                    expert_high(e + 1, 1 - j)
                silu_of(e, j, half)
                hidden_high(e, half)

            def expert_act(e, j):
                expert_half(e, j, 0)
                expert_half(e, j, 1)

            act.wait_ge(router_loaded, 16 * 5)
            act.activation(router_wh[:, :, :], router_wr[:, :, :], ACT.Copy).then_inc(router_w_hi, 1)

            def down_magnitude(t):
                cols = slice(t % 2 * D, t % 2 * D + D)
                act.wait_ge(down_done, t + 1)
                act.wait_ge(iq_ready, INNER + t - 1)
                act.activation(tr_abs[:, cols], bank[4 + t % 2][:, :], ACT.Abs, scale=128.0).then_inc(sign_ready, 1)
                act.activation(tr_sign[:, cols], bank[4 + t % 2][:, :], ACT.Sign, scale=-1.0).then_inc(sign_ready, 1)

            def copy_logits(half):
                act.wait_ge(router_done, half + 1)
                act.activation(logits_t[:, half, :], route_bank[half][0:E, :], ACT.Copy).then_inc(logits_copied, 1)

            down_magnitude(0)
            for s in range(NB + 2):
                if 0 <= s - 1 < NB:
                    ln_high(2 * NB + s - 1, q3[:, :, :])
                    act.wait_ge(sim_bias_ready, s)
                    if s >= 2:
                        act.wait_ge(context_done, s - 1)
                    act.activation(sim[:, :], bank[6][:, 0:P], ACT.Exp, bias=sim_bias[:, :], scale=CTX_SCALE,
                                   accum_out=sim_sum[:, :]).then_inc(sim_exp, 1)
                if s + 1 < NB:
                    down_magnitude(s + 1)
                if s == NB:
                    copy_logits(0)
                if s == NB + 1:
                    silu_of(0, 0, 0)
                if 0 <= s - 2 < NB:
                    t = s - 2
                    ln_high(t, xt_hi[:, :, t * P:t * P + P], 1)
                if s == NB - 2:
                    act.wait_ge(down_done, NB)
                    expert_high(0, 0)

            hidden_high(0, 0)
            act.activation(b3_hi[:, :], b3[:, :], ACT.Copy).then_inc(b3_high, 1)
            copy_logits(1)
            expert_half(0, 0, 1)
            act.wait_ge(router_step, 2)
            act.activation(r_score[:, :, :], r_score[:, :, :], ACT.Exp).then_inc(router_exp, 1)
            expert_act(1, 1)
            expert_half(2, 0, 0)
            for half in range(2):
                act.wait_ge(gates_turned, half + 1)
                act.activation(gates_t_hi[:, half * D:half * D + D], bank[4 + half][0:E + 1, :], ACT.Copy)\
                   .then_inc(gates_high, 1)
            expert_half(2, 0, 1)
            expert_act(3, 1)
            with act.Fori(2, EA // 2 - 1) as i:
                for j in range(2):
                    expert_act(i * 2 + j, j)
            for j in range(2):
                expert_act(EA - 2 + j, j)

        @block.vector
        def _(dve):
            def ln_stats_of(i, t, s=0):
                dve.bn_stats(ln_stats[s][:, i % NB, :], x_sb[:, t, :]).then_inc(ln_stat[s], 1)
                dve.wait_ge(ln_stat[s], 3 * i + 1)
                dve.bn_aggr(ln_mv[s][:, i % NB, :], ln_stats[s][:, i % NB, :]).then_inc(ln_stat[s], 1)
                dve.wait_ge(ln_stat[s], 3 * i + 2)
                dve.tensor_scalar(ln_var[s][:, i % NB, :], ln_mv[s][:, i % NB, 1:2], LN_EPS, None, ALU.add)\
                   .then_inc(ln_stat[s], 1)

            def ln_rows_of(i, t, s=0):
                dve.wait_ge(ln_rstd_ready[s], i + 1)
                if i >= 2:
                    dve.wait_ge(ln_transposed[s], i - 1)
                dve.tensor_scalar(ln_rows[s][:, i % 2, :], x_sb[:, t, :], ln_mv[s][:, i % NB, 0:1],
                                  ln_rstd[s][:, i % NB, :], ALU.subtract, ALU.mult).then_inc(ln_row_ready[s], 1)

            def ln_low(i, hi, lo, s=0):
                dve.wait_ge(ln_hi_ready[s], i + 1)
                dve.tensor_tensor(lo, ln_bank(s, i)[:, :].rearrange("p (c n) -> p c n", c=KC), hi.bitcast(F32),
                                  ALU.subtract).then_inc(ln_lo_ready[s], 1)

            def v_low(pair, half, par):
                dve.wait_ge(v_hi_ready, pair * 2 + (half + 1))
                ps = (proj_a, proj_b)[half][:, :].rearrange("p (t n) -> p t n", t=2)
                dve.tensor_tensor(v_lo[:, par, 2 * half:2 * half + 2, :], ps[:, :, HD:2 * HD],
                                  v_hi[:, par, 2 * half:2 * half + 2, :].bitcast(F32), ALU.subtract)\
                   .then_inc(v_lo_ready, 1)

            def k_norm(pair):
                dve.wait_ge(k_copied, pair * 2 + 2)
                if not (isinstance(pair, int) and pair == 0):
                    dve.wait_ge(q_ss_ready, pair * 8)
                for i in range(4):
                    dve.tensor_tensor_reduce(k_junk[:, i, :], k_rows[:, i, :], k_rows[:, i, :], 1.0 / HD, 0.0, ALU.mult,
                                             ALU.add, k_ss[:, i:i + 1]).then_inc(k_ss_ready, 1)
                dve.wait_ge(k_ss_ready, pair * 4 + 4)
                dve.tensor_scalar(k_var[:, :], k_ss[:, :], RMS_EPS, None, ALU.add).then_inc(k_var_ready, 1)

            def k_scale(pair):
                dve.wait_ge(k_rstd_ready, pair + 1)
                for i in range(4):
                    dve.tensor_scalar(k_rows[:, i, :], k_rows[:, i, :], k_rstd[:, i:i + 1], None, ALU.mult)\
                       .then_inc(k_scaled, 1)

            def k_low(pair, par):
                dve.wait_ge(k_hi_ready, pair + 1)
                dve.scalar_tensor_tensor(out=k_lo[:, par, :], in0=proj_b[:, :], scalar=head_w[:, 2:3],
                                         in1=k_hi[:, par, :].bitcast(F32), op0=ALU.mult, op1=ALU.subtract)\
                   .then_inc(k_lo_ready, 1)

            def q_norm(pair):
                for i in range(2):
                    dve.wait_ge(q_copied, pair * 2 + (i + 1))
                    if i == 0:
                        dve.wait_ge(k_ss_ready, pair * 4 + 4)
                    else:
                        dve.wait_ge(q_ss_ready, pair * 8 + 4)
                    for h in range(R):
                        row = q_rows[:, i, h * HD:h * HD + HD]
                        dve.tensor_tensor_reduce(k_junk[:, h, :], row, row, 1.0, 0.0, ALU.mult, ALU.add,
                                                 q_ss[:, i * R + h:i * R + h + 1]).then_inc(q_ss_ready, 1)
                dve.wait_ge(q_ss_ready, pair * 8 + 8)
                dve.tensor_scalar(q_var[:, :], q_ss[:, :], HD * RMS_EPS, None, ALU.add).then_inc(q_var_ready, 1)

            def q_low(pair, half, par):
                dve.wait_ge(q_hi_ready, pair * 2 + (half + 1))
                ps = (proj_a, proj_b)[half]
                two = slice(2 * half, 2 * half + 2)
                dve.tensor_tensor(q_lo[:, par, two, :].rearrange("p h n -> p (h n)"), ps[:, :],
                                  q_hi[:, par, two, :].rearrange("p h n -> p (h n)").bitcast(F32), ALU.subtract)\
                   .then_inc(q_lo_ready, 1)

            def maxima(n):
                for half in range(2):
                    dve.wait_ge(scores_done, 2 * n + (half + 1))
                    dve.tensor_reduce(row_max[:, 2 * half:2 * half + 2],
                                      scores_ps[half][:, :].rearrange("p (h n) -> p h n", h=2), AX.X, ALU.max)\
                       .then_inc(max_ready, 1)

            def bias_of(n, b):
                dve.wait_ge(max_ready, 2 * n + 2)
                i = (b % 2) * R
                dve.scalar_tensor_tensor(out=exp_bias[:, :], in0=row_max[:, :], scalar=-1.0, in1=q_rstd[:, (b // 2) % 2, i:i + R],
                                         op0=ALU.mult, op1=ALU.mult).then_inc(bias_ready, 1)

            def pt_low(n):
                for c in range(2):
                    dve.wait_ge(pt_hi_ready, 2 * n + (c + 1))
                    dve.tensor_tensor(pt_lo[:, c, :], pt_ps[c][:, :], pt_hi[:, c, :].bitcast(F32), ALU.subtract)\
                       .then_inc(pt_lo_ready, 1)

            def o_low(n, par):
                dve.wait_ge(o_hi_ready, n + 1)
                dve.tensor_tensor(o_lo[:, par, :], o_ps[:, :], o_hi[:, par, :].bitcast(F32), ALU.subtract)\
                   .then_inc(o_lo_ready, 1)

            def normalise(n):
                dve.wait_ge(exp_done, 4 * n + 4)
                dve.reciprocal(row_inv[:, :], row_sum[:, :]).then_inc(inv_ready, 1)
                dve.wait_ge(inv_ready, n + 1)
                for h in range(R):
                    dve.tensor_scalar(probs[:, h, :], probs[:, h, :], row_inv[:, h:h + 1], None, ALU.mult)\
                       .then_inc(probs_ready, 1)

            def add_y(n, b):
                dve.wait_ge(y_done, n + 1)
                dve.scalar_tensor_tensor(out=x_sb[:, b, :], in0=y_ps[:, :], scalar=gate_rows[:, 0:1],
                                         in1=x_sb[:, b, :], op0=ALU.mult, op1=ALU.add).then_inc(y_added, 1)

            def stats_pair(p):
                dve.wait_ge(x_loaded[p], 16)
                for t in (2 * p, 2 * p + 1):
                    ln_stats_of(t, t)

            def rows_pair(p):
                for t in (2 * p, 2 * p + 1):
                    ln_rows_of(t, t)

            def low_pair(p):
                for t in (2 * p, 2 * p + 1):
                    tok = slice(t * P, (t + 1) * P)
                    ln_low(t, kv_src_hi[:, 1, :, tok], kv_src_lo[:, 1, :, tok])

            stats_pair(0)
            rows_pair(0)
            dve.wait_ge(ctx_hi_ready, 1)
            dve.tensor_tensor(kv_src_lo[:, 0, :, 0:256], ctx_raw[:, :, 0:256], kv_src_hi[:, 0, :, 0:256].bitcast(F32),
                              ALU.subtract).then_inc(ctx_first_lo_ready, 1)
            low_pair(0)
            stats_pair(1)
            rows_pair(1)
            stats_pair(2)
            v_low(0, 0, 0)
            low_pair(1)
            v_low(0, 1, 0)
            k_norm(0)
            rows_pair(2)
            dve.wait_ge(small_loaded, 64)
            dve.tensor_tensor(head_w[:, 2:3], head_w[:, 0:1], head_w[:, 1:2], ALU.mult).then_inc(head_w_ready, 1)
            k_scale(0)
            k_low(0, 0)
            stats_pair(3)
            low_pair(2)
            rows_pair(3)
            q_norm(0)
            q_low(0, 0, 0)
            q_low(0, 1, 0)
            low_pair(3)
            dve.wait_ge(gates_ready, 1)

            def xt_low(t):
                ln_low(NB + t, xt_hi[:, :, t * P:t * P + P], xt_lo[:, :, t * P:t * P + P])

            def one_group(g):
                for b in range(NB):
                    n = g * NB + b
                    next_pair, par = g * PAIRS + (b // 2 + 1), (b // 2 + 1) % 2
                    if after_start(g, b, 3):
                        add_y(n - 3, (b - 3) % NB)
                    maxima(n)
                    if after_start(g, b, 1):
                        pt_low(n - 1)
                    if b % 2 == 1 and before_end(g, b, 1):
                        k_low(next_pair, par)
                    if b % 2 == 0:
                        dve.wait_ge(q_rstd_ready, g * PAIRS + (b // 2 + 1))
                    bias_of(n, b)
                    if after_start(g, b, 1):
                        o_low(n - 1, (b - 1) % 2)
                    normalise(n)
                    if b % 2 == 1 and before_end(g, b, 1):
                        q_norm(next_pair)
                    for half in range(2):
                        if b % 2 == 0 and before_end(g, b, 2):
                            v_low(next_pair, half, par)
                        if b % 2 == 1 and before_end(g, b, 1):
                            q_low(next_pair, half, par)
                    if b % 2 == 0 and before_end(g, b, 2):
                        k_norm(next_pair)
                        k_scale(next_pair)
                    if b >= 3 and last_group(g):
                        dve.wait_ge(y_added, n - 2)
                        ln_stats_of(NB + b - 3, b - 3)
                    if b == 5 and last_group(g):
                        ln_rows_of(NB, 0)
                        ln_rows_of(NB + 1, 1)
                    if b == 6 and last_group(g):
                        xt_low(0)
                        xt_low(1)
                        ln_rows_of(NB + 2, 2)
                        ln_rows_of(NB + 3, 3)
                    if b == 7 and last_group(g):
                        xt_low(2)
                        xt_low(3)
                        ln_rows_of(NB + 4, 4)

            groups(dve, one_group)
            last = G * NB - 1

            def add_last_y(t):
                add_y(last - (NB - 1) + t, t)
                dve.wait_ge(y_added, last + 1 - (NB - 1) + t)
                ln_stats_of(NB + t, t)

            add_last_y(5)
            pt_low(last)
            xt_low(4)
            ln_rows_of(NB + 5, 5)
            add_last_y(6)
            o_low(last, 1)
            xt_low(5)
            ln_rows_of(NB + 6, 6)
            add_last_y(7)
            xt_low(6)
            ln_rows_of(NB + 7, 7)
            xt_low(7)

            def inner_chunk(c, j, width, following):
                for half in range(2):
                    cols = slice(half * D, half * D + D)
                    if after_first(c) or half == 1:
                        dve.wait_ge(iq_ready, c * 2 + half)
                    dve.wait_ge(silu_gate_ready[half], c + 1)
                    dve.wait_ge(gu_done, c * 4 + (2 * half + 2))
                    dve.tensor_tensor(tr_v[0:width, cols], silu_gate[0:width, half, :],
                                      bank[2 * half + 1][0:width, :], ALU.mult).then_inc(inter_ready[half], 1)
                    dve.wait_ge(inter_ready[half], c + 1)
                    dve.tensor_scalar(tr_v[0:width, cols], tr_v[0:width, cols], 127.0, -128.0, ALU.min, ALU.max)\
                       .then_inc(inter_step, 1)
                    dve.wait_ge(sign_ready, c * 4 + (2 * half + 1))
                    dve.tensor_scalar(tr_int[0:width, cols], tr_abs[0:width, cols], ROUND, ROUND, ALU.add,
                                      ALU.subtract).then_inc(inter_step, 1)
                    dve.wait_ge(inter_step, c * 8 + (4 * half + 2))
                    dve.tensor_tensor(tr_abs[0:width, cols], tr_int[0:width, cols], tr_abs[0:width, cols], ALU.subtract)\
                       .then_inc(inter_step, 1)
                    dve.wait_ge(inter_step, c * 8 + (4 * half + 3))
                    dve.scalar_tensor_tensor(out=tr_int[0:width, cols], in0=tr_abs[0:width, cols], scalar=0.0,
                                             in1=tr_int[0:width, cols], op0=ALU.is_gt, op1=ALU.subtract)\
                       .then_inc(inter_step, 1)
                    dve.wait_ge(inter_step, c * 8 + (4 * half + 4))
                    dve.wait_ge(sign_ready, c * 4 + (2 * half + 2))
                    dve.tensor_tensor(iq[0:width, bass.ds(c, 1), cols].rearrange("p a n -> p (a n)"),
                                      tr_int[0:width, cols], tr_sign[0:width, cols], ALU.mult).then_inc(iq_ready, 1)

            chunks(dve, inner_chunk)

            def down_whole(t):
                k, cols = INNER + t, slice(t % 2 * D, t % 2 * D + D)
                dve.wait_ge(iq_ready, k)
                dve.wait_ge(sign_ready, k * 2 + 1)
                dve.tensor_scalar(tr_int[:, cols], tr_abs[:, cols], ROUND, ROUND, ALU.add, ALU.subtract)\
                   .then_inc(inter_step, 1)
                dve.wait_ge(inter_step, k * 4 + 1)
                dve.tensor_tensor(tr_v[:, cols], tr_int[:, cols], tr_abs[:, cols], ALU.subtract).then_inc(inter_step, 1)
                dve.wait_ge(inter_step, k * 4 + 2)
                dve.scalar_tensor_tensor(out=tr_v[:, cols], in0=tr_v[:, cols], scalar=0.0, in1=tr_int[:, cols],
                                         op0=ALU.is_gt, op1=ALU.subtract).then_inc(inter_step, 1)
            def down_add(t):
                k, cols = INNER + t, slice(t % 2 * D, t % 2 * D + D)
                dve.wait_ge(inter_step, k * 4 + 4)
                dve.tensor_scalar(tr_int[:, cols], tr_int[:, cols], 127.0, -128.0, ALU.min, ALU.max)\
                   .then_inc(iq_ready, 1)
                dve.wait_ge(iq_ready, k + 1)
                dve.scalar_tensor_tensor(out=x_sb[:, t, :], in0=tr_int[:, cols], scalar=gate_rows[:, 2:3],
                                         in1=x_sb[:, t, :], op0=ALU.mult, op1=ALU.add).then_inc(x2_ready, 1)
                dve.wait_ge(x2_ready, t + 1)
                ln_stats_of(2 * NB + t, t)

            def sim_max_of(t):
                dve.wait_ge(sim_done, t + 1)
                dve.tensor_reduce(sim_max[:, :], bank[6][:, 0:P], AX.X, ALU.max).then_inc(sim_max_ready, 1)
                dve.wait_ge(sim_max_ready, t + 1)
                dve.tensor_scalar(sim_bias[:, :], sim_max[:, :], -CTX_SCALE, None, ALU.mult).then_inc(sim_bias_ready, 1)

            def sim_norm(t):
                dve.wait_ge(sim_exp, t + 1)
                dve.reciprocal(sim_inv[:, :], sim_sum[:, :]).then_inc(sim_inv_ready, 1)
                dve.wait_ge(sim_inv_ready, t + 1)
                dve.tensor_scalar(sim[:, :], sim[:, :], sim_inv[:, :], None, ALU.mult).then_inc(sim_ready, 1)

            def add_context(t):
                dve.wait_ge(context_done, t + 1)
                dve.scalar_tensor_tensor(out=x_sb[:, t, :], in0=bank[7][:, :], scalar=gate_rows[:, 1:2],
                                         in1=x_sb[:, t, :], op0=ALU.mult, op1=ALU.add).then_inc(x3_ready, 1)
                dve.wait_ge(x3_ready, t + 1)
                ln_stats_of(t, t, 1)

            def router_in_low(t):
                tok = slice(t * P, t * P + P)
                ln_low(t, xt_hi[:, :, tok], xt_lo[:, :, tok], 1)

            for s in range(NB + 2):
                if s < NB:
                    down_whole(s)
                if 0 <= s - 2 < NB:
                    add_context(s - 2)
                if 0 <= s - 1 < NB:
                    sim_max_of(s - 1)
                if 0 <= s - 3 < NB:
                    router_in_low(s - 3)
                if 0 <= s - 1 < NB:
                    sim_norm(s - 1)
                if s < NB:
                    down_add(s)
                if 0 <= s - 2 < NB:
                    ln_rows_of(s - 2, s - 2, 1)
                if s < NB:
                    ln_rows_of(2 * NB + s, s)

            steps = [0]

            def step(ins):
                steps[0] += 1
                ins.then_inc(router_step, 1)
                dve.wait_ge(router_step, steps[0])

            def spread(ap, n):
                return ap.unsqueeze(len(ap.shape)).broadcast_to(list(ap.shape) + [n])

            def by_group(t):
                return t[:, :, :].rearrange("p t (g e) -> p t g e", g=EG)

            def first_of_largest(values, n, work, chosen):
                step(dve.tensor_reduce(r_stat[:, 0, :], values, AX.X, ALU.max))
                step(dve.tensor_tensor(work, values, spread(r_stat[:, 0, :], n), ALU.is_equal))
                step(dve.tensor_tensor(work, work, order[:, 0:n].unsqueeze(1).broadcast_to([P, NB, n]), ALU.mult))
                step(dve.tensor_reduce(r_stat[:, 1, :], work, AX.X, ALU.max))
                step(dve.tensor_tensor(chosen, work, spread(r_stat[:, 1, :], n), ALU.is_equal))

            def two_largest(values, n, rest, work, first, both):
                first_of_largest(values, n, work, first)
                step(dve.scalar_tensor_tensor(out=rest, in0=first, scalar=LOW, in1=values, op0=ALU.mult, op1=ALU.add))
                first_of_largest(rest, n, work, both)
                step(dve.tensor_tensor(both, both, first, ALU.add))

            def take_logits(half):
                dve.wait_ge(logits_turned, half + 1)
                dve.tensor_tensor(logits[:, 4 * half:4 * half + 4, :],
                                  route_bank[half][:, 0:4 * E].rearrange("p (t e) -> p t e", e=E),
                                  router_rows[:, 0, :].unsqueeze(1).broadcast_to([P, 4, E]), ALU.add)\
                   .then_inc(logits_ready, 1)

            def router_shift():
                dve.wait_ge(logits_ready, 2)
                dve.wait_ge(down_done, NB)
                step(dve.tensor_reduce(r_stat[:, 0, :], logits[:, :, :], AX.X, ALU.max))
                step(dve.tensor_tensor(r_score[:, :, :], logits[:, :, :], spread(r_stat[:, 0, :], E), ALU.subtract))

            def router_groups():
                dve.wait_ge(router_exp, 1)
                step(dve.tensor_reduce(r_stat[:, 0, :], r_score[:, :, :], AX.X, ALU.add))
                step(dve.reciprocal(r_stat[:, 1, :], r_stat[:, 0, :]))
                step(dve.tensor_tensor(r_score[:, :, :], r_score[:, :, :], spread(r_stat[:, 1, :], E), ALU.mult))
                step(dve.tensor_tensor(r_score[:, :, :], r_score[:, :, :],
                                       router_rows[:, 1, :].unsqueeze(1).broadcast_to([P, NB, E]), ALU.add))
                dve.wait_ge(tri_ready, 2)
                step(dve.tensor_reduce(order[:, :], tri[:, :, :], AX.X, ALU.add))
                step(dve.tensor_scalar(order[:, :], order[:, :], -1.0, float(E), ALU.mult, ALU.add))
                step(dve.tensor_reduce(r_gmax[:, :, :], by_group(r_score), AX.X, ALU.max))
                two_largest(r_gmax[:, :, :], EG, r_grest[:, :, :], r_gwork[:, :, :], r_gfirst[:, :, :], r_keep[:, :, :])

            def router_choice():
                step(dve.tensor_scalar(r_low[:, :, :], r_keep[:, :, :], -1.0, -LOW, ALU.add, ALU.mult))
                step(dve.tensor_tensor(by_group(r_masked), by_group(r_score), spread(r_keep[:, :, :], E // EG),
                                       ALU.mult))
                step(dve.tensor_tensor(by_group(r_masked), by_group(r_masked), spread(r_low[:, :, :], E // EG),
                                       ALU.add))
                two_largest(r_masked[:, :, :], E, r_rest[:, :, :], r_work[:, :, :], r_first[:, :, :], r_both[:, :, :])
                dve.scalar_tensor_tensor(out=gates[:, :, 2:EA], in0=r_score[:, :, :], scalar=gate_rows[:, 3:4],
                                         in1=r_both[:, :, :], op0=ALU.mult, op1=ALU.mult).then_inc(router_gates_ready, 1)

            def hidden(e, j, half):
                dve.wait_ge(silu_ready, e * 2 + (half + 1))
                dve.wait_ge(h_done, e * 4 + (2 * half + 2))
                dve.scalar_tensor_tensor(out=e_h[:, half, :], in0=bank[2 * half + 1][:, :],
                                         scalar=b_now[:, j, 1:2], in1=e_silu[:, half, :],
                                         op0=ALU.add, op1=ALU.mult).then_inc(h_ready, 1)
                dve.wait_ge(h_hi_ready, e * 2 + (half + 1))
                dve.tensor_tensor(h_lo[:, half, :], e_h[:, half, :], h_hi[:, half, :].bitcast(F32),
                                  ALU.subtract).then_inc(h_lo_ready, 1)

            def add_expert(e, half):
                for i in range(4):
                    t = 4 * half + i
                    dve.wait_ge(e_done, e * 8 + (t + 1))
                    dve.scalar_tensor_tensor(out=x_sb[:, t, :], in0=bank[4 + i][:, :],
                                             scalar=gates[:, t, bass.ds(e, 1)], in1=x_sb[:, t, :],
                                             op0=ALU.mult, op1=ALU.add).then_inc(e_added, 1)

            def expert_dve(e, j):
                hidden(e, j, 0)
                if after_first(e):
                    add_expert(e - 1, 1)
                hidden(e, j, 1)
                add_expert(e, 0)

            dve.tensor_scalar(gates[:, :, 0:2], minus_half[:, :].rearrange("p (t a) -> p t a", a=2), 0.0,
                              gate_rows[:, 3:4], ALU.mult, ALU.add).then_inc(shared_gate_ready, 1)
            take_logits(0)
            router_in_low(NB - 1)
            hidden(0, 0, 0)
            dve.wait_ge(shared_gate_ready, 1)
            add_expert(0, 0)
            take_logits(1)
            hidden(0, 0, 1)
            router_shift()
            router_groups()
            hidden(1, 1, 0)
            add_expert(0, 1)
            router_choice()
            hidden(1, 1, 1)
            add_expert(1, 0)
            hidden(2, 0, 0)
            add_expert(1, 1)
            for half in range(2):
                dve.wait_ge(gates_high, half + 1)
                cols = slice(half * D, half * D + D)
                dve.tensor_tensor(gates_t_lo[:, cols], bank[4 + half][0:E + 1, :], gates_t_hi[:, cols].bitcast(F32),
                                  ALU.subtract).then_inc(gates_low, 1)
            for t in range(NB):
                dve.wait_ge(bias_done, t + 1)
                dve.tensor_tensor(x_sb[:, t, :], bank[4 + t % 4][:, :], x_sb[:, t, :], ALU.add)\
                   .then_inc(bias_added, 1)
            hidden(2, 0, 1)
            dve.wait_ge(bias_added, NB)
            dve.wait_ge(router_gates_ready, 1)
            add_expert(2, 0)
            expert_dve(3, 1)
            with dve.Fori(2, EA // 2) as i:
                for j in range(2):
                    expert_dve(i * 2 + j, j)
            add_expert(EA - 1, 1)

        @block.tensor
        def _(pe):
            pe.wait_ge(consts_ready, 3)

            def turn_rows(i, s=0):
                pe.wait_ge(ln_row_ready[s], i + 1)
                for c in range(KC):
                    mm = pe.transpose(ln_bank(s, i)[:, c * P:c * P + P], ln_rows[s][:, i % 2, c * P:c * P + P],
                                      ident[:, :])
                mm.then_inc(ln_transposed[s], 1)

            def kv_tile(pair, p, i):
                half = i // 2
                tok = slice((2 * p + half) * P, (2 * p + half) * P + P)
                ps = (proj_a, proj_b)[half][:, (i % 2) * 256:(i % 2) * 256 + 256]
                for c in range(KC):
                    mm = three(pe, ps, kv_src_hi[:, i % 2, c, tok], kv_src_lo[:, i % 2, c, tok],
                               wkv_hi[:, c, :], wkv_lo[:, c, :], c == 0, c == KC - 1)
                if i % 2 == 1:
                    mm.then_inc(kv_done, 1)

            def q_tile(p, i):
                tok = slice((2 * p + i) * P, (2 * p + i) * P + P)
                for c in range(KC):
                    mm = three(pe, (proj_a, proj_b)[i][:, :], kv_src_hi[:, 1, c, tok], kv_src_lo[:, 1, c, tok],
                               wq_hi[:, c, :], wq_lo[:, c, :], c == 0, c == KC - 1)
                mm.then_inc(q_done, 1)

            def turn_q(pair):
                pe.wait_ge(q_copied, pair * 2 + 2)
                for half in range(2):
                    for h in range(2):
                        for i in range(2):
                            at_h = (2 * half + h) * HD
                            mm = pe.transpose((proj_a, proj_b)[half][:, h * 256 + i * P:h * 256 + i * P + P],
                                              q_rows[:, i, at_h:at_h + HD], ident[:, :])
                    mm.then_inc(q_turned, 1)

            def kv_half(g, p, half):
                pair = g * PAIRS + p
                if half == 0:
                    if p == 0:
                        pe.wait_ge(wkv_lo_ready, g + 1)
                    if after_start(g, 2 * p, 1):
                        pe.wait_ge(q_lo_ready, pair * 2 - 1)
                elif after_start(g, 2 * p, 1):
                    pe.wait_ge(q_lo_ready, pair * 2)
                kv_tile(pair, p, 2 * half)
                kv_tile(pair, p, 2 * half + 1)

            def q_half(g, p, half):
                pair = g * PAIRS + p
                if half == 0:
                    if p == 0:
                        pe.wait_ge(wq_lo_ready, g * R + R)
                    pe.wait_ge(v_lo_ready, pair * 2 + 1)
                    pe.wait_ge(k_copied, pair * 2 + 1)
                else:
                    pe.wait_ge(k_lo_ready, pair + 1)
                q_tile(p, half)

            def turn_k(pair):
                pe.wait_ge(k_scaled, pair * 4 + 4)
                pe.wait_ge(v_lo_ready, pair * 2 + 2)
                for i in range(4):
                    mm = pe.transpose(proj_b[:, i * P:i * P + P], k_rows[:, i, :], ident[:, :])
                mm.then_inc(k_turned, 1)

            def scores(g, b, half):
                n, pair, par = g * NB + b, g * PAIRS + b // 2, (b // 2) % 2
                pe.wait_ge(q_lo_ready, pair * 2 + (half + 1))
                pe.wait_ge(k_lo_ready, pair + 1)
                if after_start(g, b, 1):
                    pe.wait_ge(exp_done, n * 4 - 2 + 2 * half)
                i = b % 2
                for h in (2 * half, 2 * half + 1):
                    mm = three(pe, scores_ps[half][:, (h % 2) * 256:(h % 2) * 256 + 256],
                               q_hi[:, par, h, i * P:i * P + P], q_lo[:, par, h, i * P:i * P + P],
                               k_hi[:, par, i * 256:i * 256 + 256], k_lo[:, par, i * 256:i * 256 + 256], True, True)
                mm.then_inc(scores_done, 1)

            def turn_probs(n):
                pe.wait_ge(probs_ready, n * 4 + 4)
                for c in range(2):
                    for h in range(R):
                        mm = pe.transpose(pt_ps[c][:, h * P:h * P + P], probs[:, h, c * P:c * P + P], ident[:, :])
                    mm.then_inc(p_turned, 1)

            def weigh_values(g, b):
                n, pair = g * NB + b, g * PAIRS + b // 2
                par, i = (b // 2) % 2, b % 2
                pe.wait_ge(pt_lo_ready, n * 2 + 2)
                pe.wait_ge(v_lo_ready, pair * 2 + 2)
                if after_start(g, b, 1):
                    pe.wait_ge(o_lo_ready, n)
                for c in range(2):
                    mm = three(pe, o_ps[:, :], v_hi[:, par, 2 * i + c, :], v_lo[:, par, 2 * i + c, :],
                               pt_hi[:, c, :], pt_lo[:, c, :], c == 0, c == 1)
                mm.then_inc(o_done, 1)

            def project_out(g, b, heads=range(R)):
                n, par = g * NB + b, b % 2
                if heads[0] == 0:
                    pe.wait_ge(o_lo_ready, n + 1)
                    if after_start(g, b, 1):
                        pe.wait_ge(y_added, n)
                for h in heads:
                    if b == 0:
                        pe.wait_ge(wo_lo_ready, g * R + (h + 1))
                    mm = three(pe, y_ps[:, :], o_hi[:, par, h * P:h * P + P], o_lo[:, par, h * P:h * P + P],
                               wo_hi[:, h, :], wo_lo[:, h, :], h == 0, h == R - 1)
                if heads[-1] == R - 1:
                    mm.then_inc(y_done, 1)

            def turn_pair(p):
                for t in (2 * p, 2 * p + 1):
                    if 2 <= t < 6:
                        pe.wait_ge(ln_lo_ready[0], t - 1)
                    turn_rows(t)

            turn_pair(0)
            pe.wait_ge(ctx_first_lo_ready, 1)
            pe.wait_ge(ln_lo_ready[0], 2)
            kv_half(0, 0, 0)
            turn_pair(1)
            kv_half(0, 0, 1)
            q_half(0, 0, 0)
            turn_k(0)
            turn_pair(2)
            q_half(0, 0, 1)
            turn_pair(3)
            turn_q(0)
            pe.wait_ge(ln_lo_ready[0], 6)

            def turn_x(t):
                if t < 2:
                    pe.wait_ge(q_lo_ready, 2 * PAIRS * G)
                else:
                    pe.wait_ge(ln_lo_ready[0], NB + t - 1)
                turn_rows(NB + t)

            def one_group(g):
                for b in range(NB):
                    n = g * NB + b
                    ng, np_ = (g, b // 2 + 1) if b < NB - 2 else (g + 1, 0)
                    if isinstance(g, int) and g == 0 and b == 1:
                        pe.wait_ge(ln_lo_ready[0], NB)
                    if after_start(g, b, 1):
                        turn_probs(n - 1)
                    scores(g, b, 0)
                    scores(g, b, 1)
                    ahead = before_end(g, b - b % 2, 2)
                    if b % 2 == 1 and ahead:
                        turn_k(g * PAIRS + (b // 2 + 1))
                    if ahead:
                        if isinstance(g, int) and g == 0 and b < NB - 2:
                            pe.wait_ge(ctx_lo_ready, np_)
                        (kv_half, q_half)[b % 2](ng, np_, 0)
                    if b >= 6 and last_group(g):
                        turn_x(2 * (b - 6))
                        turn_x(2 * (b - 6) + 1)
                    if b >= 6 and last_group(g):
                        project_out(g, b - 2)
                    if after_start(g, b, 1):
                        weigh_values(g, b - 1)
                    if ahead:
                        (kv_half, q_half)[b % 2](ng, np_, 1)
                    back = (g, b - 2) if b >= 2 else (g - 1, b + NB - 2)
                    early = b >= 6 and last_group(g)
                    if after_start(g, b, 2) and not early:
                        project_out(*back, range(0, 2))
                    if b % 2 == 1 and ahead:
                        turn_q(g * PAIRS + (b // 2 + 1))
                    if after_start(g, b, 2) and not early:
                        project_out(*back, range(2, R))

            groups(pe, one_group)
            def inner_half(c, j, width, half):
                if after_first(c):
                    pe.wait_ge(inter_ready[half], c)
                tok = slice(half * D, half * D + D)
                for i in range(2):
                    for k in range(KC):
                        mm = three(pe, bank[2 * half + i][0:width, :], gu_hi[:, j, i, k, 0:width],
                                   gu_lo[:, j, i, k, 0:width], xt_hi[:, k, tok], xt_lo[:, k, tok],
                                   k == 0, k == KC - 1)
                    mm.then_inc(gu_done, 1)

            def inner_chunk(c, j, width, following):
                pe.wait_ge(gu_lo_ready, c + 1)
                inner_half(c, j, width, 0)
                if isinstance(c, int) and c == 0:
                    turn_x(7)
                    pe.wait_ge(ln_lo_ready[0], 2 * NB)
                inner_half(c, j, width, 1)

            turn_probs(G * NB - 1)
            turn_x(4)
            project_out(G - 1, NB - 2)
            weigh_values(G - 1, NB - 1)
            turn_x(5)
            project_out(G - 1, NB - 1)
            turn_x(6)

            chunks(pe, inner_chunk)

            def down(t, first, last):
                if t >= 2 and first == 0:
                    pe.wait_ge(sign_ready, 2 * (INNER + t) - 2)
                tok = slice(t * P, t * P + P)
                for c in range(first, last):
                    rows = P if c < CH - 1 else TAIL
                    for w in (wd_lo, wd_hi):
                        mm = pe.matmul(bank[4 + t % 2][:, :], iq[0:rows, c, tok], w[0:rows, c, :],
                                       start=(c == 0 and w is wd_lo), stop=(c == CH - 1 and w is wd_hi))
                if last == CH:
                    mm.then_inc(down_done, 1)

            def similarity(t):
                pe.wait_ge(ln_hi_ready[0], 2 * NB + t + 1)
                pe.wait_ge(ctx3_cols_loaded[t % 2], 16 * (t // 2 + 1))
                if t >= 1:
                    pe.wait_ge(sim_exp, t)
                for c in range(KC):
                    mm = pe.matmul(bank[6][:, 0:P], q3[:, c, :], ctx_cols[:, t % 2, c, :], start=(c == 0),
                                   stop=(c == KC - 1))
                mm.then_inc(sim_done, 1)

            def context(t):
                pe.wait_ge(sim_ready, t + 1)
                pe.wait_ge(ctx3_rows_loaded[t % 2], 16 * (t // 2 + 1))
                if t >= 1:
                    pe.wait_ge(x3_ready, t)
                pe.matmul(bank[7][:, :], sim[:, :], ctx_rows[:, t % 2, :], start=True, stop=True)\
                  .then_inc(context_done, 1)

            def route(half):
                pe.wait_ge(ln_lo_ready[1], 4 * half + 4)
                pe.wait_ge(router_w_ready, 1)
                if half == 0:
                    pe.wait_ge(sign_ready, 2 * (INNER + NB))
                else:
                    pe.wait_ge(silu_ready, 1)
                tok = slice(half * D, half * D + D)
                for c in range(KC):
                    mm = three(pe, route_bank[half][0:E, :], router_wh[:, c, :], router_wl[:, c, :],
                               xt_hi[:, c, tok], xt_lo[:, c, tok], c == 0, c == KC - 1)
                mm.then_inc(router_done, 1)

            def turn_logits(half):
                pe.wait_ge(logits_copied, half + 1)
                for i in range(4):
                    mm = pe.transpose(route_bank[half][:, i * E:i * E + E], logits_t[:, half, i * P:i * P + P],
                                      ident[0:E, 0:E])
                mm.then_inc(logits_turned, 1)

            def inner_part(e, j, half, i):
                if half == 0 and i == 0:
                    pe.wait_ge(e_lo_ready, e * 2 + 1)
                if after_first(e) and i == 0:
                    pe.wait_ge(h_ready, e * 2 + (half - 1))
                tok = slice(half * D, half * D + D)
                for k in range(KC):
                    mm = three(pe, bank[2 * half + i][:, :], e12_hi[:, j, i * KC + k, :], e12_lo[:, j, i * KC + k, :],
                               xt_hi[:, k, tok], xt_lo[:, k, tok], k == 0, k == KC - 1)
                mm.then_inc(h_done, 1)

            def inner(e, j, half):
                inner_part(e, j, half, 0)
                inner_part(e, j, half, 1)

            def outer(e, j, half):
                if half == 0:
                    pe.wait_ge(e_lo_ready, e * 2 + 2)
                pe.wait_ge(h_lo_ready, e * 2 + (half + 1))
                for i in range(4):
                    if isinstance(e, int) and e == 2 and half == 0:
                        pe.wait_ge(bias_added, 4 + i + 1)
                    elif after_first(e) or half == 1:
                        pe.wait_ge(e_added, e * 8 + (4 * half + i - 3))
                    tok = slice(i * P, i * P + P)
                    three(pe, bank[4 + i][:, :], h_hi[:, half, tok], h_lo[:, half, tok], e3_hi[:, j, :], e3_lo[:, j, :],
                          True, True).then_inc(e_done, 1)

            def expert_pe(e, j):
                inner(e, j, 0)
                if after_first(e):
                    outer(e - 1, 1 - j, 1)
                inner(e, j, 1)
                outer(e, j, 0)

            pe.wait_ge(iq_ready, INNER - 1)
            pe.wait_ge(wd_lo_ready, CH)
            down(0, 0, CH)
            down(1, 0, CH)
            for s in range(NB + 2):
                if 0 <= s - 1 < NB:
                    if s >= 3:
                        pe.wait_ge(ln_hi_ready[0], 2 * NB + s - 2)
                    turn_rows(2 * NB + s - 1)
                if s + 1 == NB // 2:
                    pe.wait_ge(iq_ready, INNER)
                if 2 <= s + 1 < NB:
                    down(s + 1, 0, CH // 2)
                if 0 <= s - 1 < NB:
                    similarity(s - 1)
                if 2 <= s + 1 < NB:
                    down(s + 1, CH // 2, CH)
                if s == NB - 1:
                    route(0)
                if s == NB:
                    pe.wait_ge(ln_hi_ready[0], 3 * NB - 1)
                    inner_part(0, 0, 0, 0)
                if 0 <= s - 1 < NB:
                    context(s - 1)
                if 0 <= s - 2 < NB:
                    if s - 2 >= 2:
                        pe.wait_ge(ln_lo_ready[1], s - 3)
                    turn_rows(s - 2, 1)
                if s == NB:
                    pe.wait_ge(ln_hi_ready[0], 3 * NB)
                    inner_part(0, 0, 0, 1)
            turn_logits(0)
            route(1)
            pe.wait_ge(logits_ready, 1)
            pe.wait_ge(x3_ready, NB)
            outer(0, 0, 0)
            pe.wait_ge(ln_lo_ready[1], NB)
            inner(0, 0, 1)
            turn_logits(1)
            pe.wait_ge(logits_ready, 2)
            expert_pe(1, 1)
            inner(2, 0, 0)
            outer(1, 1, 1)
            inner_part(2, 0, 1, 0)
            pe.wait_ge(router_gates_ready, 1)
            pe.wait_ge(e_added, 14)
            for half in range(2):
                for i in range(4):
                    mm = pe.transpose(bank[4 + half][0:E + 1, i * P:i * P + P], gates[:, 4 * half + i, 1:EA], ident[:, :])
                mm.then_inc(gates_turned, 1)
            inner_part(2, 0, 1, 1)
            pe.wait_ge(gates_low, 2)
            pe.wait_ge(b3_low, 1)
            pe.wait_ge(e_added, 16)
            for t in range(NB):
                if t >= 4:
                    pe.wait_ge(bias_added, t - 3)
                tok = slice(t * P, t * P + P)
                three(pe, bank[4 + t % 4][:, :], gates_t_hi[:, tok], gates_t_lo[:, tok], b3_hi[:, :], b3_lo[:, :],
                      True, True).then_inc(bias_done, 1)
            outer(2, 0, 0)
            expert_pe(3, 1)
            with pe.Fori(2, EA // 2) as i:
                for j in range(2):
                    expert_pe(i * 2 + j, j)
            outer(EA - 1, 1, 1)


def kernel(**inputs):
    import numpy as np
    import concourse.bacc as bacc
    from concourse.bass_utils import run_bass_kernel_spmd

    nc = bacc.Bacc("TRN2", target_bir_lowering=False, num_devices=1)
    a = {k: np.asarray(v) for k, v in inputs.items()}
    wq = a["L0_xattn_Wq"].reshape(KC, P, G, R * HD).transpose(2, 1, 0, 3)
    wk = a["L0_xattn_Wk"].reshape(KC, P, G, HD).transpose(2, 1, 0, 3)
    wv = a["L0_xattn_Wv"].reshape(KC, P, G, HD).transpose(2, 1, 0, 3)

    def by_expert(shared, routed):
        s = a["L1_ffn_" + shared].reshape(KC, P, 2, P).transpose(2, 1, 0, 3)
        return np.concatenate([s, a["L1_ffn_" + routed].reshape(E, KC, P, P).transpose(0, 2, 1, 3)], axis=0)

    arrays = {
        "x": a["x"],
        "ctx_t": a["ctx_4096"].reshape(NB * P, KC, P).transpose(2, 1, 0),
        "g_xattn": a["g_xattn"].reshape(1, 2),
        "g_ffn": a["g_ffn"].reshape(1, 2),
        "wq": wq,
        "wkv": np.concatenate([wk, wv], axis=3),
        "wo": a["L0_xattn_Wo"].reshape(G, R, HD, D).transpose(0, 2, 1, 3),
        "q_w": a["L0_xattn_q_norm_w"].reshape(HD, 1),
        "k_w": a["L0_xattn_k_norm_w"].reshape(HD, 1),
        "ctx": a["ctx_4096"],
        "w_gate": a["L0_ffn_w_gate"].T.reshape(KC, P, INTER).transpose(1, 0, 2),
        "w_up": a["L0_ffn_w_up"].T.reshape(KC, P, INTER).transpose(1, 0, 2),
        "w_down": a["L0_ffn_w_down"].T,
        "router_w": a["L1_ffn_router_w"].reshape(KC, P, E).transpose(1, 0, 2),
        "router_b": a["L1_ffn_router_b"].reshape(1, E),
        "router_bias": a["L1_ffn_router_bias"].reshape(1, E),
        "e_w12": np.concatenate([by_expert("sw1", "ew1"), by_expert("sw2", "ew2")], axis=2),
        "e_w3": np.concatenate([a["L1_ffn_sw3"].reshape(2, P, D), a["L1_ffn_ew3"]], axis=0),
        "e_b12": np.stack([np.concatenate([a[f"L1_ffn_sb{i}"].reshape(2, P), a[f"L1_ffn_eb{i}"]], axis=0).T
                           for i in (1, 2)], axis=2),
        "e_b3": np.concatenate([a["L1_ffn_sb3"].reshape(1, D), a["L1_ffn_eb3"]], axis=0),
    }
    arrays = {k: np.ascontiguousarray(v) for k, v in arrays.items()}
    args = {k: nc.dram_tensor(k, v.shape, mybir.dt.from_np(v.dtype), kind="ExternalInput").ap()
            for k, v in arrays.items()}
    out = nc.dram_tensor("out", (NB, P, D), F32, kind="ExternalOutput").ap()
    build(nc, out=out, **args)
    r = run_bass_kernel_spmd(nc, [arrays], core_ids=[0])
    return r.results[0]["out"]
```
